# Optimizing a Trainium2 kernel written in Bass

```python
import numpy as np
import jax
import jax.numpy as jnp

def _softmax(x, axis=-1):
    return jax.nn.softmax(x, axis=axis)

def _gelu(x):
    return jax.nn.gelu(x, approximate=True)

def _silu(x):
    return jax.nn.silu(x)

def _sigmoid(x):
    return jax.nn.sigmoid(x)

def _layernorm(x, axis=-1, eps=1e-05):
    m = jnp.mean(x, axis=axis, keepdims=True)
    v = jnp.var(x, axis=axis, keepdims=True)
    return (x - m) / jnp.sqrt(v + eps)

def _scatter_add(tgt, idx, src, axis=0):
    return tgt.at[idx].add(src)

def _segment_sum(src, seg, n):
    return jax.ops.segment_sum(src, seg, n)
kernel_name = 'mk_macaron_d2_jaxref_r8_a1fea6'

def setup_inputs(seed: int=0):
    np.random.seed(seed)
    _w = jnp.asarray

    def _L0_attn_setup():
        import jax, jax.numpy as jnp
        import numpy as np
        H = 8
        LN_EPS = 1e-05
        key = jax.random.key(seed)
        ks = jax.random.split(key, 4)
        B, S, D = (4, 256, 128)
        x = jax.random.normal(ks[0], (B, S, D), dtype=jnp.float32)
        sc = 1.0 / np.sqrt(D)
        Wq = jax.random.normal(ks[1], (D, D), dtype=jnp.float32) * sc
        Wk = jax.random.normal(ks[2], (D, D), dtype=jnp.float32) * sc
        Wv = jax.random.normal(ks[3], (D, D * H), dtype=jnp.float32) * sc
        return {'x': x, 'Wq': Wq, 'bq': jnp.zeros((D,), jnp.float32), 'Wk': Wk, 'bk': jnp.zeros((D,), jnp.float32), 'Wv': Wv, 'bv': jnp.zeros((D * H,), jnp.float32), 'gamma': jnp.ones((D,), jnp.float32), 'beta': jnp.zeros((D,), jnp.float32)}
    _L0_attn_in = _L0_attn_setup()

    def _L0_ffn_setup():
        import jax, jax.numpy as jnp
        import numpy as np
        DIM = 128

        def _reference_tuple_inner(x, W_r, W_k, W_v, mu_r, mu_k):
            B, T, C = x.shape
            x_prev = jnp.concatenate([jnp.zeros((B, 1, C), x.dtype), x[:, :-1, :]], axis=1)
            xr = mu_r * x + (1.0 - mu_r) * x_prev
            xk = mu_k * x + (1.0 - mu_k) * x_prev
            r = jax.nn.sigmoid(jnp.einsum('btc,dc->btd', xr, W_r))
            k = jnp.einsum('btc,dc->btd', xk, W_k)
            k_act = jnp.square(jax.nn.relu(k))
            out = r * jnp.einsum('btc,dc->btd', k_act, W_v)
            new_state = x[:, -1, :]
            return (out, new_state)
        key = jax.random.key(seed)
        ks = jax.random.split(key, 6)
        B, T, C = (8, 256, DIM)
        x = jax.random.normal(ks[0], (B, T, C), dtype=jnp.float32)
        s = 1.0 / np.sqrt(C)
        W_r = jax.random.uniform(ks[1], (C, C), jnp.float32, -s, s)
        W_k = jax.random.uniform(ks[2], (C, C), jnp.float32, -s, s)
        W_v = jax.random.uniform(ks[3], (C, C), jnp.float32, -s, s)
        mu_r = jax.random.uniform(ks[4], (C,), jnp.float32)
        mu_k = jax.random.uniform(ks[5], (C,), jnp.float32)
        return {'x': x, 'W_r': W_r, 'W_k': W_k, 'W_v': W_v, 'mu_r': mu_r, 'mu_k': mu_k}
    _L0_ffn_in = _L0_ffn_setup()

    def _L1_attn_setup():
        import jax, jax.numpy as jnp
        import numpy as np
        NUM_HEADS = 8
        BETA_MIN, BETA_MAX = (0.85, 0.999)
        ROPE_BASE = 10000.0

        def _rope_cache(L, d):
            half = d // 2
            inv_freq = 1.0 / ROPE_BASE ** (jnp.arange(half, dtype=jnp.float32) / half)
            freqs = jnp.arange(L, dtype=jnp.float32)[:, None] * inv_freq[None, :]
            return (jnp.cos(freqs), jnp.sin(freqs))

        def _apply_rope(x, cos, sin):
            B, H, L, D = x.shape
            xp = x.reshape(B, H, L, D // 2, 2)
            x1, x2 = (xp[..., 0], xp[..., 1])
            c = cos[None, None]
            s = sin[None, None]
            r1 = x1 * c - x2 * s
            r2 = x2 * c + x1 * s
            return jnp.stack([r1, r2], axis=-1).reshape(B, H, L, D)

        def _delta_scan(q, k, v, alpha, beta):
            B, H, L, Dh = q.shape
            qm = q.transpose(2, 0, 1, 3)
            km = k.transpose(2, 0, 1, 3)
            vm = v.transpose(2, 0, 1, 3)
            am = alpha.transpose(2, 0, 1)
            bm = beta.transpose(2, 0, 1)

            def step(state, inp):
                qt, kt, vt, at, bt = inp
                state = state * bt[..., None, None] + at[..., None, None] * (kt[..., :, None] * vt[..., None, :])
                ot = jnp.einsum('bhd,bhde->bhe', qt, state)
                return (state, ot)
            state0 = jnp.zeros((B, H, Dh, Dh), dtype=q.dtype)
            _, outs = jax.lax.scan(step, state0, (qm, km, vm, am, bm))
            return outs.transpose(1, 2, 0, 3)
        key = jax.random.key(seed)
        B, L, D, H = (2, 256, 128, NUM_HEADS)
        ks = jax.random.split(key, 8)
        scale = np.sqrt(6.0 / (D + D)).astype(np.float32)
        Wq = jax.random.uniform(ks[0], (D, D), jnp.float32, -scale, scale)
        Wk = jax.random.uniform(ks[1], (D, D), jnp.float32, -scale, scale)
        Wv = jax.random.uniform(ks[2], (D, D), jnp.float32, -scale, scale)
        Wo = jax.random.uniform(ks[3], (D, D), jnp.float32, -scale, scale)
        bo = jnp.zeros((D,), jnp.float32)
        Wbeta = jax.random.normal(ks[4], (H, D), jnp.float32) * 0.02
        bbeta = jnp.full((H,), float(np.log(0.97 / 0.03)), jnp.float32)
        Walpha = jax.random.normal(ks[5], (H, D), jnp.float32) * 0.02
        balpha = jnp.zeros((H,), jnp.float32)
        x = jax.random.normal(ks[6], (B, L, D), jnp.float32)
        return {'x': x, 'Wq': Wq, 'Wk': Wk, 'Wv': Wv, 'Wbeta': Wbeta, 'bbeta': bbeta, 'Walpha': Walpha, 'balpha': balpha, 'Wo': Wo, 'bo': bo}
    _L1_attn_in = _L1_attn_setup()

    def _L1_ffn_setup():
        import jax, jax.numpy as jnp
        import numpy as np
        IN_DIM = 128
        HIDDEN = 128
        OUT_DIM = 128
        NUM_EXPERTS = 16
        TOP_K = 2
        ROUTER_TEMP = 1.0
        LN_EPS = 1e-05

        def _layernorm(h, g, b):
            mu = jnp.mean(h, axis=-1, keepdims=True)
            var = jnp.mean(jnp.square(h - mu), axis=-1, keepdims=True)
            return (h - mu) * jax.lax.rsqrt(var + LN_EPS) * g + b
        key = jax.random.key(seed)
        ks = jax.random.split(key, 8)
        s_in = 1.0 / np.sqrt(IN_DIM)
        s_h = 1.0 / np.sqrt(HIDDEN)
        x = jax.random.normal(ks[0], (4, 256, IN_DIM), dtype=jnp.float32)
        Wr = jax.random.uniform(ks[1], (IN_DIM, NUM_EXPERTS), jnp.float32, -s_in, s_in)
        br = jax.random.uniform(ks[2], (NUM_EXPERTS,), jnp.float32, -s_in, s_in)
        W1 = jax.random.uniform(ks[3], (NUM_EXPERTS, IN_DIM, HIDDEN), jnp.float32, -s_in, s_in)
        b1 = jax.random.uniform(ks[4], (NUM_EXPERTS, HIDDEN), jnp.float32, -s_in, s_in)
        g1 = jnp.ones((NUM_EXPERTS, HIDDEN), jnp.float32)
        be1 = jnp.zeros((NUM_EXPERTS, HIDDEN), jnp.float32)
        W2 = jax.random.uniform(ks[5], (NUM_EXPERTS, HIDDEN, OUT_DIM), jnp.float32, -s_h, s_h)
        b2 = jax.random.uniform(ks[6], (NUM_EXPERTS, OUT_DIM), jnp.float32, -s_h, s_h)
        return {'x': x, 'Wr': Wr, 'br': br, 'W1': W1, 'b1': b1, 'g1': g1, 'be1': be1, 'W2': W2, 'b2': b2}
    _L1_ffn_in = _L1_ffn_setup()
    _d = {'L0_attn_x': _L0_attn_in['x'], 'L0_attn_Wq': _L0_attn_in['Wq'], 'L0_attn_bq': _L0_attn_in['bq'], 'L0_attn_Wk': _L0_attn_in['Wk'], 'L0_attn_bk': _L0_attn_in['bk'], 'L0_attn_Wv': _L0_attn_in['Wv'], 'L0_attn_bv': _L0_attn_in['bv'], 'L0_attn_gamma': _L0_attn_in['gamma'], 'L0_attn_beta': _L0_attn_in['beta'], 'L0_ffn_W_r': _L0_ffn_in['W_r'], 'L0_ffn_W_k': _L0_ffn_in['W_k'], 'L0_ffn_W_v': _L0_ffn_in['W_v'], 'L0_ffn_mu_r': _L0_ffn_in['mu_r'], 'L0_ffn_mu_k': _L0_ffn_in['mu_k'], 'L1_attn_Wq': _L1_attn_in['Wq'], 'L1_attn_Wk': _L1_attn_in['Wk'], 'L1_attn_Wv': _L1_attn_in['Wv'], 'L1_attn_Wbeta': _L1_attn_in['Wbeta'], 'L1_attn_bbeta': _L1_attn_in['bbeta'], 'L1_attn_Walpha': _L1_attn_in['Walpha'], 'L1_attn_balpha': _L1_attn_in['balpha'], 'L1_attn_Wo': _L1_attn_in['Wo'], 'L1_attn_bo': _L1_attn_in['bo'], 'L1_ffn_Wr': _L1_ffn_in['Wr'], 'L1_ffn_br': _L1_ffn_in['br'], 'L1_ffn_W1': _L1_ffn_in['W1'], 'L1_ffn_b1': _L1_ffn_in['b1'], 'L1_ffn_g1': _L1_ffn_in['g1'], 'L1_ffn_be1': _L1_ffn_in['be1'], 'L1_ffn_W2': _L1_ffn_in['W2'], 'L1_ffn_b2': _L1_ffn_in['b2']}
    _x0 = _d['L0_attn_x']
    _d['L0_attn_x'] = jax.random.normal(jax.random.fold_in(jax.random.key(seed), 1), (2, 1024, 128), dtype=_x0.dtype)
    del _x0
    return _d

def reference(L0_attn_x, L0_attn_Wq, L0_attn_bq, L0_attn_Wk, L0_attn_bk, L0_attn_Wv, L0_attn_bv, L0_attn_gamma, L0_attn_beta, L0_ffn_W_r, L0_ffn_W_k, L0_ffn_W_v, L0_ffn_mu_r, L0_ffn_mu_k, L1_attn_Wq, L1_attn_Wk, L1_attn_Wv, L1_attn_Wbeta, L1_attn_bbeta, L1_attn_Walpha, L1_attn_balpha, L1_attn_Wo, L1_attn_bo, L1_ffn_Wr, L1_ffn_br, L1_ffn_W1, L1_ffn_b1, L1_ffn_g1, L1_ffn_be1, L1_ffn_W2, L1_ffn_b2):

    def _L0_attn_ref(x, Wq, bq, Wk, bk, Wv, bv, gamma, beta):
        import jax, jax.numpy as jnp
        import numpy as np
        H = 8
        LN_EPS = 1e-05
        B, S, D = x.shape
        dk = D // H
        mu = jnp.mean(x, axis=-1, keepdims=True)
        var = jnp.mean(jnp.square(x - mu), axis=-1, keepdims=True)
        xn = (x - mu) * jax.lax.rsqrt(var + LN_EPS) * gamma + beta
        q = (xn @ Wq + bq).reshape(B, S, H, dk).transpose(0, 2, 1, 3)
        k = (xn @ Wk + bk).reshape(B, S, H, dk).transpose(0, 2, 1, 3)
        v = (xn @ Wv + bv).reshape(B, S, H, D).transpose(0, 2, 1, 3)
        scores = jnp.einsum('bhsd,bhtd->bhst', q, k) / jnp.sqrt(jnp.asarray(dk, x.dtype))
        p = jax.nn.softmax(scores, axis=-1)
        att = jnp.einsum('bhst,bhtd->bhsd', p, v)
        out = att.reshape(S, B, D, H).sum(axis=-1).reshape(B, S, D)
        return out

    def _L0_ffn_ref(x, W_r, W_k, W_v, mu_r, mu_k):
        import jax, jax.numpy as jnp
        import numpy as np
        DIM = 128

        def _reference_tuple_inner(x, W_r, W_k, W_v, mu_r, mu_k):
            B, T, C = x.shape
            x_prev = jnp.concatenate([jnp.zeros((B, 1, C), x.dtype), x[:, :-1, :]], axis=1)
            xr = mu_r * x + (1.0 - mu_r) * x_prev
            xk = mu_k * x + (1.0 - mu_k) * x_prev
            r = jax.nn.sigmoid(jnp.einsum('btc,dc->btd', xr, W_r))
            k = jnp.einsum('btc,dc->btd', xk, W_k)
            k_act = jnp.square(jax.nn.relu(k))
            out = r * jnp.einsum('btc,dc->btd', k_act, W_v)
            new_state = x[:, -1, :]
            return (out, new_state)
        return _reference_tuple_inner(x, W_r, W_k, W_v, mu_r, mu_k)[0]

    def _L1_attn_ref(x, Wq, Wk, Wv, Wbeta, bbeta, Walpha, balpha, Wo, bo):
        import jax, jax.numpy as jnp
        import numpy as np
        NUM_HEADS = 8
        BETA_MIN, BETA_MAX = (0.85, 0.999)
        ROPE_BASE = 10000.0

        def _rope_cache(L, d):
            half = d // 2
            inv_freq = 1.0 / ROPE_BASE ** (jnp.arange(half, dtype=jnp.float32) / half)
            freqs = jnp.arange(L, dtype=jnp.float32)[:, None] * inv_freq[None, :]
            return (jnp.cos(freqs), jnp.sin(freqs))

        def _apply_rope(x, cos, sin):
            B, H, L, D = x.shape
            xp = x.reshape(B, H, L, D // 2, 2)
            x1, x2 = (xp[..., 0], xp[..., 1])
            c = cos[None, None]
            s = sin[None, None]
            r1 = x1 * c - x2 * s
            r2 = x2 * c + x1 * s
            return jnp.stack([r1, r2], axis=-1).reshape(B, H, L, D)

        def _delta_scan(q, k, v, alpha, beta):
            B, H, L, Dh = q.shape
            qm = q.transpose(2, 0, 1, 3)
            km = k.transpose(2, 0, 1, 3)
            vm = v.transpose(2, 0, 1, 3)
            am = alpha.transpose(2, 0, 1)
            bm = beta.transpose(2, 0, 1)

            def step(state, inp):
                qt, kt, vt, at, bt = inp
                state = state * bt[..., None, None] + at[..., None, None] * (kt[..., :, None] * vt[..., None, :])
                ot = jnp.einsum('bhd,bhde->bhe', qt, state)
                return (state, ot)
            state0 = jnp.zeros((B, H, Dh, Dh), dtype=q.dtype)
            _, outs = jax.lax.scan(step, state0, (qm, km, vm, am, bm))
            return outs.transpose(1, 2, 0, 3)
        B, L, D = x.shape
        H = NUM_HEADS
        Dh = D // H
        split = lambda y: y.reshape(B, L, H, Dh).transpose(0, 2, 1, 3)
        q = split(x @ Wq.T)
        k = split(x @ Wk.T)
        v = split(x @ Wv.T)
        cos, sin = _rope_cache(L, Dh)
        q = _apply_rope(q, cos, sin)
        k = _apply_rope(k, cos, sin)
        beta = BETA_MIN + (BETA_MAX - BETA_MIN) * jax.nn.sigmoid(x @ Wbeta.T + bbeta)
        alpha = jax.nn.sigmoid(x @ Walpha.T + balpha)
        beta = beta.transpose(0, 2, 1)
        alpha = alpha.transpose(0, 2, 1)
        out = _delta_scan(q, k, v, alpha, beta)
        out = out.transpose(0, 2, 1, 3).reshape(B, L, D)
        return out @ Wo.T + bo

    def _L1_ffn_ref(x, Wr, br, W1, b1, g1, be1, W2, b2):
        import jax, jax.numpy as jnp
        import numpy as np
        IN_DIM = 128
        HIDDEN = 128
        OUT_DIM = 128
        NUM_EXPERTS = 16
        TOP_K = 2
        ROUTER_TEMP = 1.0
        LN_EPS = 1e-05

        def _layernorm(h, g, b):
            mu = jnp.mean(h, axis=-1, keepdims=True)
            var = jnp.mean(jnp.square(h - mu), axis=-1, keepdims=True)
            return (h - mu) * jax.lax.rsqrt(var + LN_EPS) * g + b
        orig_shape = x.shape[:-1]
        x_flat = x.reshape(-1, x.shape[-1])
        logits = (x_flat @ Wr + br) / max(ROUTER_TEMP, 1e-06)
        probs = jax.nn.softmax(logits, axis=-1)
        topk_w, topk_idx = jax.lax.top_k(probs, TOP_K)
        topk_w = topk_w / jnp.clip(jnp.sum(topk_w, axis=-1, keepdims=True), 1e-09)
        h = jnp.einsum('nc,ech->neh', x_flat, W1) + b1
        h = _layernorm(h, g1, be1)
        h = jax.nn.gelu(h, approximate=False)
        expert_out = jnp.einsum('neh,eho->neo', h, W2) + b2
        sel = jnp.take_along_axis(expert_out, topk_idx[:, :, None], axis=1)
        y_flat = jnp.sum(sel * topk_w[:, :, None], axis=1)
        return y_flat.reshape(*orig_shape, y_flat.shape[-1])
    x = L0_attn_x
    x = x + 0.5 * _L0_ffn_ref(_layernorm(x, axis=-1), L0_ffn_W_r, L0_ffn_W_k, L0_ffn_W_v, L0_ffn_mu_r, L0_ffn_mu_k)
    x = x + _L0_attn_ref(_layernorm(x, axis=-1), L0_attn_Wq, L0_attn_bq, L0_attn_Wk, L0_attn_bk, L0_attn_Wv, L0_attn_bv, L0_attn_gamma, L0_attn_beta)
    x = x + 0.5 * _L0_ffn_ref(_layernorm(x, axis=-1), L0_ffn_W_r, L0_ffn_W_k, L0_ffn_W_v, L0_ffn_mu_r, L0_ffn_mu_k)
    x = x + 0.5 * _L1_ffn_ref(_layernorm(x, axis=-1), L1_ffn_Wr, L1_ffn_br, L1_ffn_W1, L1_ffn_b1, L1_ffn_g1, L1_ffn_be1, L1_ffn_W2, L1_ffn_b2)
    x = x + _L1_attn_ref(_layernorm(x, axis=-1), L1_attn_Wq, L1_attn_Wk, L1_attn_Wv, L1_attn_Wbeta, L1_attn_bbeta, L1_attn_Walpha, L1_attn_balpha, L1_attn_Wo, L1_attn_bo)
    x = x + 0.5 * _L1_ffn_ref(_layernorm(x, axis=-1), L1_ffn_Wr, L1_ffn_br, L1_ffn_W1, L1_ffn_b1, L1_ffn_g1, L1_ffn_be1, L1_ffn_W2, L1_ffn_b2)
    return x

_drawn_inputs = setup_inputs


def setup_inputs(seed=0):
    import zlib

    import numpy as np

    out = dict(_drawn_inputs(seed))
    spreads = {'L0_attn_bq': (0.0, 0.1),
     'L0_attn_bk': (0.0, 2.0),
     'L0_attn_bv': (0.0, 0.1),
     'L0_attn_gamma': (1.0, 0.2),
     'L0_attn_beta': (0.0, 0.1),
     'L1_attn_bbeta': (3.4760987758636475, 0.2),
     'L1_attn_balpha': (0.0, 0.1),
     'L1_attn_bo': (0.0, 2.0),
     'L1_ffn_g1': (1.0, 0.2),
     'L1_ffn_be1': (0.0, 0.432)}
    factors = {'L0_ffn_mu_r': 3.151, 'L1_ffn_b1': 3.164}
    for name, (base, spread) in spreads.items():
        noise = np.random.default_rng([zlib.crc32(name.encode()), seed]).standard_normal(out[name].shape)
        drawn = base * np.exp(spread * noise) if base else spread * noise
        out[name] = jnp.asarray(drawn.astype(out[name].dtype))
    for name, factor in factors.items():
        out[name] = (out[name] * factor).astype(out[name].dtype)
    return out
```

```python
from contextlib import ExitStack

import concourse.bass as bass
from concourse import mybir

F32 = mybir.dt.float32
BF16 = mybir.dt.bfloat16
I32 = mybir.dt.int32
ACT = mybir.ActivationFunctionType
ALU = mybir.AluOpType
AX = mybir.AxisListType

P = 128
B, S = 2, 1024
NT = B * S // P
TB = NT // B
NH, DK = 8, 16
NE = 16
EPS = 1e-5
BETA_MIN, BETA_MAX = 0.85, 0.999
RSQRT_SEED = float(0x5F3759DF)
PAD = 8

WCOLS = {}
_at = 0
for _name, _n in (("ffn_r", P), ("ffn_k", P), ("ffn_v", P), ("att_q", P), ("att_k", P),
                  ("lin_qkvab", 3 * P + 2 * NH), ("lin_o", P), ("router", NE), ("mu_r", 1), ("mu_k", 1),
                  ("gamma", 1), ("beta", 1), ("bq", 1), ("bk", 1), ("g1", NE), ("be1", NE)):
    WCOLS[_name] = (_at, _n)
    _at += _n
WTOTAL = _at
CCOLS = {}
_at = 0
for _name, _n in (("ident", P), ("causal", P), ("blocks", P), ("cos", TB * DK // 2), ("sin", TB * DK // 2),
                  ("rank", NE), ("parity", 2), ("ones", 1), ("restart", 1)):
    CCOLS[_name] = (_at, _n)
    _at += _n
CTOTAL = _at
RCOLS = {}
_at = 0
for _name, _n in (("bv", NH * P), ("bo", P), ("ab", 2 * NH), ("br", NE)):
    RCOLS[_name] = (_at, _n)
    _at += _n
RTOTAL = _at


def build(nc, A):
    with ExitStack() as ctx:
        def sb(name, shape, dt=F32):
            return ctx.enter_context(nc.sbuf_tensor(name, shape, dt))

        def sem(name):
            return ctx.enter_context(nc.semaphore(name))

        x = sb("x", [P, NT, P])
        xl = sb("xl", [P, NT, P])
        xt = sb("xt", [P, B, PAD + S])
        w = sb("w", [P, WTOTAL])
        cst = sb("cst", [P, CTOTAL])
        row = sb("row", [P, RTOTAL])
        w1 = sb("w1", [P, NE, P])
        w2 = sb("w2", [P, NE, P])
        wvs = sb("wvs", [P, P])
        bvs = sb("bvs", [P, P])
        b1 = sb("b1", [NE, P])
        b1r = sb("b1r", [NE, P])
        b1p = sb("b1p", [NE, 3, P], BF16)
        b2 = sb("b2", [NE, P])
        b1row = sb("b1row", [3, NE * P], BF16)
        ones3 = sb("ones3", [3, P], BF16)
        identb = sb("identb", [P, P], BF16)
        stat = sb("stat", [P, NT, 6])
        small = sb("small", [P, 24, 64])
        smalli = sb("smalli", [P, 2, 64], I32)
        arena = sb("arena", [P, 32 * 1024])
        ps = ctx.enter_context(nc.psum_tensor("ps", [P, 8, 512], F32))
        scratch = nc.dram_tensor("att_parts", [B, 2, 3, P, S], BF16, kind="Internal").ap()

        def wc(name):
            a, n = WCOLS[name]
            return w[:, a:a + n]

        def cc(name):
            a, n = CCOLS[name]
            return cst[:, a:a + n]

        def rc(name):
            a, n = RCOLS[name]
            return row[:, a:a + n]

        def arena_f(at, *shape):
            n = 1
            for d in shape:
                n *= d
            v = arena[:, at:at + n]
            names = "abcd"[:len(shape)]
            if len(shape) == 1:
                return v
            return v.rearrange("p (" + " ".join(names) + ") -> p " + " ".join(names),
                               **{k: d for k, d in zip(names, shape)})

        def arena_b(at, *shape):
            n = 1
            for d in shape:
                n *= d
            v = arena[:, at:at + n // 2].bitcast(BF16)
            names = "abcd"[:len(shape)]
            return v.rearrange("p (" + " ".join(names) + ") -> p " + " ".join(names),
                               **{k: d for k, d in zip(names, shape)})

        s_x = [sem(f"x_loaded{half}") for half in range(B)]
        s_w = sem("weights_loaded")
        s_mix = sem("expert_weights_loaded")
        s_out = sem("out_stored")
        s_v = sem("vector_steps")
        s_set = sem("constants_set")
        s_b1 = sem("b1_parts_ready")
        s_b1row = sem("b1_rows_loaded")
        s_wv = sem("wv_loaded")
        s_wvs = sem("summed_wv_ready")

        class Steps:

            def __init__(self, eng, s):
                self.eng, self.s, self.n = eng, s, 0

            def step(self, ins):
                ins.then_inc(self.s, 1)
                self.n += 1
                self.eng.wait_ge(self.s, self.n)

        def bc(ap, shape):
            return ap.to_broadcast(shape)

        class Norm:
            stat = sem("norm_stats")
            xl_v, xl_a = sem("norm_xl_by_vector"), sem("norm_xl_by_scalar")
            tp = sem("norm_turned")
            xt_v, xt_a = sem("norm_xt_by_vector"), sem("norm_xt_by_scalar")

            def __init__(self, k):
                self.k = k

        rstd = small[:, 0, 0:NT]
        nmr = small[:, 1, 0:NT]
        mean = small[:, 2, 0:NT]

        def rsqrt(vs, out, v, n, at=12):
            y, t, hv = small[:, at, 0:n], small[:, at + 1, 0:n], small[:, at + 2, 0:n]
            vs.step(nc.vector.tensor_scalar(smalli[:, 0, 0:n], v.bitcast(I32), 1, None, ALU.logical_shift_right))
            vs.step(nc.vector.tensor_scalar(y.bitcast(I32), smalli[:, 0, 0:n], -1.0, RSQRT_SEED, ALU.mult, ALU.add))
            vs.step(nc.vector.tensor_scalar(hv, v, -0.5, None, ALU.mult))
            for it in range(3):
                vs.step(nc.vector.tensor_tensor(t, y, y, ALU.mult))
                vs.step(nc.vector.tensor_tensor(t, t, hv, ALU.mult))
                vs.step(nc.vector.scalar_tensor_tensor(out=out if it == 2 else y, in0=t, scalar=1.5, in1=y,
                                                       op0=ALU.add, op1=ALU.mult))

        def norm_vector_stats(dve, vs, n, half, double):
            lo, hi = TB * half, TB * (half + 1)
            for t in range(lo, hi):
                ins = nc.vector.bn_stats(stat[:, t, :], x[:, t, :])
            vs.step(ins)
            me, mo = stat[:, lo:hi, 1], stat[:, lo:hi, 4]
            ve, vo = stat[:, lo:hi, 2], stat[:, lo:hi, 5]
            d, d2, v, v4 = (small[:, i, 0:TB] for i in (4, 5, 6, 7))
            nc.vector.tensor_tensor(d, me, mo, ALU.subtract)
            nc.vector.tensor_tensor(v, ve, vo, ALU.add)
            vs.step(nc.vector.tensor_tensor(mean[:, lo:hi], me, mo, ALU.add))
            nc.vector.tensor_scalar(mean[:, lo:hi], mean[:, lo:hi], 0.5, None, ALU.mult)
            vs.step(nc.vector.tensor_tensor(d2, d, d, ALU.mult))
            vs.step(nc.vector.scalar_tensor_tensor(out=v4, in0=v, scalar=4.0 / P, in1=d2, op0=ALU.mult, op1=ALU.add))
            vs.step(nc.vector.tensor_scalar(v, v4, 0.25, EPS, ALU.mult, ALU.add))
            r = rstd[:, lo:hi]
            rsqrt(vs, r, v, TB)
            if double:
                u, r2 = small[:, 8, 0:TB], small[:, 9, 0:TB]
                vs.step(nc.vector.tensor_tensor(d2, r, r, ALU.mult))
                vs.step(nc.vector.scalar_tensor_tensor(out=u, in0=v4, scalar=0.25, in1=d2, op0=ALU.mult, op1=ALU.mult))
                vs.step(nc.vector.tensor_scalar(u, u, EPS, None, ALU.add))
                rsqrt(vs, r2, u, TB)
                vs.step(nc.vector.tensor_tensor(r, r, r2, ALU.mult))
            nc.vector.scalar_tensor_tensor(out=nmr[:, lo:hi], in0=mean[:, lo:hi], scalar=-1.0, in1=r,
                                           op0=ALU.mult, op1=ALU.mult).then_inc(n.stat, 1)
            for t in range(lo, hi, 2):
                ins = nc.vector.tensor_scalar(xl[:, t, :], x[:, t, :], mean[:, t:t + 1], rstd[:, t:t + 1],
                                              ALU.subtract, ALU.mult)
            ins.then_inc(n.xl_v, 1)

        def norm_scalar_apply(act, n, half):
            act.wait_ge(n.stat, 2 * n.k + half + 1)
            for t in range(TB * half + 1, TB * (half + 1), 2):
                ins = nc.scalar.activation(xl[:, t, :], x[:, t, :], ACT.Identity, bias=nmr[:, t:t + 1],
                                           scale=rstd[:, t:t + 1])
            ins.then_inc(n.xl_a, 1)

        def norm_tensor(pe, n, half):
            pe.wait_ge(n.xl_v, 2 * n.k + half + 1)
            pe.wait_ge(n.xl_a, 2 * n.k + half + 1)
            for g in range(2):
                if half == 1:
                    pe.wait_ge(n.xt_a if g == 0 else n.xt_v, 2 * n.k + 1)
                for j in range(4):
                    ins = pe.transpose(ps[:, 6 + g, j * P:(j + 1) * P], xl[:, TB * half + 4 * g + j, :], cc("ident"))
                ins.then_inc(n.tp, 1)

        def xt_out(half, g, permuted):
            if permuted:
                v = xt[:, half, PAD:PAD + S].rearrange("c (j r) -> c j r", j=8)[:, :, 64 * g:64 * g + 64]
                return v
            return xt[:, half, PAD + 512 * g:PAD + 512 * (g + 1)]

        def norm_xt_in(g, permuted):
            if permuted:
                return ps[:, 6 + g, :].rearrange("c (r j) -> c j r", j=8)
            return ps[:, 6 + g, :]

        def norm_scalar_xt(act, n, half, permuted=False, affine=False):
            act.wait_ge(n.tp, 4 * n.k + 2 * half + 1)
            if affine:
                ins = nc.scalar.activation(xt_out(half, 0, permuted), norm_xt_in(0, permuted), ACT.Identity,
                                           bias=wc("beta"), scale=wc("gamma"))
            else:
                ins = nc.scalar.activation(xt_out(half, 0, permuted), norm_xt_in(0, permuted), ACT.Copy)
            ins.then_inc(n.xt_a, 1)

        def norm_vector_xt(dve, n, half, permuted=False, affine=False):
            dve.wait_ge(n.tp, 4 * n.k + 2 * half + 2)
            if affine:
                ins = nc.vector.tensor_scalar(xt_out(half, 1, permuted), norm_xt_in(1, permuted), wc("gamma"),
                                              wc("beta"), ALU.mult, ALU.add)
            else:
                ins = nc.vector.tensor_copy(xt_out(half, 1, permuted), norm_xt_in(1, permuted))
            ins.then_inc(n.xt_v, 1)

        class Ffn:
            def __init__(self, f):
                self.mixed = sem(f"f{f}_mixed")
                self.k, self.r, self.v = sem(f"f{f}_k"), sem(f"f{f}_r"), sem(f"f{f}_v")
                self.relu, self.ka = sem(f"f{f}_relu"), sem(f"f{f}_relu_squared")
                self.rs = sem(f"f{f}_sigmoid")
                self.done = sem(f"f{f}_gated")

        f_xd = arena_f(0, B, S)
        f_xr = arena_f(2048, B, S)
        f_xk = arena_f(4096, B, S)
        f_relu = arena_f(6144, 4, 512)
        f_ka = arena_f(8192, 4, 512)
        f_rs = arena_f(10240, 4, 512)
        f_t = arena_f(12288, 4, 512)

        def ffn_vector_mix(dve, vs, n, f, half):
            dve.wait_ge(n.xt_a, 2 * n.k + half + 1)
            dve.wait_ge(n.xt_v, 2 * n.k + half + 1)
            cur, prev = xt[:, half, PAD:PAD + S], xt[:, half, PAD - 1:PAD - 1 + S]
            vs.step(nc.vector.tensor_tensor(f_xd[:, half, :], cur, prev, ALU.subtract))
            nc.vector.scalar_tensor_tensor(out=f_xk[:, half, :], in0=f_xd[:, half, :], scalar=wc("mu_k"), in1=prev,
                                           op0=ALU.mult, op1=ALU.add).then_inc(f.mixed, 1)
            nc.vector.scalar_tensor_tensor(out=f_xr[:, half, :], in0=f_xd[:, half, :], scalar=wc("mu_r"), in1=prev,
                                           op0=ALU.mult, op1=ALU.add).then_inc(f.mixed, 1)

        def ffn_tensor(pe, f, half):
            for q in (2 * half, 2 * half + 1):
                pe.wait_ge(f.mixed, 2 * half + 1)
                if half:
                    pe.wait_ge(f.relu, q - 1)
                at = 512 * (q % 2)
                pe.matmul(ps[:, q % 2, :], wc("ffn_k"), f_xk[:, half, at:at + 512], start=True, stop=True).then_inc(f.k, 1)
            for q in (2 * half, 2 * half + 1):
                pe.wait_ge(f.mixed, 2 * half + 2)
                if half:
                    pe.wait_ge(f.rs, q - 1)
                for j in range(4):
                    at = 512 * (q % 2) + j * P
                    ins = pe.matmul(ps[:, 2 + q % 2, j * P:(j + 1) * P], f_xr[:, half, at:at + P], wc("ffn_r"),
                                    start=True, stop=True)
                ins.then_inc(f.r, 1)
            for q in (2 * half, 2 * half + 1):
                pe.wait_ge(f.ka, q + 1)
                if half:
                    pe.wait_ge(f.done, q - 1)
                for j in range(4):
                    ins = pe.matmul(ps[:, 4 + q % 2, j * P:(j + 1) * P], f_ka[:, q, j * P:(j + 1) * P], wc("ffn_v"),
                                    start=True, stop=True)
                ins.then_inc(f.v, 1)

        def ffn_scalar(act, f, half):
            for q in (2 * half, 2 * half + 1):
                act.wait_ge(f.k, q + 1)
                nc.scalar.activation(f_relu[:, q, :], ps[:, q % 2, :], ACT.Relu).then_inc(f.relu, 1)
                act.wait_ge(f.relu, q + 1)
                nc.scalar.activation(f_ka[:, q, :], f_relu[:, q, :], ACT.Square).then_inc(f.ka, 1)
            for q in (2 * half, 2 * half + 1):
                act.wait_ge(f.r, q + 1)
                nc.scalar.activation(f_rs[:, q, :], ps[:, 2 + q % 2, :], ACT.Sigmoid).then_inc(f.rs, 1)

        def ffn_vector_add(dve, vs, f, half):
            for q in (2 * half, 2 * half + 1):
                dve.wait_ge(f.rs, q + 1)
                dve.wait_ge(f.v, q + 1)
                nc.vector.tensor_tensor(f_t[:, q, :], ps[:, 4 + q % 2, :], f_rs[:, q, :], ALU.mult).then_inc(f.done, 1)
                dve.wait_ge(f.done, q + 1)
                xq = x[:, 4 * q:4 * q + 4, :]
                vs.step(nc.vector.scalar_tensor_tensor(
                    out=xq, in0=f_t[:, q, :].rearrange("p (a b) -> p a b", a=4), scalar=0.5, in1=xq,
                    op0=ALU.mult, op1=ALU.add))

        NQ = 4
        a_qs = arena_b(0, B, NH, S)
        a_ks = arena_b(8192, B, NH, S)
        a_v = arena_f(16384, NT, NH, 32)
        a_p = arena_f(20480, 8, S)
        a_parts = arena_b(20480, B, 6, S)
        a_f = arena_f(20480 + 6144, S)
        a_r = arena_f(20480 + 7168, S)
        a_ot = arena_f(28672, S)
        a_tmp = arena_f(29696, 2, 4, P)
        a_nm = arena_f(30720, 2, 2, 8)
        a_nmr = arena_f(30752, 4, 8)
        a_nmb = arena_b(30784, 2, 24)
        a_nmt = arena_b(30832, 2, P)
        a_rd = arena_f(30960, 8, 4)

        class a:
            raw, f32 = sem("a_qk_product"), sem("a_qk_float")
            p1, r1, p2, p3 = sem("a_part1"), sem("a_rest1"), sem("a_part2"), sem("a_part3")
            vps, v = sem("a_values_product"), sem("a_values")
            stored = [sem(f"a_parts_stored{b}") for b in range(B)]
            stack = [sem(f"a_stack{i}") for i in range(4)]
            onesk = sem("a_ones_set")
            mp, mpu = sem("a_ring_filled"), sem("a_ring_taken")
            nm = sem("a_negmax_parts")
            nmrow = [sem(f"a_negmax_rows{i}") for i in range(B * NH)]
            st, ex, av = sem("a_scores"), sem("a_probs"), sem("a_values_summed")
            ot_a, ot_v = sem("a_out_by_scalar"), sem("a_out_by_vector")
            otp, done = sem("a_out_turned"), sem("a_out_normalised")

        HEADS = [(b, h) for b in range(B) for h in range(NH)]

        ring = []
        for hd in range(len(HEADS)):
            for u in range(16):
                ring.append(("mp", hd, u))
                if u == 2 and hd:
                    ring.append(("turn", hd - 1, 0))
        ring.append(("turn", len(HEADS) - 1, 0))
        turn_at = {hd: i for i, (k, hd, u) in enumerate(ring) if k == "turn"}
        ring_before = [turn_at[4 * q + 3] + 1 for q in range(4)] + [len(ring)]

        def ring_upto(quad, slot):
            lo, hi = ring_before[quad], ring_before[quad + 1]
            return min(hi, lo + (slot * (hi - lo) + 29) // 30)

        def att_tensor_project(pe, n, half):
            pe.wait_ge(n.xt_a, 2 * n.k + half + 1)
            pe.wait_ge(n.xt_v, 2 * n.k + half + 1)
            if half == 0:
                pe.wait_ge(s_wvs, 2)
            for i, name in enumerate(("att_q", "att_k")):
                if half:
                    pe.wait_ge(a.f32, i + 1)
                for g in range(2):
                    ins = pe.matmul(ps[:, 2 * i + g, :], wc(name), xt[:, half, PAD + 512 * g:PAD + 512 * (g + 1)],
                                    start=True, stop=True)
                ins.then_inc(a.raw, 1)
            if half:
                pe.wait_ge(a.v, 1)
            for t in range(TB):
                ins = pe.matmul(ps[:, 4 + t // 4, (t % 4) * P:(t % 4 + 1) * P],
                                xt[:, half, PAD + t * P:PAD + (t + 1) * P], wvs[:, :], start=True, stop=True)
            ins.then_inc(a.vps, 1)

        def att_scalar_project(act, half):
            for i in range(2):
                u = 2 * half + i
                act.wait_ge(a.raw, u + 1)
                if u:
                    act.wait_ge(a.r1, u)
                nc.scalar.activation(a_f[:, :].rearrange("p (a b) -> p a b", a=2), ps[:, 2 * i:2 * i + 2, :],
                                     ACT.Identity, bias=wc("bq" if i == 0 else "bk")).then_inc(a.f32, 1)
                act.wait_ge(a.f32, u + 1)
                nc.scalar.activation(a_parts[:, half, 3 * i, :], a_f[:, :], ACT.Copy).then_inc(a.p1, 1)
                act.wait_ge(a.r1, u + 1)
                nc.scalar.activation(a_parts[:, half, 3 * i + 1, :], a_r[:, :], ACT.Copy).then_inc(a.p2, 1)

        def att_vector_project(dve, half):
            for i in range(2):
                u = 2 * half + i
                dve.wait_ge(a.p1, u + 1)
                if u:
                    dve.wait_ge(a.p3, u)
                nc.vector.tensor_tensor(a_r[:, :], a_f[:, :], a_parts[:, half, 3 * i, :], ALU.subtract).then_inc(a.r1, 1)
                if i == 0:
                    dve.wait_ge(a.vps, half + 1)
                    nc.vector.tensor_tensor(
                        a_v[:, TB * half:TB * (half + 1), :, 0:DK],
                        ps[:, 4:6, :].rearrange("p a (b c d) -> p (a b) c d", b=4, c=NH),
                        bc(bvs[:, :].rearrange("p (c d) -> p c d", c=NH).unsqueeze(1), [P, TB, NH, DK]),
                        ALU.add).then_inc(a.v, 1)
                dve.wait_ge(a.r1, u + 1)
                dve.wait_ge(a.p2, u + 1)
                nc.vector.tensor_tensor(a_parts[:, half, 3 * i + 2, :], a_r[:, :], a_parts[:, half, 3 * i + 1, :],
                                        ALU.subtract).then_inc(a.p3, 1)

        def att_sync_stack(sp):
            for b in range(B):
                for i in range(2):
                    sp.wait_ge(a.p3, 2 * b + i + 1)
                    sp.dma_start(scratch[b, i].rearrange("k p s -> p k s"),
                                 a_parts[:, b, 3 * i:3 * i + 3, :]).then_inc(a.stored[b], 16)
                for quad in range(2):
                    sp.wait_ge(a.stored[b], 32)
                    hs = slice(4 * quad, 4 * quad + 4)
                    for i, dst, rows in ((0, a_qs, (0, 0, 0, 1, 1, 2)), (1, a_ks, (0, 1, 2, 0, 1, 0))):
                        for g, part in enumerate(rows):
                            src = scratch[b, i, part].rearrange("(h d) s -> d h s", d=DK)[:, hs, :]
                            sp.dma_start(dst[16 * g:16 * g + 16, b, hs, :], src).then_inc(a.stack[2 * b + quad], 16)

        def att_sync_negmax_rows(sp):
            for hd, (b, h) in enumerate(HEADS):
                sp.wait_ge(a.mpu, turn_at[hd] + 1)
                sp.dma_start(a_qs[96:99, b, h, :].rearrange("i (j s) -> i j s", j=8),
                             a_nmt[0:24, hd % 2, :]).then_inc(a.nmrow[hd], 16)

        def att_tensor(pe):
            class done:
                ring = 0

            def ring_units(upto):
                while done.ring < upto:
                    u = done.ring
                    kind, hd, k = ring[u]
                    b, h = HEADS[hd]
                    bank = 6 + u % 2
                    if kind == "mp":
                        if k == 0 and hd % 4 == 0:
                            pe.wait_ge(a.stack[hd // 4], 16 * 12)
                        if u >= 2:
                            pe.wait_ge(a.mpu, u - 1)
                        j, half = k // 2, k % 2
                        pe.matmul(ps[:, bank, :], a_qs[0:96, b, h, j * P:(j + 1) * P],
                                  a_ks[0:96, b, h, half * 512:(half + 1) * 512], start=True, stop=True).then_inc(a.mp, 1)
                    else:
                        pe.wait_ge(a.nm, hd + 1)
                        pe.wait_ge(a.mpu, u - 1)
                        pe.transpose(ps[0:24, bank, 0:64].bitcast(BF16), a_nmb[:, hd % 2, :], identb[:, :])\
                            .then_inc(a.mp, 1)
                    done.ring += 1

            def scores(v):
                step, h4 = v // 4, v % 4
                quad, i = step // 8, step % 8
                b, h = HEADS[4 * quad + h4]
                if i == 0:
                    pe.wait_ge(a.nmrow[4 * quad + h4], 16)
                if v >= 2:
                    pe.wait_ge(a.ex, v - 1)
                for half in range(2):
                    ins = pe.matmul(ps[:, 2 * (v % 2) + half, :], a_ks[0:99, b, h, i * P:(i + 1) * P],
                                    a_qs[0:99, b, h, half * 512:(half + 1) * 512], start=True, stop=True)
                ins.then_inc(a.st, 1)

            def values(step):
                quad, i = step // 8, step % 8
                b = HEADS[4 * quad][0]
                if i == 0 and quad:
                    pe.wait_ge(a.done, quad)
                pe.wait_ge(a.ex, 4 * step + 4)
                for half in range(2):
                    for h4 in range(4):
                        h = HEADS[4 * quad + h4][1]
                        ins = pe.matmul(ps[32 * h4:32 * h4 + 32, 4 + half, :], a_v[:, TB * b + i, h, :],
                                        a_p[:, (4 * step + h4) % 8, half * 512:(half + 1) * 512],
                                        start=(i == 0), stop=(i == 7))
                ins.then_inc(a.av, 1)

            def turn_out(quad):
                pe.wait_ge(a.ot_a, quad + 1)
                pe.wait_ge(a.ot_v, quad + 1)
                for j in range(8):
                    ins = pe.transpose(ps[:, 4 + j // 4, (j % 4) * P:(j % 4 + 1) * P], a_ot[:, j * P:(j + 1) * P],
                                       cc("ident"))
                ins.then_inc(a.otp, 1)

            pe.wait_ge(a.v, 2)
            ring_units(ring_before[0])
            for step in range(32):
                quad = step // 8
                for h4 in range(4):
                    scores(4 * step + h4)
                    ring_units(ring_upto(quad, 4 * (step % 8) + h4 + 1))
                if step % 8 == 1 and quad:
                    turn_out(quad - 1)
                if step:
                    values(step - 1)
                if step == 31:
                    values(31)
                    turn_out(3)

        def att_vector(dve, vs):
            class done:
                ring = 0

            def ring_units(upto):
                while done.ring < upto:
                    u = done.ring
                    kind, hd, k = ring[u]
                    dve.wait_ge(a.mp, u + 1)
                    if kind == "mp":
                        nc.vector.tensor_reduce(a_nm[:, hd % 2, k % 2, k // 2:k // 2 + 1], ps[:, 6 + u % 2, :], AX.X,
                                                ALU.max, negate=True).then_inc(a.mpu, 1)
                        if k == 15:
                            dve.wait_ge(a.mpu, u + 1)
                            nm, r1, r2 = a_nmr[:, 0, :], a_nmr[:, 1, :], a_nmr[:, 2, :]
                            parts = a_nmb[:, hd % 2, :].rearrange("p (i j) -> p i j", i=3)
                            vs.step(nc.vector.tensor_tensor(nm, a_nm[:, hd % 2, 0, :], a_nm[:, hd % 2, 1, :], ALU.min))
                            vs.step(nc.vector.tensor_copy(parts[:, 0, :], nm))
                            vs.step(nc.vector.tensor_tensor(r1, nm, parts[:, 0, :], ALU.subtract))
                            vs.step(nc.vector.tensor_copy(parts[:, 1, :], r1))
                            nc.vector.tensor_tensor(parts[:, 2, :], r1, parts[:, 1, :], ALU.subtract).then_inc(a.nm, 1)
                    else:
                        if hd >= 2:
                            dve.wait_ge(a.nmrow[hd - 2], 16)
                        nc.vector.tensor_copy(a_nmt[0:24, hd % 2, :], ps[0:24, 6 + u % 2, 0:64].bitcast(BF16))\
                            .then_inc(a.mpu, 1)
                    done.ring += 1

            def out_copy(quad):
                dve.wait_ge(a.av, 8 * (quad + 1))
                if quad:
                    dve.wait_ge(a.otp, quad)
                nc.vector.tensor_copy(a_ot[:, 512:1024], ps[:, 5, :]).then_inc(a.ot_v, 1)

            def out_add(quad):
                dve.wait_ge(a.otp, quad + 1)
                b, h0 = HEADS[4 * quad]
                o = ps[:, 4:6, :].rearrange("p a (j h e) -> p (a j) h e", j=4, h=4)
                vs.step(nc.vector.reciprocal(a_rd[:, :, :], o[:, :, :, DK]))
                for half in range(2):
                    dst = a_tmp[:, quad % 2, :, :].rearrange("p h (j g) -> p j h g", j=8)[:, 4 * half:4 * half + 4]
                    ins = nc.vector.tensor_tensor(
                        dst, o[:, 4 * half:4 * half + 4, :, 0:DK],
                        bc(a_rd[:, 4 * half:4 * half + 4, :].unsqueeze(3), [P, 4, 4, DK]), ALU.mult)
                ins.then_inc(a.done, 1)
                dve.wait_ge(a.done, quad + 1)
                xq = x[:, TB * b + h0:TB * b + h0 + 4, :]
                vs.step(nc.vector.tensor_tensor(xq, xq, a_tmp[:, quad % 2, :, :], ALU.add))

            ring_units(ring_before[0])
            for quad in range(4):
                if quad:
                    ring_units(ring_upto(quad, 4))
                    out_copy(quad - 1)
                    ring_units(ring_upto(quad, 8))
                    out_add(quad - 1)
                ring_units(ring_before[quad + 1])
            out_copy(3)
            out_add(3)

        def att_scalar(act):
            for b in range(B):
                act.wait_ge(a.stored[b], 32)
            for v in range(128):
                step = v // 4
                if v % 32 == 4 and v > 4:
                    quad = v // 32 - 1
                    act.wait_ge(a.av, 8 * (quad + 1))
                    if quad:
                        act.wait_ge(a.otp, quad)
                    nc.scalar.activation(a_ot[:, 0:512], ps[:, 4, :], ACT.Copy).then_inc(a.ot_a, 1)
                if step >= 2:
                    act.wait_ge(a.av, step - 1)
                act.wait_ge(a.st, v + 1)
                nc.scalar.activation(a_p[:, v % 8, :].rearrange("p (a b) -> p a b", a=2),
                                     ps[:, 2 * (v % 2):2 * (v % 2) + 2, :], ACT.Exp, scale=0.25).then_inc(a.ex, 1)
            act.wait_ge(a.av, 32)
            act.wait_ge(a.otp, 3)
            nc.scalar.activation(a_ot[:, 0:512], ps[:, 4, :], ACT.Copy).then_inc(a.ot_a, 1)

        def att_pool_set(pool):
            nc.gpsimd.memset(a_ks[96:99, :, :, :], 1.0).then_inc(a.onesk, 1)
            pool.wait_ge(a.onesk, 1)
            nc.gpsimd.memset(a_v[:, :, :, DK:32], 0.0).then_inc(a.onesk, 1)
            pool.wait_ge(a.onesk, 2)
            nc.gpsimd.memset(a_v[:, :, :, DK:DK + 1], 1.0).then_inc(a.onesk, 1)


        class Mix:
            def __init__(self, m):
                self.logits, self.e = sem(f"m{m}_logits"), sem(f"m{m}_logit_gap")
                self.w, self.wt, self.wtc = sem(f"m{m}_weights"), sem(f"m{m}_weights_turned"), sem(f"m{m}_weights_by_expert")
                self.h, self.hc, self.hq, self.sqr = sem(f"m{m}_h"), sem(f"m{m}_h_copied"), sem(f"m{m}_h_squared"), sem(f"m{m}_h_sums")
                self.z, self.zt, self.ac = sem(f"m{m}_normed"), sem(f"m{m}_normed_turned"), sem(f"m{m}_gelu")
                self.y, self.tmp, self.done = sem(f"m{m}_y"), sem(f"m{m}_y_weighted"), sem(f"m{m}_x_added")

        m_s = arena_f(0, 10, NT, NE)
        m_wt = arena_f(2560, NT * P)
        m_h = arena_f(4608, 2, 4, 512)
        m_sq = arena_f(8704, 2, 512)
        m_z = arena_f(9728, 2, 4, 512)
        m_a = arena_f(13824, 4, 512)
        m_tmp = arena_f(15872, 4, 512)
        m_ss = arena_f(17920, 2, 16)
        m_rs = arena_f(17952, 2, 16)
        m_e = arena_f(17984, 4, NT)
        m_w = m_s[:, 9]
        NSU = 16

        def mix_tensor_logits(pe, n, m, half):
            pe.wait_ge(n.xt_a, 2 * n.k + half + 1)
            pe.wait_ge(n.xt_v, 2 * n.k + half + 1)
            for t in range(TB * half, TB * (half + 1)):
                at = PAD + (t % TB) * P
                ins = pe.matmul(ps[:, 4, t * NE:(t + 1) * NE], xt[:, half, at:at + P], wc("router"), start=True, stop=True)
            ins.then_inc(m.logits, 1)

        def mix_vector_route(dve, vs, m):
            lg, t, oh1, oh2, l2 = (m_s[:, i] for i in range(5))
            m1, m2, d, r = (m_e[:, i, :] for i in range(4))
            full = [P, NT, NE]
            dve.wait_ge(m.logits, 2)
            vs.step(nc.vector.tensor_tensor(lg, ps[:, 4, 0:NT * NE].rearrange("p (t e) -> p t e", e=NE),
                                            bc(rc("br").unsqueeze(1), full), ALU.add))
            rank = bc(cc("rank").unsqueeze(1), full)
            src = lg
            for mx, oh in ((m1, oh1), (m2, oh2)):
                vs.step(nc.vector.tensor_reduce(mx, src, AX.X, ALU.max))
                vs.step(nc.vector.tensor_tensor(t, src, bc(mx.unsqueeze(2), full), ALU.is_equal))
                vs.step(nc.vector.tensor_tensor(t, t, rank, ALU.mult))
                vs.step(nc.vector.tensor_reduce(r, t, AX.X, ALU.max))
                vs.step(nc.vector.tensor_tensor(oh, t, bc(r.unsqueeze(2), full), ALU.is_equal))
                if src is lg:
                    vs.step(nc.vector.scalar_tensor_tensor(out=l2, in0=oh, scalar=-3.0e38, in1=lg, op0=ALU.mult,
                                                           op1=ALU.add))
                src = l2
            nc.vector.tensor_tensor(d, m2, m1, ALU.subtract).then_inc(m.e, 1)
            dve.wait_ge(m.e, 2)
            vs.step(nc.vector.tensor_scalar(r, d, 1.0, 2.0, ALU.add, ALU.mult))
            vs.step(nc.vector.reciprocal(m1, r))
            vs.step(nc.vector.tensor_tensor(m2, d, m1, ALU.mult))
            nc.vector.tensor_tensor(oh1, oh1, bc(m1.unsqueeze(2), full), ALU.mult)
            vs.step(nc.vector.tensor_tensor(oh2, oh2, bc(m2.unsqueeze(2), full), ALU.mult))
            nc.vector.tensor_tensor(m_w, oh1, oh2, ALU.add).then_inc(m.w, 1)

        def mix_scalar_route(act, m):
            act.wait_ge(m.e, 1)
            nc.scalar.activation(m_e[:, 2, :], m_e[:, 2, :], ACT.Exp).then_inc(m.e, 1)

        def mix_tensor(pe, n, m):
            def hidden(s, j):
                u = 4 * s + j
                q, eq = s // 4, s % 4
                half, at = q // 2, PAD + 512 * (q % 2) + j * P
                if u == 0:
                    pe.wait_ge(s_b1row, 48)
                    pe.wait_ge(s_set, 3)
                if u >= 2:
                    pe.wait_ge(m.hq, u - 1)
                pe.matmul(ps[:, u % 2, :], ones3[:, :], b1row[:, 512 * eq:512 * (eq + 1)], start=True, stop=False)
                pe.matmul(ps[:, u % 2, :], xt[:, half, at:at + P],
                          w1[:, 4 * eq:4 * eq + 4, :].rearrange("c e f -> c (e f)"), start=False, stop=True)\
                    .then_inc(m.h, 1)

            def turn(s, e):
                u = 4 * s + e
                pe.wait_ge(m.z, 4 * s + 4)
                if u >= 2:
                    pe.wait_ge(m.ac, u - 1)
                for j in range(4):
                    ins = pe.transpose(ps[:, 2 + u % 2, j * P:(j + 1) * P], m_z[:, s % 2, j, e * P:(e + 1) * P], cc("ident"))
                ins.then_inc(m.zt, 1)

            def out(s, e):
                u = 4 * s + e
                v = u + s // 4
                pe.wait_ge(m.ac, u + 1)
                if v >= 2:
                    pe.wait_ge(m.tmp, v - 1)
                if v < 2:
                    pe.wait_ge(m.w, 1)
                for j in range(4):
                    ins = pe.matmul(ps[:, 4 + v % 2, j * P:(j + 1) * P], m_a[:, u % 4, j * P:(j + 1) * P],
                                    w2[:, 4 * (s % 4) + e, :], start=True, stop=True)
                ins.then_inc(m.y, 1)

            def out_bias(q):
                v = 17 * q + 16
                if q == 0:
                    pe.wait_ge(m.wtc, 1)
                pe.wait_ge(m.tmp, v - 1)
                for j in range(4):
                    ins = pe.matmul(ps[:, 4 + v % 2, j * P:(j + 1) * P],
                                    m_wt[0:NE, (4 * q + j) * P:(4 * q + j + 1) * P], b2[:, :], start=True, stop=True)
                ins.then_inc(m.y, 1)

            def turn_weights():
                pe.wait_ge(m.w, 1)
                for g in range(2):
                    for k in range(8):
                        t = 8 * g + k
                        if k == 4 or (g and k == 0):
                            pass
                        ins = pe.transpose(ps[0:NE, 6 + (k // 4), (k % 4) * P:(k % 4 + 1) * P],
                                           m_w[:, t, :], cc("ident"))
                    ins.then_inc(m.wt, 1)
                    if g == 0:
                        pe.wait_ge(m.wtc, 1)

            for j in range(4):
                hidden(0, j)
            for j in range(4):
                hidden(1, j)
            turn_weights()
            for s in range(NSU):
                for e in range(4):
                    if s + 2 < NSU:
                        hidden(s + 2, e)
                    turn(s, e)
                    if e:
                        out(s, e - 1)
                out(s, 3)
                if s % 4 == 3:
                    out_bias(s // 4)

        def mix_scalar(act, m):
            def hidden(s, j):
                u = 4 * s + j
                if s >= 2 and j == 0:
                    act.wait_ge(m.z, 4 * (s - 2) + 4)
                act.wait_ge(m.h, u + 1)
                nc.scalar.activation(m_h[:, s % 2, j, :], ps[:, u % 2, :], ACT.Copy).then_inc(m.hc, 1)
                if u >= 2:
                    act.wait_ge(m.sqr, u - 1)
                nc.scalar.activation(m_sq[:, u % 2, :], ps[:, u % 2, :], ACT.Square).then_inc(m.hq, 1)

            for s in range(2):
                for j in range(4):
                    hidden(s, j)
            for g in range(2):
                act.wait_ge(m.wt, g + 1)
                nc.scalar.activation(m_wt[0:NE, 1024 * g:1024 * (g + 1)].rearrange("p (a b) -> p a b", a=2),
                                     ps[0:NE, 6:8, :], ACT.Copy).then_inc(m.wtc, 1)
            for s in range(NSU):
                for e in range(4):
                    if s + 2 < NSU:
                        hidden(s + 2, e)
                    u = 4 * s + e
                    ex = 4 * (s % 4) + e
                    act.wait_ge(m.zt, u + 1)
                    if u >= 4:
                        act.wait_ge(m.y, u - 4 + (u - 4) // 16 + 1)
                    nc.scalar.activation(m_a[:, u % 4, :], ps[:, 2 + u % 2, :], ACT.Gelu,
                                         bias=wc("be1")[:, ex:ex + 1], scale=wc("g1")[:, ex:ex + 1]).then_inc(m.ac, 1)

        def mix_vector(dve, vs, m):
            def squares(s, j):
                u = 4 * s + j
                dve.wait_ge(m.hq, u + 1)
                nc.vector.tensor_reduce(m_ss[:, s % 2, 4 * j:4 * j + 4],
                                        m_sq[:, u % 2, :].rearrange("p (e f) -> p e f", e=4), AX.X, ALU.add)\
                    .then_inc(m.sqr, 1)

            def rstds(s):
                dve.wait_ge(m.sqr, 4 * s + 4)
                v = m_ss[:, s % 2, :]
                vs.step(nc.vector.tensor_scalar(v, v, 1.0 / P, EPS, ALU.mult, ALU.add))
                rsqrt(vs, m_rs[:, s % 2, :], v, 16)

            def scaled(s, j):
                dve.wait_ge(m.hc, 4 * s + 4)
                if s >= 2 and j == 0:
                    dve.wait_ge(m.zt, 4 * (s - 2) + 4)
                nc.vector.tensor_tensor(
                    m_z[:, s % 2, j, :].rearrange("p (e f) -> p e f", e=4),
                    m_h[:, s % 2, j, :].rearrange("p (e f) -> p e f", e=4),
                    bc(m_rs[:, s % 2, 4 * j:4 * j + 4].unsqueeze(2), [P, 4, P]), ALU.mult).then_inc(m.z, 1)

            def weighted(v):
                q, k = v // 17, v % 17
                dve.wait_ge(m.y, v + 1)
                if v >= 4:
                    dve.wait_ge(m.done, v - 3)
                y = ps[:, 4 + v % 2, :].rearrange("p (j o) -> p j o", j=4)
                dst = m_tmp[:, v % 4, :].rearrange("p (j o) -> p j o", j=4)
                if k < 16:
                    wgt = m_w[:, 4 * q:4 * q + 4, k:k + 1]
                    nc.vector.tensor_tensor(dst, y, bc(wgt, [P, 4, P]), ALU.mult).then_inc(m.tmp, 1)
                else:
                    nc.vector.tensor_copy(dst, y).then_inc(m.tmp, 1)

            for j in range(4):
                squares(0, j)
            rstds(0)
            for j in range(4):
                squares(1, j)
            for j in range(4):
                scaled(0, j)
            rstds(1)
            for s in range(NSU):
                v0 = 4 * s + s // 4
                for j in range(4):
                    if s + 2 < NSU:
                        squares(s + 2, j)
                    if s + 1 < NSU:
                        scaled(s + 1, j)
                    if j:
                        weighted(v0 + j - 1)
                weighted(v0 + 3)
                if s % 4 == 3:
                    weighted(v0 + 4)
                if s + 2 < NSU:
                    rstds(s + 2)

        def mix_pool(pool, m, stored=None):
            for v in range(68):
                q = v // 17
                pool.wait_ge(m.tmp, v + 1)
                if v:
                    pool.wait_ge(m.done, v)
                xq = x[:, 4 * q:4 * q + 4, :]
                nc.gpsimd.tensor_tensor(xq, xq, m_tmp[:, v % 4, :].rearrange("p (j o) -> p j o", j=4), ALU.add)\
                    .then_inc(m.done, 1)

        NG = 3 * P + 2 * NH
        l_g = arena_f(0, NT, NG)
        l_q = arena_f(6400, NT, P)
        l_k = arena_f(8448, NT, P)
        l_tv = arena_f(10496, 4, 512)
        l_tp = arena_f(12544, 4, 512)
        l_gate = arena_f(14592, NT, 2 * NH)
        l_ln = arena_f(14848, NT, NH)
        l_dq = arena_f(14976, NT, NH)
        l_dk = arena_f(15104, NT, NH)
        l_lnx = arena_f(15616, NT, P)
        l_ot = arena_f(15616, NT, P)
        l_qm = arena_f(17664, 2, NT * P)
        l_kt = arena_f(21760, NT * P)
        l_as = arena_f(23808, 2, NH, P)
        l_s = arena_f(25856, NT, P)
        l_te = arena_f(27904, NT, P)
        l_et = arena_f(29952, NT)
        l_o = arena_f(30080, NT, P)

        class l:
            g, g_in = sem("l_products"), sem("l_products_in")
            gate, sig, bet, ln, lnx = sem("l_gates"), sem("l_sigmoids"), sem("l_beta"), sem("l_ln_beta"), sem("l_ln_beta_wide")
            cum, dec, dk = sem("l_sums"), sem("l_decays"), sem("l_key_decay")
            q, kp = sem("l_q"), sem("l_k_steps")
            qt, qm, kt, ktc = sem("l_q_turned"), sem("l_q_in"), sem("l_k_turned"), sem("l_k_in")
            kv, te, s = sem("l_kv"), sem("l_kv_in"), sem("l_states")
            sc, as_ = sem("l_scores"), sem("l_scores_masked")
            o, oc, ot, otc = sem("l_out"), sem("l_out_in"), sem("l_out_turned"), sem("l_out_turned_in")
            done, y, bo = sem("l_projected"), sem("l_x_added"), sem("l_bias_added")

        def lin_tensor(pe, n):
            for t in range(NT):
                half = t // TB
                if t % TB == 0:
                    pe.wait_ge(n.xt_a, 2 * n.k + half + 1)
                    pe.wait_ge(n.xt_v, 2 * n.k + half + 1)
                if t >= 2:
                    pe.wait_ge(l.g_in, t - 1)
                at = PAD + (t % TB) * P
                pe.matmul(ps[:, t % 2, 0:NG], xt[:, half, at:at + P], wc("lin_qkvab"), start=True, stop=True).then_inc(l.g, 1)
            pe.wait_ge(l.lnx, 1)
            pe.matmul(ps[:, 4, 0:P], cc("causal"), l_ln.rearrange("p t h -> p (t h)"), start=True, stop=True)
            for t in range(NT):
                ins = pe.matmul(ps[:, 4, 256 + t:257 + t], l_lnx[:, t, :], cc("ones"), start=True, stop=True)
            ins.then_inc(l.cum, 1)
            pe.wait_ge(l.q, 2)
            for g in range(4):
                if g >= 2:
                    pe.wait_ge(l.qm, 2 * (g - 1))
                for j in range(4):
                    ins = pe.transpose(ps[:, 2 + g % 2, j * P:(j + 1) * P], l_q[:, 4 * g + j, :], cc("ident"))
                ins.then_inc(l.qt, 1)
            pe.wait_ge(l.kp, 14)
            for g in range(4):
                if g >= 2:
                    pe.wait_ge(l.ktc, g - 1)
                for j in range(4):
                    ins = pe.transpose(ps[:, 6 + g % 2, j * P:(j + 1) * P], l_k[:, 4 * g + j, :], cc("ident"))
                ins.then_inc(l.kt, 1)
                if g == 0:
                    pe.wait_ge(l.g_in, NT)
                if g >= 2:
                    pe.wait_ge(l.te, g - 1)
                for j in range(4):
                    t = 4 * g + j
                    ins = pe.matmul(ps[:, g % 2, j * P:(j + 1) * P], l_k[:, t, :], l_g[:, t, 2 * P:3 * P], start=True, stop=True)
                ins.then_inc(l.kv, 1)
            pe.wait_ge(l.te, 4)
            pe.wait_ge(l.qm, 8)
            pe.wait_ge(l.ktc, 4)
            pe.wait_ge(l.dec, 3)

            def scores(t):
                if t:
                    pe.wait_ge(l.as_, t)
                for i in range(4):
                    r = slice(32 * i, 32 * i + 32)
                    ins = pe.matmul(ps[:, i, 0:256], l_kt[r, t * P:(t + 1) * P], l_qm[r, :, t * P:(t + 1) * P],
                                    start=True, stop=True)
                ins.then_inc(l.sc, 1)

            def values(t):
                if t >= 2:
                    pe.wait_ge(l.oc, t - 1)
                pe.wait_ge(l.s, 1)
                for par in range(2):
                    pe.matmul(ps[:, 4 + t % 2, 0:P], l_qm[:, par, t * P:(t + 1) * P], l_s[:, t, :],
                              start=(par == 0), stop=False)
                pe.wait_ge(l.as_, t + 1)
                for h in range(NH):
                    ins = pe.matmul(ps[:, 4 + t % 2, h * DK:(h + 1) * DK], l_as[:, t % 2, h, :],
                                    l_g[:, t, 2 * P + h * DK:2 * P + (h + 1) * DK], start=False, stop=(h == NH - 1))
                ins.then_inc(l.o, 1)

            def turn(g):
                pe.wait_ge(l.oc, 4 * g + 4)
                if g >= 1:
                    pe.wait_ge(l.otc, g)
                for j in range(4):
                    ins = pe.transpose(ps[:, 6, j * P:(j + 1) * P], l_o[:, 4 * g + j, :], cc("ident"))
                ins.then_inc(l.ot, 1)

            def project(g):
                pe.wait_ge(l.otc, g + 1)
                if g >= 1:
                    pe.wait_ge(l.y, g)
                for j in range(4):
                    ins = pe.matmul(ps[:, 7, j * P:(j + 1) * P], l_ot[:, 4 * g + j, :], wc("lin_o"), start=True, stop=True)
                ins.then_inc(l.done, 1)

            for t in range(NT):
                scores(t)
                if t:
                    values(t - 1)
                if t >= 6 and t % 4 == 2:
                    turn(t // 4 - 1)
                if t >= 6 and t % 4 == 3:
                    project(t // 4 - 1)
            values(NT - 1)
            turn(3)
            project(3)

        def lin_scalar(act):
            for t in range(NT):
                act.wait_ge(l.g, t + 1)
                nc.scalar.activation(l_g[:, t, :], ps[:, t % 2, 0:NG], ACT.Copy).then_inc(l.g_in, 1)
            act.wait_ge(l.gate, 1)
            nc.scalar.activation(l_gate[:, :, :], l_gate[:, :, :], ACT.Sigmoid).then_inc(l.sig, 1)
            act.wait_ge(l.bet, 1)
            nc.scalar.activation(l_ln[:, :, :], l_ln[:, :, :], ACT.Ln).then_inc(l.ln, 1)
            act.wait_ge(l.cum, 1)
            cum = ps[:, 4, 0:P].rearrange("p (t h) -> p t h", h=NH)
            nc.scalar.activation(l_dq[:, :, :], cum, ACT.Exp).then_inc(l.dec, 1)
            nc.scalar.activation(l_dk[:, :, :], cum, ACT.Exp, scale=-1.0).then_inc(l.dec, 1)
            nc.scalar.activation(l_et[:, :], ps[:, 4, 256:256 + NT], ACT.Exp).then_inc(l.dec, 1)
            for g in range(4):
                act.wait_ge(l.qt, g + 1)
                for par in range(2):
                    nc.scalar.activation(l_qm[:, par, 512 * g:512 * (g + 1)], ps[:, 2 + g % 2, :], ACT.Copy,
                                         scale=cc("parity")[:, par:par + 1]).then_inc(l.qm, 1)

            def out(t):
                act.wait_ge(l.o, t + 1)
                nc.scalar.activation(l_o[:, t, :], ps[:, 4 + t % 2, 0:P], ACT.Copy).then_inc(l.oc, 1)

            def turned(g):
                act.wait_ge(l.ot, g + 1)
                nc.scalar.activation(l_ot[:, 4 * g:4 * g + 4, :].rearrange("p a b -> p (a b)"), ps[:, 6, :], ACT.Copy)\
                    .then_inc(l.otc, 1)

            for t in range(NT):
                out(t)
                if t >= 5 and t % 4 == 1:
                    turned(t // 4 - 1)
            turned(3)

        def lin_rope(eng, src, t4, b, after, each=False):
            pairs = src[:, TB * b:TB * (b + 1), :].rearrange("p t (h i two) -> p t h i two", h=NH, two=2)
            x1, x2 = pairs[:, :, :, :, 0], pairs[:, :, :, :, 1]
            sh = [P, TB, NH, DK // 2]
            cos = bc(cc("cos").rearrange("p (t i) -> p t i", t=TB).unsqueeze(2), sh)
            sin = bc(cc("sin").rearrange("p (t i) -> p t i", t=TB).unsqueeze(2), sh)
            tt = [t4[:, i, :].rearrange("p (t h i) -> p t h i", t=TB, h=NH) for i in range(4)]
            for out, a0, a1 in ((tt[0], x1, cos), (tt[1], x2, sin), (tt[2], x2, cos), (tt[3], x1, sin)):
                ins = eng.tensor_tensor(out, a0, a1, ALU.mult)
                if each:
                    after(ins)
            if not each:
                after(ins)
            return ((x1, tt[0], tt[1], ALU.subtract), (x2, tt[2], tt[3], ALU.add))

        def lin_vector(dve, vs):
            full = [P, NT, NH, DK]
            dve.wait_ge(l.g_in, NT)
            nc.vector.tensor_tensor(l_gate[:, :, :], l_g[:, :, 3 * P:NG], bc(rc("ab").unsqueeze(1), [P, NT, 2 * NH]),
                                    ALU.add).then_inc(l.gate, 1)
            dve.wait_ge(l.sig, 1)
            nc.vector.tensor_scalar(l_ln[:, :, :], l_gate[:, :, NH:2 * NH], BETA_MAX - BETA_MIN, BETA_MIN, ALU.mult,
                                    ALU.add).then_inc(l.bet, 1)
            dve.wait_ge(l.ln, 1)
            nc.vector.tensor_copy(l_lnx[:, :, :].rearrange("p t (h d) -> p t h d", h=NH),
                                  bc(l_ln[:, :, :].unsqueeze(3), full)).then_inc(l.lnx, 1)
            dve.wait_ge(l.dec, 2)
            nc.vector.tensor_tensor(l_dk[:, :, :], l_dk[:, :, :], l_gate[:, :, 0:NH], ALU.mult).then_inc(l.dk, 1)
            for b in range(B):
                ts = slice(TB * b, TB * (b + 1))
                vs.step(nc.vector.tensor_tensor(
                    l_q[:, ts, :].rearrange("p t (h d) -> p t h d", h=NH),
                    l_g[:, ts, 0:P].rearrange("p t (h d) -> p t h d", h=NH),
                    bc(l_dq[:, ts, :].unsqueeze(3), [P, TB, NH, DK]), ALU.mult))
                outs = lin_rope(nc.vector, l_q, l_tv, b, vs.step)
                for k, (dst, a0, a1, op) in enumerate(outs):
                    ins = nc.vector.tensor_tensor(dst, a0, a1, op)
                    if k:
                        ins.then_inc(l.q, 1)
                        dve.wait_ge(l.q, b + 1)
            for g in range(4):
                dve.wait_ge(l.kt, g + 1)
                nc.vector.tensor_copy(l_kt[:, 512 * g:512 * (g + 1)], ps[:, 6 + g % 2, :]).then_inc(l.ktc, 1)
                dve.wait_ge(l.kv, g + 1)
                if g == 0:
                    dve.wait_ge(l.dec, 3)
                te = l_te[:, 4 * g:4 * g + 4, :]
                nc.vector.tensor_tensor(te, ps[:, g % 2, :].rearrange("p (a b) -> p a b", a=4),
                                        bc(cc("blocks").unsqueeze(1), [P, 4, P]), ALU.mult).then_inc(l.te, 1)
                dve.wait_ge(l.te, g + 1)
                vs.step(nc.vector.tensor_tensor(te, te, bc(l_et[:, 4 * g:4 * g + 4].unsqueeze(2), [P, 4, P]), ALU.mult))
            for b in range(B):
                vs.step(nc.vector.memset(l_s[:, TB * b, :], 0.0))
            for i in range(TB - 1):
                for b in range(B):
                    t = TB * b + i
                    ins = nc.vector.scalar_tensor_tensor(out=l_s[:, t + 1, :], in0=l_s[:, t, :], scalar=l_et[:, t:t + 1],
                                                         in1=l_te[:, t, :], op0=ALU.mult, op1=ALU.add)
                    if i == TB - 2 and b == B - 1:
                        ins.then_inc(l.s, 1)
                    else:
                        vs.step(ins)
            for t in range(NT):
                dve.wait_ge(l.sc, t + 1)
                if t >= 2:
                    dve.wait_ge(l.o, t - 1)
                nc.vector.tensor_tensor(
                    l_as[:, t % 2, :, :].rearrange("p (i k) t -> p i k t", i=4),
                    ps[:, 0:4, 0:256].rearrange("p i (k t) -> p i k t", k=2),
                    bc(cc("causal").unsqueeze(1).unsqueeze(1), [P, 4, 2, P]), ALU.mult).then_inc(l.as_, 1)
                if t >= 8 and t % 4 == 0:
                    lin_vector_add(dve, t // 4 - 2)
            lin_vector_add(dve, 2)
            lin_vector_add(dve, 3)

        def lin_vector_add(dve, g):
            dve.wait_ge(l.done, g + 1)
            if g == 0:
                dve.wait_ge(l.bo, 2)
            xq = x[:, 4 * g:4 * g + 4, :]
            nc.vector.tensor_tensor(xq, xq, ps[:, 7, :].rearrange("p (a b) -> p a b", a=4), ALU.add).then_inc(l.y, 1)

        def lin_pool(pool, n):
            pool.wait_ge(n.xl_a, 2 * n.k + 2)
            pool.wait_ge(n.xl_v, 2 * n.k + 2)
            for b in range(B):
                xb = x[:, TB * b:TB * (b + 1), :]
                nc.gpsimd.tensor_tensor(xb, xb, bc(rc("bo").unsqueeze(1), [P, TB, P]), ALU.add).then_inc(l.bo, 1)
            pool.wait_ge(l.dk, 1)
            cnt = [0]

            def after(ins):
                ins.then_inc(l.kp, 1)
                cnt[0] += 1
                pool.wait_ge(l.kp, cnt[0])

            for b in range(B):
                ts = slice(TB * b, TB * (b + 1))
                after(nc.gpsimd.tensor_tensor(
                    l_k[:, ts, :].rearrange("p t (h d) -> p t h d", h=NH),
                    l_g[:, ts, P:2 * P].rearrange("p t (h d) -> p t h d", h=NH),
                    bc(l_dk[:, ts, :].unsqueeze(3), [P, TB, NH, DK]), ALU.mult))
                tt = lin_rope(nc.gpsimd, l_k, l_tp, b, after, True)
                for dst, a0, a1, op in tt:
                    after(nc.gpsimd.tensor_tensor(dst, a0, a1, op))

        n0, f0 = Norm(0), Ffn(0)
        n1 = Norm(1)
        n2, f2 = Norm(2), Ffn(2)
        n3, m3 = Norm(3), Mix(3)
        n4 = Norm(4)
        n5, m5 = Norm(5), Mix(5)

        block = ctx.enter_context(nc.Block())

        @block.sync
        def _(sp):
            for g in range(4):
                sp.dma_start(x[:, 4 * g:4 * g + 4, :],
                             A["x"].rearrange("(t p) d -> p t d", p=P)[:, 4 * g:4 * g + 4, :]).then_inc(s_x[g // 2], 16)
            sp.dma_start(w[:, :], A["wpack"]).then_inc(s_w, 16)
            sp.dma_start(cst[:, :], A["consts"]).then_inc(s_w, 16)
            sp.dma_start(row[:, :], A["rows"].to_broadcast([P, RTOTAL])).then_inc(s_w, 16)
            sp.dma_start(arena_f(20480, NH * P), A["wv"]).then_inc(s_wv, 16)
            sp.dma_start(w1[:, :, :], A["w1"].rearrange("e c f -> c e f")).then_inc(s_mix, 16)
            sp.dma_start(w2[:, :, :], A["w2"].rearrange("e c f -> c e f")).then_inc(s_mix, 16)
            sp.dma_start(b1[:, :], A["b1"]).then_inc(s_mix, 16)
            sp.dma_start(b2[:, :], A["b2"]).then_inc(s_mix, 16)
            sp.wait_ge(s_b1, 1)
            for i in range(3):
                sp.dma_start(b1row[i:i + 1, :].rearrange("i (e f) -> i e f", e=NE), b1p[:, i, :]).then_inc(s_b1row, 16)
            att_sync_stack(sp)
            att_sync_negmax_rows(sp)
            out_view = A["out"].rearrange("(t p) d -> p t d", p=P)
            for q in range(4):
                sp.wait_ge(m5.done, 17 * (q + 1))
                sp.dma_start(out_view[:, 4 * q:4 * q + 4, :], x[:, 4 * q:4 * q + 4, :]).then_inc(s_out, 16)
            sp.wait_ge(s_out, 64)

        @block.gpsimd
        def _(pool):
            nc.gpsimd.memset(ones3[:, :], 1.0).then_inc(s_set, 1)
            nc.gpsimd.memset(xt[:, :, 0:PAD], 0.0).then_inc(s_set, 1)
            pool.wait_ge(s_w, 48)
            nc.gpsimd.tensor_copy(identb[:, :], cc("ident")).then_inc(s_set, 1)
            pool.wait_ge(n1.stat, 3)
            att_pool_set(pool)
            mix_pool(pool, m3)
            lin_pool(pool, n4)
            mix_pool(pool, m5)

        @block.vector
        def _(dve):
            vs = Steps(dve, s_v)
            for half in range(2):
                dve.wait_ge(s_x[half], 32)
                norm_vector_stats(dve, vs, n0, half, False)
            dve.wait_ge(s_set, 3)
            dve.wait_ge(s_w, 48)
            for half in range(2):
                norm_vector_xt(dve, n0, half)
                ffn_vector_mix(dve, vs, n0, f0, half)
            dve.wait_ge(s_wv, 16)
            nc.vector.tensor_reduce(wvs[:, :], arena_f(20480, P, 8), AX.X, ALU.add).then_inc(s_wvs, 1)
            nc.vector.tensor_reduce(bvs[:, :], rc("bv").rearrange("p (a b) -> p a b", b=8), AX.X, ALU.add)\
                .then_inc(s_wvs, 1)
            ffn_vector_add(dve, vs, f0, 0)
            ffn_vector_add(dve, vs, f0, 1)
            for half in range(2):
                norm_vector_stats(dve, vs, n1, half, True)
            for half in range(2):
                norm_vector_xt(dve, n1, half, permuted=True, affine=True)
            dve.wait_ge(s_wvs, 2)
            att_vector_project(dve, 0)
            att_vector_project(dve, 1)
            dve.wait_ge(s_mix, 64)
            mw, mb = small[:, 20, 0:NE], small[0:NE, 21, 0:1]
            vs.step(nc.vector.tensor_reduce(mw, w1[:, :, :], AX.X, ALU.add))
            vs.step(nc.vector.tensor_scalar(mw, mw, 1.0 / P, None, ALU.mult))
            vs.step(nc.vector.tensor_tensor(w1[:, :, :], w1[:, :, :], bc(mw.unsqueeze(2), [P, NE, P]), ALU.subtract))
            vs.step(nc.vector.tensor_reduce(mb, b1[:, :], AX.X, ALU.add))
            vs.step(nc.vector.tensor_scalar(mb, mb, 1.0 / P, None, ALU.mult))
            vs.step(nc.vector.tensor_scalar(b1[:, :], b1[:, :], mb, None, ALU.subtract))
            vs.step(nc.vector.tensor_copy(b1p[:, 0, :], b1[:, :]))
            vs.step(nc.vector.tensor_tensor(b1r[:, :], b1[:, :], b1p[:, 0, :], ALU.subtract))
            vs.step(nc.vector.tensor_copy(b1p[:, 1, :], b1r[:, :]))
            nc.vector.tensor_tensor(b1p[:, 2, :], b1r[:, :], b1p[:, 1, :], ALU.subtract).then_inc(s_b1, 1)
            att_vector(dve, vs)
            for half in range(2):
                norm_vector_stats(dve, vs, n2, half, False)
            for half in range(2):
                norm_vector_xt(dve, n2, half)
                ffn_vector_mix(dve, vs, n2, f2, half)
            ffn_vector_add(dve, vs, f2, 0)
            ffn_vector_add(dve, vs, f2, 1)
            for half in range(2):
                norm_vector_stats(dve, vs, n3, half, False)
            for half in range(2):
                norm_vector_xt(dve, n3, half)
            mix_vector_route(dve, vs, m3)
            mix_vector(dve, vs, m3)
            for half in range(2):
                dve.wait_ge(m3.done, 34 * (half + 1))
                norm_vector_stats(dve, vs, n4, half, False)
            for half in range(2):
                norm_vector_xt(dve, n4, half)
            lin_vector(dve, vs)
            dve.wait_ge(l.y, 4)
            for half in range(2):
                norm_vector_stats(dve, vs, n5, half, False)
            for half in range(2):
                norm_vector_xt(dve, n5, half)
            mix_vector_route(dve, vs, m5)
            mix_vector(dve, vs, m5)

        @block.scalar
        def _(act):
            for half in range(2):
                norm_scalar_apply(act, n0, half)
            act.wait_ge(s_w, 48)
            for half in range(2):
                norm_scalar_xt(act, n0, half)
            for half in range(2):
                ffn_scalar(act, f0, half)
            for half in range(2):
                norm_scalar_apply(act, n1, half)
            for half in range(2):
                norm_scalar_xt(act, n1, half, permuted=True, affine=True)
            for half in range(2):
                att_scalar_project(act, half)
            att_scalar(act)
            for half in range(2):
                norm_scalar_apply(act, n2, half)
            for half in range(2):
                norm_scalar_xt(act, n2, half)
            for half in range(2):
                ffn_scalar(act, f2, half)
            for half in range(2):
                norm_scalar_apply(act, n3, half)
            for half in range(2):
                norm_scalar_xt(act, n3, half)
            mix_scalar_route(act, m3)
            mix_scalar(act, m3)
            for half in range(2):
                norm_scalar_apply(act, n4, half)
            for half in range(2):
                norm_scalar_xt(act, n4, half)
            lin_scalar(act)
            for half in range(2):
                norm_scalar_apply(act, n5, half)
            for half in range(2):
                norm_scalar_xt(act, n5, half)
            mix_scalar_route(act, m5)
            mix_scalar(act, m5)

        @block.tensor
        def _(pe):
            pe.wait_ge(s_w, 48)
            pe.wait_ge(s_set, 3)
            for half in range(2):
                norm_tensor(pe, n0, half)
            for half in range(2):
                ffn_tensor(pe, f0, half)
            for half in range(2):
                norm_tensor(pe, n1, half)
            for half in range(2):
                att_tensor_project(pe, n1, half)
            pe.wait_ge(a.onesk, 3)
            att_tensor(pe)
            for half in range(2):
                norm_tensor(pe, n2, half)
            for half in range(2):
                ffn_tensor(pe, f2, half)
            for half in range(2):
                norm_tensor(pe, n3, half)
            for half in range(2):
                mix_tensor_logits(pe, n3, m3, half)
            mix_tensor(pe, n3, m3)
            for half in range(2):
                norm_tensor(pe, n4, half)
            lin_tensor(pe, n4)
            for half in range(2):
                norm_tensor(pe, n5, half)
            for half in range(2):
                mix_tensor_logits(pe, n5, m5, half)
            mix_tensor(pe, n5, m5)


def shape_constants(np):
    c = np.zeros((P, CTOTAL), np.float32)

    def put(name, v):
        a, n = CCOLS[name]
        c[:, a:a + n] = v
    i = np.arange(P)
    put("ident", np.eye(P))
    put("causal", (i[:, None] <= i[None, :]))
    put("blocks", (i[:, None] // DK == i[None, :] // DK))
    half = DK // 2
    inv = (np.float32(1.0) / np.power(np.float32(10000.0), np.arange(half, dtype=np.float32) / np.float32(half)))
    ang = np.arange(S, dtype=np.float32)[:, None] * inv.astype(np.float32)[None, :]
    for name, f in (("cos", np.cos), ("sin", np.sin)):
        put(name, f(ang).astype(np.float32).reshape(TB, P, half).transpose(1, 0, 2).reshape(P, TB * half))
    put("rank", NE - np.arange(NE)[None, :])
    put("parity", (i[:, None] // DK) % 2 == np.arange(2)[None, :])
    put("ones", 1.0)
    return c


def kernel(**inputs):
    import numpy as _np
    import concourse.bacc as _bacc
    from concourse.bass_utils import run_bass_kernel_spmd as _run

    g = {k: _np.ascontiguousarray(v) for k, v in inputs.items()}
    col = lambda v: v.reshape(P, 1)
    rowv = lambda v: v.reshape(1, -1)
    wpack = _np.concatenate([
        g["L0_ffn_W_r"].T, g["L0_ffn_W_k"].T, g["L0_ffn_W_v"].T, g["L0_attn_Wq"], g["L0_attn_Wk"],
        g["L1_attn_Wq"].T, g["L1_attn_Wk"].T, g["L1_attn_Wv"].T, g["L1_attn_Walpha"].T, g["L1_attn_Wbeta"].T,
        g["L1_attn_Wo"].T, g["L1_ffn_Wr"], col(g["L0_ffn_mu_r"]), col(g["L0_ffn_mu_k"]), col(g["L0_attn_gamma"]),
        col(g["L0_attn_beta"]), col(g["L0_attn_bq"]), col(g["L0_attn_bk"]), g["L1_ffn_g1"].T, g["L1_ffn_be1"].T], axis=1)
    rows = _np.concatenate([rowv(g["L0_attn_bv"]), rowv(g["L1_attn_bo"]), rowv(g["L1_attn_balpha"]),
                            rowv(g["L1_attn_bbeta"]), rowv(g["L1_ffn_br"])], axis=1)
    arrays = {
        "x": g["L0_attn_x"].reshape(B * S, P), "wpack": _np.ascontiguousarray(wpack), "consts": shape_constants(_np),
        "rows": _np.ascontiguousarray(rows), "wv": g["L0_attn_Wv"], "w1": g["L1_ffn_W1"], "w2": g["L1_ffn_W2"],
        "b1": g["L1_ffn_b1"], "b2": g["L1_ffn_b2"]}
    nc = _bacc.Bacc("TRN2", target_bir_lowering=False, num_devices=1)
    A = {k: nc.dram_tensor(f"in_{k}", v.shape, F32, kind="ExternalInput").ap() for k, v in arrays.items()}
    A["out"] = nc.dram_tensor("out_x", (B * S, P), F32, kind="ExternalOutput").ap()
    build(nc, A)
    r = _run(nc, [{f"in_{k}": v for k, v in arrays.items()}], core_ids=[0])
    return r.results[0]["out_x"].reshape(B, S, P)
```

```python
from contextlib import ExitStack

import concourse.bass as bass
from concourse import mybir

F32 = mybir.dt.float32
BF16 = mybir.dt.bfloat16
I32 = mybir.dt.int32
ACT = mybir.ActivationFunctionType
ALU = mybir.AluOpType
AX = mybir.AxisListType

P = 128
B, S = 2, 1024
NT = B * S // P
TB = NT // B
NH, DK = 8, 16
NE = 16
EPS = 1e-5
BETA_MIN, BETA_MAX = 0.85, 0.999
RSQRT_SEED = float(0x5F3759DF)
PAD = 8

WCOLS = {}
_at = 0
for _name, _n in (("ffn_r", P), ("ffn_k", P), ("ffn_v", P), ("att_q", P), ("att_k", P),
                  ("lin_qkvab", 3 * P + 2 * NH), ("lin_o", P), ("router", NE), ("mu_r", 1), ("mu_k", 1),
                  ("gamma", 1), ("beta", 1), ("bq", 1), ("bk", 1), ("g1", NE), ("be1", NE)):
    WCOLS[_name] = (_at, _n)
    _at += _n
WTOTAL = _at
CCOLS = {}
_at = 0
for _name, _n in (("ident", P), ("causal", P), ("blocks", P), ("cos", TB * DK // 2), ("sin", TB * DK // 2),
                  ("rank", NE), ("quarter", 4), ("ones", 1), ("restart", 1)):
    CCOLS[_name] = (_at, _n)
    _at += _n
CTOTAL = _at
RCOLS = {}
_at = 0
for _name, _n in (("bv", NH * P), ("bo", P), ("ab", 2 * NH), ("br", NE)):
    RCOLS[_name] = (_at, _n)
    _at += _n
RTOTAL = _at


def build(nc, A):
    with ExitStack() as ctx:
        def sb(name, shape, dt=F32):
            return ctx.enter_context(nc.sbuf_tensor(name, shape, dt))

        def sem(name):
            return ctx.enter_context(nc.semaphore(name))

        x = sb("x", [P, NT, P])
        xl = sb("xl", [P, NT, P])
        xt = sb("xt", [P, B, PAD + S])
        w = sb("w", [P, WTOTAL])
        cst = sb("cst", [P, CTOTAL])
        row = sb("row", [P, RTOTAL])
        w1 = sb("w1", [P, NE, P])
        w2 = sb("w2", [P, NE, P])
        wvs = sb("wvs", [P, P])
        bvs = sb("bvs", [P, P])
        b1 = sb("b1", [NE, P])
        b1r = sb("b1r", [NE, P])
        b1p = sb("b1p", [NE, 3, P], BF16)
        b2 = sb("b2", [NE, P])
        b1row = sb("b1row", [3, NE * P], BF16)
        ones3 = sb("ones3", [3, P], BF16)
        identb = sb("identb", [P, P], BF16)
        zerob = sb("zerob", [P, 512], BF16)
        stat = sb("stat", [P, NT, 6])
        small = sb("small", [P, 24, 64])
        smalli = sb("smalli", [P, 2, 64], I32)
        arena = sb("arena", [P, 32 * 1024])
        ps = ctx.enter_context(nc.psum_tensor("ps", [P, 8, 512], F32))
        scratch = nc.dram_tensor("att_parts", [B, 2, NH, 3, DK, S], BF16, kind="Internal").ap()

        def wc(name):
            a, n = WCOLS[name]
            return w[:, a:a + n]

        def cc(name):
            a, n = CCOLS[name]
            return cst[:, a:a + n]

        def rc(name):
            a, n = RCOLS[name]
            return row[:, a:a + n]

        def arena_f(at, *shape):
            n = 1
            for d in shape:
                n *= d
            v = arena[:, at:at + n]
            names = "abcd"[:len(shape)]
            if len(shape) == 1:
                return v
            return v.rearrange("p (" + " ".join(names) + ") -> p " + " ".join(names),
                               **{k: d for k, d in zip(names, shape)})

        def arena_b(at, *shape):
            n = 1
            for d in shape:
                n *= d
            v = arena[:, at:at + n // 2].bitcast(BF16)
            names = "abcd"[:len(shape)]
            return v.rearrange("p (" + " ".join(names) + ") -> p " + " ".join(names),
                               **{k: d for k, d in zip(names, shape)})

        s_x = [sem(f"x_loaded{half}") for half in range(B)]
        s_w = sem("weights_loaded")
        s_mix = sem("expert_weights_loaded")
        s_out = sem("out_stored")
        s_v = sem("vector_steps")
        s_set = sem("constants_set")
        s_b1 = sem("b1_parts_ready")
        s_b1row = sem("b1_rows_loaded")
        s_wv = sem("wv_loaded")
        s_wvs = sem("summed_wv_ready")

        class Steps:

            def __init__(self, eng, s):
                self.eng, self.s, self.n = eng, s, 0

            def step(self, ins):
                ins.then_inc(self.s, 1)
                self.n += 1
                self.eng.wait_ge(self.s, self.n)

        def keep_clock(pe, bank, n):
            for _ in range(n):
                pe.matmul(ps[:, bank, :], zerob[:, 0:P], zerob[:, :], start=True, stop=True)

        def bc(ap, shape):
            return ap.to_broadcast(shape)

        class Norm:
            stat = sem("norm_stats")
            xl_v, xl_a = sem("norm_xl_by_vector"), sem("norm_xl_by_scalar")
            tp = sem("norm_turned")
            xt_v, xt_a = sem("norm_xt_by_vector"), sem("norm_xt_by_scalar")

            def __init__(self, first, stride=1):
                self.first, self.stride = first, stride

            def before(self, half):
                return self.first + self.stride * half

        rstd = small[:, 0, 0:NT]
        nmr = small[:, 1, 0:NT]
        mean = small[:, 2, 0:NT]

        def rsqrt(vs, out, v, n, at=12):
            y, t, hv = small[:, at, 0:n], small[:, at + 1, 0:n], small[:, at + 2, 0:n]
            vs.step(nc.vector.tensor_scalar(smalli[:, 0, 0:n], v.bitcast(I32), 1, None, ALU.logical_shift_right))
            vs.step(nc.vector.tensor_scalar(y.bitcast(I32), smalli[:, 0, 0:n], -1.0, RSQRT_SEED, ALU.mult, ALU.add))
            vs.step(nc.vector.tensor_scalar(hv, v, -0.5, None, ALU.mult))
            for it in range(3):
                vs.step(nc.vector.tensor_tensor(t, y, y, ALU.mult))
                vs.step(nc.vector.tensor_tensor(t, t, hv, ALU.mult))
                vs.step(nc.vector.scalar_tensor_tensor(out=out if it == 2 else y, in0=t, scalar=1.5, in1=y,
                                                       op0=ALU.add, op1=ALU.mult))

        def norm_vector_stats(dve, vs, n, half, double):
            lo, hi = TB * half, TB * (half + 1)
            for t in range(lo, hi):
                ins = nc.vector.bn_stats(stat[:, t, :], x[:, t, :])
            vs.step(ins)
            me, mo = stat[:, lo:hi, 1], stat[:, lo:hi, 4]
            ve, vo = stat[:, lo:hi, 2], stat[:, lo:hi, 5]
            d, d2, v, v4 = (small[:, i, 0:TB] for i in (4, 5, 6, 7))
            nc.vector.tensor_tensor(d, me, mo, ALU.subtract)
            nc.vector.tensor_tensor(v, ve, vo, ALU.add)
            vs.step(nc.vector.tensor_tensor(mean[:, lo:hi], me, mo, ALU.add))
            nc.vector.tensor_scalar(mean[:, lo:hi], mean[:, lo:hi], 0.5, None, ALU.mult)
            vs.step(nc.vector.tensor_tensor(d2, d, d, ALU.mult))
            vs.step(nc.vector.scalar_tensor_tensor(out=v4, in0=v, scalar=4.0 / P, in1=d2, op0=ALU.mult, op1=ALU.add))
            vs.step(nc.vector.tensor_scalar(v, v4, 0.25, EPS, ALU.mult, ALU.add))
            r = rstd[:, lo:hi]
            rsqrt(vs, r, v, TB)
            if double:
                u, r2 = small[:, 8, 0:TB], small[:, 9, 0:TB]
                vs.step(nc.vector.tensor_tensor(d2, r, r, ALU.mult))
                vs.step(nc.vector.scalar_tensor_tensor(out=u, in0=v4, scalar=0.25, in1=d2, op0=ALU.mult, op1=ALU.mult))
                vs.step(nc.vector.tensor_scalar(u, u, EPS, None, ALU.add))
                rsqrt(vs, r2, u, TB)
                vs.step(nc.vector.tensor_tensor(r, r, r2, ALU.mult))
            nc.vector.scalar_tensor_tensor(out=nmr[:, lo:hi], in0=mean[:, lo:hi], scalar=-1.0, in1=r,
                                           op0=ALU.mult, op1=ALU.mult).then_inc(n.stat, 1)
            for t in range(lo, hi, 2):
                ins = nc.vector.tensor_scalar(xl[:, t, :], x[:, t, :], mean[:, t:t + 1], rstd[:, t:t + 1],
                                              ALU.subtract, ALU.mult)
            ins.then_inc(n.xl_v, 1)

        def norm_scalar_apply(act, n, half):
            act.wait_ge(n.stat, n.before(half) + 1)
            for t in range(TB * half + 1, TB * (half + 1), 2):
                ins = nc.scalar.activation(xl[:, t, :], x[:, t, :], ACT.Identity, bias=nmr[:, t:t + 1],
                                           scale=rstd[:, t:t + 1])
            ins.then_inc(n.xl_a, 1)

        def norm_tensor(pe, n, half):
            pe.wait_ge(n.xl_v, n.before(half) + 1)
            pe.wait_ge(n.xl_a, n.before(half) + 1)
            for g in range(2):
                if n.before(half):
                    pe.wait_ge(n.xt_a if g == 0 else n.xt_v, n.before(half))
                for j in range(4):
                    ins = pe.transpose(ps[:, 6 + g, j * P:(j + 1) * P], xl[:, TB * half + 4 * g + j, :], cc("ident"))
                ins.then_inc(n.tp, 1)

        def xt_out(half, g, permuted):
            if permuted:
                v = xt[:, half, PAD:PAD + S].rearrange("c (j r) -> c j r", j=8)[:, :, 64 * g:64 * g + 64]
                return v
            return xt[:, half, PAD + 512 * g:PAD + 512 * (g + 1)]

        def norm_xt_in(g, permuted):
            if permuted:
                return ps[:, 6 + g, :].rearrange("c (r j) -> c j r", j=8)
            return ps[:, 6 + g, :]

        def norm_scalar_xt(act, n, half, permuted=False, affine=False):
            act.wait_ge(n.tp, 2 * n.before(half) + 1)
            if affine:
                ins = nc.scalar.activation(xt_out(half, 0, permuted), norm_xt_in(0, permuted), ACT.Identity,
                                           bias=wc("beta"), scale=wc("gamma"))
            else:
                ins = nc.scalar.activation(xt_out(half, 0, permuted), norm_xt_in(0, permuted), ACT.Copy)
            ins.then_inc(n.xt_a, 1)

        def norm_vector_xt(dve, n, half, permuted=False, affine=False):
            dve.wait_ge(n.tp, 2 * n.before(half) + 2)
            if affine:
                ins = nc.vector.tensor_scalar(xt_out(half, 1, permuted), norm_xt_in(1, permuted), wc("gamma"),
                                              wc("beta"), ALU.mult, ALU.add)
            else:
                ins = nc.vector.tensor_copy(xt_out(half, 1, permuted), norm_xt_in(1, permuted))
            ins.then_inc(n.xt_v, 1)

        class Ffn:
            def __init__(self, f):
                self.mixed = sem(f"f{f}_mixed")
                self.k, self.r, self.v = sem(f"f{f}_k"), sem(f"f{f}_r"), sem(f"f{f}_v")
                self.relu, self.ka = sem(f"f{f}_relu"), sem(f"f{f}_relu_squared")
                self.rs = sem(f"f{f}_sigmoid")
                self.done = sem(f"f{f}_gated")

        f_at = [[20480 + S * i for i in range(7)], [4096 + S * i for i in range(4)] + [12288 + S * i for i in range(3)]]
        f_xd, f_xr, f_xk = ([arena_f(f_at[b][i], S) for b in range(B)] for i in range(3))
        f_relu, f_ka, f_rs, f_t = ([arena_f(f_at[q // 2][i] + 512 * (q % 2), 512) for q in range(2 * B)]
                                   for i in range(3, 7))

        def ffn_vector_mix(dve, vs, n, f, half):
            dve.wait_ge(n.xt_a, n.before(half) + 1)
            dve.wait_ge(n.xt_v, n.before(half) + 1)
            cur, prev = xt[:, half, PAD:PAD + S], xt[:, half, PAD - 1:PAD - 1 + S]
            vs.step(nc.vector.tensor_tensor(f_xd[half], cur, prev, ALU.subtract))
            nc.vector.scalar_tensor_tensor(out=f_xk[half], in0=f_xd[half], scalar=wc("mu_k"), in1=prev,
                                           op0=ALU.mult, op1=ALU.add).then_inc(f.mixed, 1)
            nc.vector.scalar_tensor_tensor(out=f_xr[half], in0=f_xd[half], scalar=wc("mu_r"), in1=prev,
                                           op0=ALU.mult, op1=ALU.add).then_inc(f.mixed, 1)

        def ffn_tensor(pe, f, half, projected=False):
            if projected:
                pe.wait_ge(a.f32, 2)
                pe.wait_ge(a.v, 1)
            for q in (2 * half, 2 * half + 1):
                pe.wait_ge(f.mixed, 2 * half + 1)
                if half:
                    pe.wait_ge(f.relu, q - 1)
                at = 512 * (q % 2)
                pe.matmul(ps[:, q % 2, :], wc("ffn_k"), f_xk[half][:, at:at + 512], start=True, stop=True).then_inc(f.k, 1)
            for q in (2 * half, 2 * half + 1):
                pe.wait_ge(f.mixed, 2 * half + 2)
                if half:
                    pe.wait_ge(f.rs, q - 1)
                for j in range(4):
                    at = 512 * (q % 2) + j * P
                    ins = pe.matmul(ps[:, 2 + q % 2, j * P:(j + 1) * P], f_xr[half][:, at:at + P], wc("ffn_r"),
                                    start=True, stop=True)
                ins.then_inc(f.r, 1)
            for q in (2 * half, 2 * half + 1):
                pe.wait_ge(f.ka, q + 1)
                if half:
                    pe.wait_ge(f.done, q - 1)
                for j in range(4):
                    ins = pe.matmul(ps[:, 4 + q % 2, j * P:(j + 1) * P], f_ka[q][:, j * P:(j + 1) * P], wc("ffn_v"),
                                    start=True, stop=True)
                ins.then_inc(f.v, 1)

        def ffn_scalar(act, f, half):
            for q in (2 * half, 2 * half + 1):
                act.wait_ge(f.k, q + 1)
                nc.scalar.activation(f_relu[q], ps[:, q % 2, :], ACT.Relu).then_inc(f.relu, 1)
                act.wait_ge(f.relu, q + 1)
                nc.scalar.activation(f_ka[q], f_relu[q], ACT.Square).then_inc(f.ka, 1)
            for q in (2 * half, 2 * half + 1):
                act.wait_ge(f.r, q + 1)
                nc.scalar.activation(f_rs[q], ps[:, 2 + q % 2, :], ACT.Sigmoid).then_inc(f.rs, 1)

        def ffn_vector_add(dve, vs, f, half):
            for q in (2 * half, 2 * half + 1):
                dve.wait_ge(f.rs, q + 1)
                dve.wait_ge(f.v, q + 1)
                nc.vector.tensor_tensor(f_t[q], ps[:, 4 + q % 2, :], f_rs[q], ALU.mult).then_inc(f.done, 1)
                dve.wait_ge(f.done, q + 1)
                xq = x[:, 4 * q:4 * q + 4, :]
                vs.step(nc.vector.scalar_tensor_tensor(
                    out=xq, in0=f_t[q].rearrange("p (a b) -> p a b", a=4), scalar=0.5, in1=xq,
                    op0=ALU.mult, op1=ALU.add))

        NQ = 4
        a_qs = arena_b(0, B, NH, S)
        a_ks = arena_b(8192, B, NH, S)
        a_v = arena_f(16384, NT, NH, 32)
        a_p = arena_f(20480, 8, S)
        a_parts = arena_b(20480, B, 6, S)
        a_f = arena_f(20480 + 6144, S)
        a_r = arena_f(20480 + 7168, S)
        a_ot = arena_f(28672, S)
        a_tmp = arena_f(29696, 2, 4, P)
        a_nm = arena_f(30720, 2, 2, 8)
        a_nmr = arena_f(30752, 4, 8)
        a_nmb = arena_b(30784, 2, 24)
        a_nmt = arena_b(30832, 2, P)
        a_rd = arena_f(30960, 8, 4)

        class a:
            raw, f32 = sem("a_qk_product"), sem("a_qk_float")
            p1, r1, p2, p3 = sem("a_part1"), sem("a_rest1"), sem("a_part2"), sem("a_part3")
            vps, v = sem("a_values_product"), sem("a_values")
            stored = [sem(f"a_parts_stored{b}") for b in range(B)]
            stack = [sem(f"a_stack{i}") for i in range(4)]
            onesk = sem("a_ones_set")
            mp, mpu = sem("a_ring_filled"), sem("a_ring_taken")
            nm = sem("a_negmax_parts")
            nmrow = [sem(f"a_negmax_rows{i}") for i in range(B * NH)]
            st, ex, av = sem("a_scores"), sem("a_probs"), sem("a_values_summed")
            ot_a, ot_v = sem("a_out_by_scalar"), sem("a_out_by_vector")
            otp, done = sem("a_out_turned"), sem("a_out_normalised")

        HEADS = [(b, h) for b in range(B) for h in range(NH)]

        ring = []
        for hd in range(len(HEADS)):
            for u in range(16):
                ring.append(("mp", hd, u))
                if u == 2 and hd:
                    ring.append(("turn", hd - 1, 0))
        ring.append(("turn", len(HEADS) - 1, 0))
        turn_at = {hd: i for i, (k, hd, u) in enumerate(ring) if k == "turn"}
        ring_before = [turn_at[4 * q + 3] + 1 for q in range(4)] + [len(ring)]

        def ring_upto(quad, slot):
            lo, hi = ring_before[quad], ring_before[quad + 1]
            return min(hi, lo + (slot * (hi - lo) + 59) // 60)

        def att_tensor_project(pe, n, half):
            pe.wait_ge(n.xt_a, n.before(half) + 1)
            pe.wait_ge(n.xt_v, n.before(half) + 1)
            if half == 0:
                pe.wait_ge(s_wvs, 2)
            for i, name in enumerate(("att_q", "att_k")):
                if half:
                    pe.wait_ge(a.f32, i + 1)
                for g in range(2):
                    ins = pe.matmul(ps[:, 2 * i + g, :], wc(name), xt[:, half, PAD + 512 * g:PAD + 512 * (g + 1)],
                                    start=True, stop=True)
                ins.then_inc(a.raw, 1)
            if half:
                pe.wait_ge(a.v, 1)
            for t in range(TB):
                ins = pe.matmul(ps[:, 4 + t // 4, (t % 4) * P:(t % 4 + 1) * P],
                                xt[:, half, PAD + t * P:PAD + (t + 1) * P], wvs[:, :], start=True, stop=True)
            ins.then_inc(a.vps, 1)

        def att_scalar_project(act, half):
            for i in range(2):
                u = 2 * half + i
                act.wait_ge(a.raw, u + 1)
                if u:
                    act.wait_ge(a.r1, u)
                nc.scalar.activation(a_f[:, :].rearrange("p (a b) -> p a b", a=2), ps[:, 2 * i:2 * i + 2, :],
                                     ACT.Identity, bias=wc("bq" if i == 0 else "bk")).then_inc(a.f32, 1)
                act.wait_ge(a.f32, u + 1)
                nc.scalar.activation(a_parts[:, half, 3 * i, :], a_f[:, :], ACT.Copy).then_inc(a.p1, 1)
                act.wait_ge(a.r1, u + 1)
                nc.scalar.activation(a_parts[:, half, 3 * i + 1, :], a_r[:, :], ACT.Copy).then_inc(a.p2, 1)

        def att_vector_project(dve, half):
            for i in range(2):
                u = 2 * half + i
                dve.wait_ge(a.p1, u + 1)
                if u:
                    dve.wait_ge(a.p3, u)
                nc.vector.tensor_tensor(a_r[:, :], a_f[:, :], a_parts[:, half, 3 * i, :], ALU.subtract).then_inc(a.r1, 1)
                if i == 0:
                    dve.wait_ge(a.vps, half + 1)
                    nc.vector.tensor_tensor(
                        a_v[:, TB * half:TB * (half + 1), :, 0:DK],
                        ps[:, 4:6, :].rearrange("p a (b c d) -> p (a b) c d", b=4, c=NH),
                        bc(bvs[:, :].rearrange("p (c d) -> p c d", c=NH).unsqueeze(1), [P, TB, NH, DK]),
                        ALU.add).then_inc(a.v, 1)
                dve.wait_ge(a.r1, u + 1)
                dve.wait_ge(a.p2, u + 1)
                nc.vector.tensor_tensor(a_parts[:, half, 3 * i + 2, :], a_r[:, :], a_parts[:, half, 3 * i + 1, :],
                                        ALU.subtract).then_inc(a.p3, 1)

        def att_sync_stack(sp, b):
            for i in range(2):
                sp.wait_ge(a.p3, 2 * b + i + 1)
                for k in range(3):
                    sp.dma_start(scratch[b, i, :, k], a_parts[:, b, 3 * i + k, :]).then_inc(a.stored[b], 16)
            sp.wait_ge(a.stored[b], 96)
            for quad in range(2):
                hs = slice(NQ * quad, NQ * quad + NQ)
                for i, dst, runs in ((0, a_qs, ((0, 1), (0, 1), (0, 1), (1, 1), (1, 1), (2, 1))), (1, a_ks, ((0, 3), (0, 2), (0, 1)))):
                    at = 0
                    for part, n in runs:
                        sp.dma_start(dst[at:at + DK * n, b, hs, :],
                                     scratch[b, i, hs, part:part + n].rearrange("h k d s -> (k d) h s"))\
                            .then_inc(a.stack[2 * b + quad], 16)
                        at += DK * n

        def att_sync_negmax_rows(sp):
            for hd, (b, h) in enumerate(HEADS):
                sp.wait_ge(a.mpu, turn_at[hd] + 1)
                sp.dma_start(a_qs[96:99, b, h, :].rearrange("i (j s) -> i j s", j=8),
                             a_nmt[0:24, hd % 2, :]).then_inc(a.nmrow[hd], 16)

        def att_tensor(pe):
            class done:
                ring = 0

            def ring_units(upto):
                while done.ring < upto:
                    u = done.ring
                    kind, hd, k = ring[u]
                    b, h = HEADS[hd]
                    bank = 6 + u % 2
                    if kind == "mp":
                        if k == 0 and hd % 4 == 0:
                            pe.wait_ge(a.stack[hd // 4], 16 * 9)
                        if u >= 2:
                            pe.wait_ge(a.mpu, u - 1)
                        j, half = k // 2, k % 2
                        pe.matmul(ps[:, bank, :], a_qs[0:96, b, h, j * P:(j + 1) * P],
                                  a_ks[0:96, b, h, half * 512:(half + 1) * 512], start=True, stop=True).then_inc(a.mp, 1)
                    else:
                        pe.wait_ge(a.nm, hd + 1)
                        pe.wait_ge(a.mpu, u - 1)
                        pe.transpose(ps[0:24, bank, 0:64].bitcast(BF16), a_nmb[:, hd % 2, :], identb[:, :])\
                            .then_inc(a.mp, 1)
                    done.ring += 1

            def scores(v):
                step, h4 = v // 4, v % 4
                quad, i = step // 8, step % 8
                b, h = HEADS[4 * quad + h4]
                if i == 0:
                    pe.wait_ge(a.nmrow[4 * quad + h4], 16)
                if v >= 2:
                    pe.wait_ge(a.ex, v - 1)
                for half in range(2):
                    ins = pe.matmul(ps[:, 2 * (v % 2) + half, :], a_ks[0:99, b, h, i * P:(i + 1) * P],
                                    a_qs[0:99, b, h, half * 512:(half + 1) * 512], start=True, stop=True)
                ins.then_inc(a.st, 1)

            def values(step, half):
                quad, i = step // 8, step % 8
                b = HEADS[4 * quad][0]
                if i == 0 and quad:
                    pe.wait_ge(a.done, quad)
                pe.wait_ge(a.ex, 4 * step + 4)
                for h4 in range(4):
                    h = HEADS[4 * quad + h4][1]
                    ins = pe.matmul(ps[32 * h4:32 * h4 + 32, 4 + half, :], a_v[:, TB * b + i, h, :],
                                    a_p[:, (4 * step + h4) % 8, half * 512:(half + 1) * 512],
                                    start=(i == 0), stop=(i == 7))
                if half:
                    ins.then_inc(a.av, 1)

            def turn_out(quad):
                pe.wait_ge(a.ot_a, quad + 1)
                pe.wait_ge(a.ot_v, quad + 1)
                for j in range(8):
                    ins = pe.transpose(ps[:, 4 + j // 4, (j % 4) * P:(j % 4 + 1) * P], a_ot[:, j * P:(j + 1) * P],
                                       cc("ident"))
                ins.then_inc(a.otp, 1)

            pe.wait_ge(a.v, 2)
            ring_units(ring_before[0])
            for step in range(32):
                quad, i = step // 8, step % 8
                for h4 in range(4):
                    scores(4 * step + h4)
                    ring_units(ring_upto(quad, 8 * i + 2 * h4 + 1))
                    if h4 % 2 == 1 and step:
                        if i == 1 and quad and h4 == 1:
                            turn_out(quad - 1)
                        values(step - 1, h4 // 2)
                    ring_units(ring_upto(quad, 8 * i + 2 * h4 + 2))
            for half in range(2):
                values(31, half)
            turn_out(3)

        def att_vector(dve, vs, in_last_quad):
            class done:
                ring = 0

            def ring_units(upto):
                while done.ring < upto:
                    u = done.ring
                    kind, hd, k = ring[u]
                    dve.wait_ge(a.mp, u + 1)
                    if kind == "mp":
                        nc.vector.tensor_reduce(a_nm[:, hd % 2, k % 2, k // 2:k // 2 + 1], ps[:, 6 + u % 2, :], AX.X,
                                                ALU.max, negate=True).then_inc(a.mpu, 1)
                        if k == 15:
                            dve.wait_ge(a.mpu, u + 1)
                            nm, r1, r2 = a_nmr[:, 0, :], a_nmr[:, 1, :], a_nmr[:, 2, :]
                            parts = a_nmb[:, hd % 2, :].rearrange("p (i j) -> p i j", i=3)
                            vs.step(nc.vector.tensor_tensor(nm, a_nm[:, hd % 2, 0, :], a_nm[:, hd % 2, 1, :], ALU.min))
                            vs.step(nc.vector.tensor_copy(parts[:, 0, :], nm))
                            vs.step(nc.vector.tensor_tensor(r1, nm, parts[:, 0, :], ALU.subtract))
                            vs.step(nc.vector.tensor_copy(parts[:, 1, :], r1))
                            nc.vector.tensor_tensor(parts[:, 2, :], r1, parts[:, 1, :], ALU.subtract).then_inc(a.nm, 1)
                    else:
                        if hd >= 2:
                            dve.wait_ge(a.nmrow[hd - 2], 16)
                        nc.vector.tensor_copy(a_nmt[0:24, hd % 2, :], ps[0:24, 6 + u % 2, 0:64].bitcast(BF16))\
                            .then_inc(a.mpu, 1)
                    done.ring += 1

            def out_copy(quad):
                dve.wait_ge(a.av, 8 * (quad + 1))
                if quad:
                    dve.wait_ge(a.otp, quad)
                nc.vector.tensor_copy(a_ot[:, 512:1024], ps[:, 5, :]).then_inc(a.ot_v, 1)

            def out_add(quad):
                dve.wait_ge(a.otp, quad + 1)
                b, h0 = HEADS[4 * quad]
                o = ps[:, 4:6, :].rearrange("p a (j h e) -> p (a j) h e", j=4, h=4)
                vs.step(nc.vector.reciprocal(a_rd[:, :, :], o[:, :, :, DK]))
                for half in range(2):
                    dst = a_tmp[:, quad % 2, :, :].rearrange("p h (j g) -> p j h g", j=8)[:, 4 * half:4 * half + 4]
                    ins = nc.vector.tensor_tensor(
                        dst, o[:, 4 * half:4 * half + 4, :, 0:DK],
                        bc(a_rd[:, 4 * half:4 * half + 4, :].unsqueeze(3), [P, 4, 4, DK]), ALU.mult)
                ins.then_inc(a.done, 1)
                dve.wait_ge(a.done, quad + 1)
                xq = x[:, TB * b + h0:TB * b + h0 + 4, :]
                vs.step(nc.vector.tensor_tensor(xq, xq, a_tmp[:, quad % 2, :, :], ALU.add))

            ring_units(ring_before[0])
            for quad in range(4):
                if quad:
                    ring_units(ring_upto(quad, 8))
                    out_copy(quad - 1)
                    ring_units(ring_upto(quad, 11))
                    out_add(quad - 1)
                ring_units(ring_before[quad + 1])
            in_last_quad(dve, vs)
            out_copy(3)
            out_add(3)

        def att_scalar(act):
            for b in range(B):
                act.wait_ge(a.stored[b], 96)
            for v in range(128):
                step = v // 4
                if v % 32 == 4 and v > 4:
                    quad = v // 32 - 1
                    act.wait_ge(a.av, 8 * (quad + 1))
                    if quad:
                        act.wait_ge(a.otp, quad)
                    nc.scalar.activation(a_ot[:, 0:512], ps[:, 4, :], ACT.Copy).then_inc(a.ot_a, 1)
                if step >= 2:
                    act.wait_ge(a.av, step - 1)
                act.wait_ge(a.st, v + 1)
                nc.scalar.activation(a_p[:, v % 8, :].rearrange("p (a b) -> p a b", a=2),
                                     ps[:, 2 * (v % 2):2 * (v % 2) + 2, :], ACT.Exp, scale=0.25).then_inc(a.ex, 1)
            act.wait_ge(a.av, 32)
            act.wait_ge(a.otp, 3)
            nc.scalar.activation(a_ot[:, 0:512], ps[:, 4, :], ACT.Copy).then_inc(a.ot_a, 1)

        def att_pool_set(pool):
            nc.gpsimd.memset(a_ks[96:99, 0, :, :], 1.0).then_inc(a.onesk, 1)
            pool.wait_ge(a.onesk, 1)
            nc.gpsimd.memset(a_v[:, :, :, DK:32], 0.0).then_inc(a.onesk, 1)
            pool.wait_ge(a.onesk, 2)
            nc.gpsimd.memset(a_v[:, :, :, DK:DK + 1], 1.0).then_inc(a.onesk, 1)
            pool.wait_ge(a.onesk, 3)
            pool.wait_ge(n1.stat, n1.before(1) + 1)
            nc.gpsimd.memset(a_ks[96:99, 1, :, :], 1.0).then_inc(a.onesk, 1)

        class Mix:
            def __init__(self, m):
                self.logits, self.e = sem(f"m{m}_logits"), sem(f"m{m}_logit_gap")
                self.w, self.wt, self.wtc = sem(f"m{m}_weights"), sem(f"m{m}_weights_turned"), sem(f"m{m}_weights_by_expert")
                self.h, self.hc, self.hq, self.sqr = sem(f"m{m}_h"), sem(f"m{m}_h_copied"), sem(f"m{m}_h_squared"), sem(f"m{m}_h_sums")
                self.z, self.zt, self.ac = sem(f"m{m}_normed"), sem(f"m{m}_normed_turned"), sem(f"m{m}_gelu")
                self.y, self.tmp, self.done = sem(f"m{m}_y"), sem(f"m{m}_y_weighted"), sem(f"m{m}_x_added")

        m_s = arena_f(0, 10, NT, NE)
        m_wt = arena_f(2560, NT * P)
        m_h = arena_f(4608, 2, 4, 512)
        m_sq = arena_f(8704, 2, 512)
        m_z = arena_f(9728, 2, 4, 512)
        m_a = arena_f(13824, 4, 512)
        m_tmp = arena_f(15872, 4, 512)
        m_ss = arena_f(17920, 2, 16)
        m_rs = arena_f(17952, 2, 16)
        m_e = arena_f(17984, 4, NT)
        m_w = m_s[:, 9]
        NSU = 16

        def mix_tensor_logits(pe, n, m, half):
            pe.wait_ge(n.xt_a, n.before(half) + 1)
            pe.wait_ge(n.xt_v, n.before(half) + 1)
            for t in range(TB * half, TB * (half + 1)):
                at = PAD + (t % TB) * P
                ins = pe.matmul(ps[:, 4, t * NE:(t + 1) * NE], xt[:, half, at:at + P], wc("router"), start=True, stop=True)
            ins.then_inc(m.logits, 1)

        def mix_vector_route(dve, vs, m):
            lg, t, oh1, oh2, l2 = (m_s[:, i] for i in range(5))
            m1, m2, d, r = (m_e[:, i, :] for i in range(4))
            full = [P, NT, NE]
            dve.wait_ge(m.logits, 2)
            vs.step(nc.vector.tensor_tensor(lg, ps[:, 4, 0:NT * NE].rearrange("p (t e) -> p t e", e=NE),
                                            bc(rc("br").unsqueeze(1), full), ALU.add))
            rank = bc(cc("rank").unsqueeze(1), full)
            src = lg
            for mx, oh in ((m1, oh1), (m2, oh2)):
                vs.step(nc.vector.tensor_reduce(mx, src, AX.X, ALU.max))
                vs.step(nc.vector.tensor_tensor(t, src, bc(mx.unsqueeze(2), full), ALU.is_equal))
                vs.step(nc.vector.tensor_tensor(t, t, rank, ALU.mult))
                vs.step(nc.vector.tensor_reduce(r, t, AX.X, ALU.max))
                vs.step(nc.vector.tensor_tensor(oh, t, bc(r.unsqueeze(2), full), ALU.is_equal))
                if src is lg:
                    vs.step(nc.vector.scalar_tensor_tensor(out=l2, in0=oh, scalar=-3.0e38, in1=lg, op0=ALU.mult,
                                                           op1=ALU.add))
                src = l2
            nc.vector.tensor_tensor(d, m2, m1, ALU.subtract).then_inc(m.e, 1)
            dve.wait_ge(m.e, 2)
            vs.step(nc.vector.tensor_scalar(r, d, 1.0, 2.0, ALU.add, ALU.mult))
            vs.step(nc.vector.reciprocal(m1, r))
            vs.step(nc.vector.tensor_tensor(m2, d, m1, ALU.mult))
            nc.vector.tensor_tensor(oh1, oh1, bc(m1.unsqueeze(2), full), ALU.mult)
            vs.step(nc.vector.tensor_tensor(oh2, oh2, bc(m2.unsqueeze(2), full), ALU.mult))
            nc.vector.tensor_tensor(m_w, oh1, oh2, ALU.add).then_inc(m.w, 1)

        def mix_scalar_route(act, m):
            act.wait_ge(m.e, 1)
            nc.scalar.activation(m_e[:, 2, :], m_e[:, 2, :], ACT.Exp).then_inc(m.e, 1)

        def mix_tensor(pe, n, m):
            def hidden(s, j):
                u = 4 * s + j
                q, eq = s // 4, s % 4
                half, at = q // 2, PAD + 512 * (q % 2) + j * P
                if u == 0:
                    pe.wait_ge(s_b1row, 48)
                    pe.wait_ge(s_set, 4)
                if u >= 2:
                    pe.wait_ge(m.hq, u - 1)
                pe.matmul(ps[:, u % 2, :], ones3[:, :], b1row[:, 512 * eq:512 * (eq + 1)], start=True, stop=False)
                pe.matmul(ps[:, u % 2, :], xt[:, half, at:at + P],
                          w1[:, 4 * eq:4 * eq + 4, :].rearrange("c e f -> c (e f)"), start=False, stop=True)\
                    .then_inc(m.h, 1)

            def turn(s, e):
                u = 4 * s + e
                pe.wait_ge(m.z, 4 * s + 4)
                if u >= 2:
                    pe.wait_ge(m.ac, u - 1)
                for j in range(4):
                    ins = pe.transpose(ps[:, 2 + u % 2, j * P:(j + 1) * P], m_z[:, s % 2, j, e * P:(e + 1) * P], cc("ident"))
                ins.then_inc(m.zt, 1)

            def out(s, e):
                u = 4 * s + e
                v = u + s // 4
                pe.wait_ge(m.ac, u + 1)
                if v >= 2:
                    pe.wait_ge(m.tmp, v - 1)
                if v < 2:
                    pe.wait_ge(m.w, 1)
                for j in range(4):
                    ins = pe.matmul(ps[:, 4 + v % 2, j * P:(j + 1) * P], m_a[:, u % 4, j * P:(j + 1) * P],
                                    w2[:, 4 * (s % 4) + e, :], start=True, stop=True)
                ins.then_inc(m.y, 1)

            def out_bias(q):
                v = 17 * q + 16
                if q == 0:
                    pe.wait_ge(m.wtc, 1)
                pe.wait_ge(m.tmp, v - 1)
                for j in range(4):
                    ins = pe.matmul(ps[:, 4 + v % 2, j * P:(j + 1) * P],
                                    m_wt[0:NE, (4 * q + j) * P:(4 * q + j + 1) * P], b2[:, :], start=True, stop=True)
                ins.then_inc(m.y, 1)

            def turn_weights():
                pe.wait_ge(m.w, 1)
                for g in range(2):
                    for k in range(8):
                        t = 8 * g + k
                        if k == 4 or (g and k == 0):
                            pass
                        ins = pe.transpose(ps[0:NE, 6 + (k // 4), (k % 4) * P:(k % 4 + 1) * P],
                                           m_w[:, t, :], cc("ident"))
                    ins.then_inc(m.wt, 1)
                    if g == 0:
                        pe.wait_ge(m.wtc, 1)

            for j in range(4):
                hidden(0, j)
            for j in range(4):
                hidden(1, j)
            turn_weights()
            for s in range(NSU):
                for e in range(4):
                    if s + 2 < NSU:
                        hidden(s + 2, e)
                    turn(s, e)
                    if e:
                        out(s, e - 1)
                out(s, 3)
                if s % 4 == 3:
                    out_bias(s // 4)

        def mix_scalar(act, m):
            def hidden(s, j):
                u = 4 * s + j
                if s >= 2 and j == 0:
                    act.wait_ge(m.z, 4 * (s - 2) + 4)
                act.wait_ge(m.h, u + 1)
                nc.scalar.activation(m_h[:, s % 2, j, :], ps[:, u % 2, :], ACT.Copy).then_inc(m.hc, 1)
                if u >= 2:
                    act.wait_ge(m.sqr, u - 1)
                nc.scalar.activation(m_sq[:, u % 2, :], ps[:, u % 2, :], ACT.Square).then_inc(m.hq, 1)

            for s in range(2):
                for j in range(4):
                    hidden(s, j)
            for g in range(2):
                act.wait_ge(m.wt, g + 1)
                nc.scalar.activation(m_wt[0:NE, 1024 * g:1024 * (g + 1)].rearrange("p (a b) -> p a b", a=2),
                                     ps[0:NE, 6:8, :], ACT.Copy).then_inc(m.wtc, 1)
            for s in range(NSU):
                for e in range(4):
                    if s + 2 < NSU:
                        hidden(s + 2, e)
                    u = 4 * s + e
                    ex = 4 * (s % 4) + e
                    act.wait_ge(m.zt, u + 1)
                    if u >= 4:
                        act.wait_ge(m.y, u - 4 + (u - 4) // 16 + 1)
                    nc.scalar.activation(m_a[:, u % 4, :], ps[:, 2 + u % 2, :], ACT.Gelu,
                                         bias=wc("be1")[:, ex:ex + 1], scale=wc("g1")[:, ex:ex + 1]).then_inc(m.ac, 1)

        def mix_vector(dve, vs, m):
            def squares(s, j):
                u = 4 * s + j
                dve.wait_ge(m.hq, u + 1)
                nc.vector.tensor_reduce(m_ss[:, s % 2, 4 * j:4 * j + 4],
                                        m_sq[:, u % 2, :].rearrange("p (e f) -> p e f", e=4), AX.X, ALU.add)\
                    .then_inc(m.sqr, 1)

            def rstds(s):
                dve.wait_ge(m.sqr, 4 * s + 4)
                v = m_ss[:, s % 2, :]
                vs.step(nc.vector.tensor_scalar(v, v, 1.0 / P, EPS, ALU.mult, ALU.add))
                rsqrt(vs, m_rs[:, s % 2, :], v, 16)

            def scaled(s, j):
                dve.wait_ge(m.hc, 4 * s + 4)
                if s >= 2 and j == 0:
                    dve.wait_ge(m.zt, 4 * (s - 2) + 4)
                nc.vector.tensor_tensor(
                    m_z[:, s % 2, j, :].rearrange("p (e f) -> p e f", e=4),
                    m_h[:, s % 2, j, :].rearrange("p (e f) -> p e f", e=4),
                    bc(m_rs[:, s % 2, 4 * j:4 * j + 4].unsqueeze(2), [P, 4, P]), ALU.mult).then_inc(m.z, 1)

            def weighted(v):
                q, k = v // 17, v % 17
                dve.wait_ge(m.y, v + 1)
                if v >= 4:
                    dve.wait_ge(m.done, v - 3)
                y = ps[:, 4 + v % 2, :].rearrange("p (j o) -> p j o", j=4)
                dst = m_tmp[:, v % 4, :].rearrange("p (j o) -> p j o", j=4)
                if k < 16:
                    wgt = m_w[:, 4 * q:4 * q + 4, k:k + 1]
                    nc.vector.tensor_tensor(dst, y, bc(wgt, [P, 4, P]), ALU.mult).then_inc(m.tmp, 1)
                else:
                    nc.vector.tensor_copy(dst, y).then_inc(m.tmp, 1)

            for j in range(4):
                squares(0, j)
            rstds(0)
            for j in range(4):
                squares(1, j)
            for j in range(4):
                scaled(0, j)
            rstds(1)
            for s in range(NSU):
                v0 = 4 * s + s // 4
                for j in range(4):
                    if s + 2 < NSU:
                        squares(s + 2, j)
                    if s + 1 < NSU:
                        scaled(s + 1, j)
                    if j:
                        weighted(v0 + j - 1)
                weighted(v0 + 3)
                if s % 4 == 3:
                    weighted(v0 + 4)
                if s + 2 < NSU:
                    rstds(s + 2)

        def mix_pool(pool, m, stored=None):
            for v in range(68):
                q = v // 17
                pool.wait_ge(m.tmp, v + 1)
                if v:
                    pool.wait_ge(m.done, v)
                xq = x[:, 4 * q:4 * q + 4, :]
                nc.gpsimd.tensor_tensor(xq, xq, m_tmp[:, v % 4, :].rearrange("p (j o) -> p j o", j=4), ALU.add)\
                    .then_inc(m.done, 1)

        NG = 3 * P + 2 * NH
        l_g = arena_f(0, NT, NG)
        l_q = arena_f(6400, NT, P)
        l_k = arena_f(8448, NT, P)
        l_tv = arena_f(10496, 4, 512)
        l_tp = arena_f(12544, 4, 512)
        l_gate = arena_f(14592, NT, 2 * NH)
        l_ln = arena_f(14848, NT, NH)
        l_dq = arena_f(14976, NT, NH)
        l_dk = arena_f(15104, NT, NH)
        l_lnx = arena_f(15616, NT, P)
        l_ot = arena_f(15616, NT, P)
        l_qm = arena_f(17664, 4, NT * P)
        l_kt = arena_f(8448, NT * P)
        l_as = arena_f(10496, 2, NH, P)
        l_te = arena_f(25856, NT, P)
        l_et = arena_f(27904, NT)
        l_vp = arena_f(28032, NT, NH, 2 * DK)
        l_qt = arena_f(6400, NT * P)
        l_s = xl

        class l:
            g, g_in = sem("l_products"), sem("l_products_in")
            gate, sig, bet, ln, lnx = sem("l_gates"), sem("l_sigmoids"), sem("l_beta"), sem("l_ln_beta"), sem("l_ln_beta_wide")
            cum, dec, dk = sem("l_sums"), sem("l_decays"), sem("l_key_decay")
            q, kp = sem("l_q"), sem("l_k_steps")
            qt, qm, kt, ktc = sem("l_q_turned"), sem("l_q_in"), sem("l_k_turned"), sem("l_k_in")
            kv, te, s = sem("l_kv"), sem("l_kv_in"), sem("l_states")
            sc, as_ = sem("l_scores"), sem("l_scores_masked")
            vp, o, oc = sem("l_values_spread"), sem("l_out"), sem("l_out_in")
            done, y, bo = sem("l_projected"), sem("l_x_added"), sem("l_bias_added")

        def lin_tensor(pe, n):
            for t in range(NT):
                half = t // TB
                if t % TB == 0:
                    pe.wait_ge(n.xt_a, n.before(half) + 1)
                    pe.wait_ge(n.xt_v, n.before(half) + 1)
                if t >= 2:
                    pe.wait_ge(l.g_in, t - 1)
                at = PAD + (t % TB) * P
                pe.matmul(ps[:, t % 2, 0:NG], xt[:, half, at:at + P], wc("lin_qkvab"), start=True, stop=True).then_inc(l.g, 1)
            pe.wait_ge(l.lnx, 1)
            pe.matmul(ps[:, 4, 0:P], cc("causal"), l_ln.rearrange("p t h -> p (t h)"), start=True, stop=True)
            for t in range(NT):
                ins = pe.matmul(ps[:, 4, 256 + t:257 + t], l_lnx[:, t, :], cc("ones"), start=True, stop=True)
            ins.then_inc(l.cum, 1)
            pe.wait_ge(l.q, 2)
            for g in range(4):
                if g >= 2:
                    pe.wait_ge(l.qm, 5 * (g - 1))
                for j in range(4):
                    ins = pe.transpose(ps[:, 2 + g % 2, j * P:(j + 1) * P], l_q[:, 4 * g + j, :], cc("ident"))
                ins.then_inc(l.qt, 1)
            pe.wait_ge(l.kp, 14)
            for g in range(4):
                if g >= 2:
                    pe.wait_ge(l.ktc, g - 1)
                for j in range(4):
                    ins = pe.transpose(ps[:, 6 + g % 2, j * P:(j + 1) * P], l_k[:, 4 * g + j, :], cc("ident"))
                ins.then_inc(l.kt, 1)
                if g == 0:
                    pe.wait_ge(l.g_in, NT)
                if g >= 2:
                    pe.wait_ge(l.te, g - 1)
                for j in range(4):
                    t = 4 * g + j
                    ins = pe.matmul(ps[:, g % 2, j * P:(j + 1) * P], l_k[:, t, :], l_g[:, t, 2 * P:3 * P], start=True, stop=True)
                ins.then_inc(l.kv, 1)
            pe.wait_ge(l.qm, 20)
            pe.wait_ge(l.ktc, 4)
            keep_clock(pe, 5, 40)
            pe.wait_ge(l.te, 4)
            pe.wait_ge(l.vp, 3)

            def scores(t, k):
                if t >= 2:
                    pe.wait_ge(l.as_, 2 * (t - 2) + k + 1)
                r = slice(64 * k, 64 * k + 64)
                pe.matmul(ps[:, 2 * (t % 2) + k, :], l_kt[r, t * P:(t + 1) * P], l_qm[r, :, t * P:(t + 1) * P],
                          start=True, stop=True).then_inc(l.sc, 1)

            def values(t):
                g, at = t // 4, (t % 4) * P
                if t % 4 == 0 and g >= 2:
                    pe.wait_ge(l.oc, g - 1)
                if t == 0:
                    pe.wait_ge(l.s, 1)
                pe.matmul(ps[:, 4 + g % 2, at:at + P], l_s[:, t, :], l_qt[:, t * P:(t + 1) * P], start=True, stop=False)
                pe.wait_ge(l.as_, 2 * t + 2)
                for par in range(2):
                    for i in range(4):
                        ins = pe.matmul(ps[32 * i:32 * i + 32, 4 + g % 2, at:at + P], l_vp[:, t, 2 * i + par, :],
                                        l_as[:, t % 2, 2 * i + par, :], start=False, stop=(par == 1))
                ins.then_inc(l.o, 1)

            def project(g):
                pe.wait_ge(l.oc, g + 1)
                if g >= 2:
                    pe.wait_ge(l.y, g - 1)
                for j in range(4):
                    ins = pe.matmul(ps[:, 6 + g % 2, j * P:(j + 1) * P], l_ot[:, 4 * g + j, :], wc("lin_o"),
                                    start=True, stop=True)
                ins.then_inc(l.done, 1)

            for t in range(NT):
                scores(t, 0)
                scores(t, 1)
                if t:
                    values(t - 1)
                if t >= 6 and t % 4 == 2:
                    project(t // 4 - 1)
            values(NT - 1)
            project(3)

        def lin_scalar(act):
            for t in range(NT):
                act.wait_ge(l.g, t + 1)
                nc.scalar.activation(l_g[:, t, :], ps[:, t % 2, 0:NG], ACT.Copy).then_inc(l.g_in, 1)
            act.wait_ge(l.g_in, NT)
            act.wait_ge(l.vp, 1)
            for par in range(2):
                nc.scalar.activation(
                    l_vp.rearrange("p t (i two) d -> p t i two d", two=2)[:, :, :, par, DK * par:DK * par + DK],
                    l_g[:, :, 2 * P:3 * P].rearrange("p t (i two d) -> p t i two d", two=2, d=DK)[:, :, :, par, :],
                    ACT.Copy).then_inc(l.vp, 1)
            act.wait_ge(l.gate, 1)
            nc.scalar.activation(l_gate[:, :, :], l_gate[:, :, :], ACT.Sigmoid).then_inc(l.sig, 1)
            act.wait_ge(l.bet, 1)
            nc.scalar.activation(l_ln[:, :, :], l_ln[:, :, :], ACT.Ln).then_inc(l.ln, 1)
            act.wait_ge(l.cum, 1)
            cum = ps[:, 4, 0:P].rearrange("p (t h) -> p t h", h=NH)
            nc.scalar.activation(l_dq[:, :, :], cum, ACT.Exp).then_inc(l.dec, 1)
            nc.scalar.activation(l_dk[:, :, :], cum, ACT.Exp, scale=-1.0).then_inc(l.dec, 1)
            nc.scalar.activation(l_et[:, :], ps[:, 4, 256:256 + NT], ACT.Exp).then_inc(l.dec, 1)
            for g in range(4):
                act.wait_ge(l.qt, g + 1)
                for m in range(4):
                    nc.scalar.activation(l_qm[:, m, 512 * g:512 * (g + 1)], ps[:, 2 + g % 2, :], ACT.Copy,
                                         scale=cc("quarter")[:, m:m + 1]).then_inc(l.qm, 1)
                nc.scalar.activation(l_qt[:, 512 * g:512 * (g + 1)], ps[:, 2 + g % 2, :], ACT.Copy).then_inc(l.qm, 1)

            for g in range(4):
                act.wait_ge(l.o, 4 * g + 4)
                nc.scalar.activation(l_ot[:, 4 * g:4 * g + 4, :].rearrange("p a b -> p (a b)"), ps[:, 4 + g % 2, :],
                                     ACT.Copy).then_inc(l.oc, 1)

        def lin_rope(eng, src, t4, b, after, each=False):
            pairs = src[:, TB * b:TB * (b + 1), :].rearrange("p t (h i two) -> p t h i two", h=NH, two=2)
            x1, x2 = pairs[:, :, :, :, 0], pairs[:, :, :, :, 1]
            sh = [P, TB, NH, DK // 2]
            cos = bc(cc("cos").rearrange("p (t i) -> p t i", t=TB).unsqueeze(2), sh)
            sin = bc(cc("sin").rearrange("p (t i) -> p t i", t=TB).unsqueeze(2), sh)
            tt = [t4[:, i, :].rearrange("p (t h i) -> p t h i", t=TB, h=NH) for i in range(4)]
            for out, a0, a1 in ((tt[0], x1, cos), (tt[1], x2, sin), (tt[2], x2, cos), (tt[3], x1, sin)):
                ins = eng.tensor_tensor(out, a0, a1, ALU.mult)
                if each:
                    after(ins)
            if not each:
                after(ins)
            return ((x1, tt[0], tt[1], ALU.subtract), (x2, tt[2], tt[3], ALU.add))

        def lin_vector(dve, vs):
            full = [P, NT, NH, DK]
            dve.wait_ge(l.g_in, NT)
            nc.vector.tensor_tensor(l_gate[:, :, :], l_g[:, :, 3 * P:NG], bc(rc("ab").unsqueeze(1), [P, NT, 2 * NH]),
                                    ALU.add).then_inc(l.gate, 1)
            dve.wait_ge(l.sig, 1)
            nc.vector.tensor_scalar(l_ln[:, :, :], l_gate[:, :, NH:2 * NH], BETA_MAX - BETA_MIN, BETA_MIN, ALU.mult,
                                    ALU.add).then_inc(l.bet, 1)
            dve.wait_ge(l.ln, 1)
            nc.vector.tensor_copy(l_lnx[:, :, :].rearrange("p t (h d) -> p t h d", h=NH),
                                  bc(l_ln[:, :, :].unsqueeze(3), full)).then_inc(l.lnx, 1)
            dve.wait_ge(l.dec, 2)
            nc.vector.tensor_tensor(l_dk[:, :, :], l_dk[:, :, :], l_gate[:, :, 0:NH], ALU.mult).then_inc(l.dk, 1)
            for b in range(B):
                ts = slice(TB * b, TB * (b + 1))
                vs.step(nc.vector.tensor_tensor(
                    l_q[:, ts, :].rearrange("p t (h d) -> p t h d", h=NH),
                    l_g[:, ts, 0:P].rearrange("p t (h d) -> p t h d", h=NH),
                    bc(l_dq[:, ts, :].unsqueeze(3), [P, TB, NH, DK]), ALU.mult))
                outs = lin_rope(nc.vector, l_q, l_tv, b, vs.step)
                for k, (dst, a0, a1, op) in enumerate(outs):
                    ins = nc.vector.tensor_tensor(dst, a0, a1, op)
                    if k:
                        ins.then_inc(l.q, 1)
                        dve.wait_ge(l.q, b + 1)
            for g in range(4):
                dve.wait_ge(l.kt, g + 1)
                dve.wait_ge(l.kv, g + 1)
                nc.vector.tensor_copy(l_kt[:, 512 * g:512 * (g + 1)], ps[:, 6 + g % 2, :]).then_inc(l.ktc, 1)
                if g == 0:
                    dve.wait_ge(l.dec, 3)
                te = l_te[:, 4 * g:4 * g + 4, :]
                nc.vector.tensor_tensor(te, ps[:, g % 2, :].rearrange("p (a b) -> p a b", a=4),
                                        bc(cc("blocks").unsqueeze(1), [P, 4, P]), ALU.mult).then_inc(l.te, 1)
                dve.wait_ge(l.te, g + 1)
                vs.step(nc.vector.tensor_tensor(te, te, bc(l_et[:, 4 * g:4 * g + 4].unsqueeze(2), [P, 4, P]), ALU.mult))
            for b in range(B):
                vs.step(nc.vector.memset(l_s[:, TB * b, :], 0.0))
            for i in range(TB - 1):
                for b in range(B):
                    t = TB * b + i
                    ins = nc.vector.scalar_tensor_tensor(out=l_s[:, t + 1, :], in0=l_s[:, t, :], scalar=l_et[:, t:t + 1],
                                                         in1=l_te[:, t, :], op0=ALU.mult, op1=ALU.add)
                    if i == TB - 2 and b == B - 1:
                        ins.then_inc(l.s, 1)
                    else:
                        vs.step(ins)
            for t in range(NT):
                for k in range(2):
                    dve.wait_ge(l.sc, 2 * t + k + 1)
                    if t >= 2:
                        dve.wait_ge(l.o, t - 1)
                    nc.vector.tensor_tensor(
                        l_as[:, t % 2, 4 * k:4 * k + 4, :], ps[:, 2 * (t % 2) + k, :].rearrange("p (m t) -> p m t", m=4),
                        bc(cc("causal").unsqueeze(1), [P, 4, P]), ALU.mult).then_inc(l.as_, 1)
                if t >= 8 and t % 4 == 0:
                    lin_vector_add(dve, t // 4 - 2)
            lin_vector_add(dve, 2)
            lin_vector_add(dve, 3)

        def lin_vector_add(dve, g):
            dve.wait_ge(l.done, g + 1)
            if g == 0:
                dve.wait_ge(l.bo, 2)
            xq = x[:, 4 * g:4 * g + 4, :]
            nc.vector.tensor_tensor(xq, xq, ps[:, 6 + g % 2, :].rearrange("p (a b) -> p a b", a=4), ALU.add).then_inc(l.y, 1)

        def lin_pool(pool, n):
            pool.wait_ge(n.xl_a, n.before(1) + 1)
            pool.wait_ge(n.xl_v, n.before(1) + 1)
            for b in range(B):
                xb = x[:, TB * b:TB * (b + 1), :]
                nc.gpsimd.tensor_tensor(xb, xb, bc(rc("bo").unsqueeze(1), [P, TB, P]), ALU.add).then_inc(l.bo, 1)
            pool.wait_ge(l.dk, 1)
            cnt = [0]

            def after(ins):
                ins.then_inc(l.kp, 1)
                cnt[0] += 1
                pool.wait_ge(l.kp, cnt[0])

            for b in range(B):
                ts = slice(TB * b, TB * (b + 1))
                after(nc.gpsimd.tensor_tensor(
                    l_k[:, ts, :].rearrange("p t (h d) -> p t h d", h=NH),
                    l_g[:, ts, P:2 * P].rearrange("p t (h d) -> p t h d", h=NH),
                    bc(l_dk[:, ts, :].unsqueeze(3), [P, TB, NH, DK]), ALU.mult))
                tt = lin_rope(nc.gpsimd, l_k, l_tp, b, after, True)
                for dst, a0, a1, op in tt:
                    after(nc.gpsimd.tensor_tensor(dst, a0, a1, op))

        n0, f0 = Norm(0, 2), Ffn(0)
        n1 = Norm(1, 2)
        n2, f2 = Norm(4), Ffn(2)
        n3, m3 = Norm(6), Mix(3)
        n4 = Norm(8)
        n5, m5 = Norm(10), Mix(5)

        block = ctx.enter_context(nc.Block())

        @block.sync
        def _(sp):
            for g in range(4):
                sp.dma_start(x[:, 4 * g:4 * g + 4, :],
                             A["x"].rearrange("(t p) d -> p t d", p=P)[:, 4 * g:4 * g + 4, :]).then_inc(s_x[g // 2], 16)
            sp.dma_start(w[:, :], A["wpack"]).then_inc(s_w, 16)
            sp.dma_start(cst[:, :], A["consts"]).then_inc(s_w, 16)
            sp.dma_start(row[:, :], A["rows"].to_broadcast([P, RTOTAL])).then_inc(s_w, 16)
            sp.dma_start(arena_f(28672, NH * P), A["wv"]).then_inc(s_wv, 16)
            sp.dma_start(w1[:, :, :], A["w1"].rearrange("e c f -> c e f")).then_inc(s_mix, 16)
            sp.dma_start(w2[:, :, :], A["w2"].rearrange("e c f -> c e f")).then_inc(s_mix, 16)
            sp.dma_start(b1[:, :], A["b1"]).then_inc(s_mix, 16)
            sp.dma_start(b2[:, :], A["b2"]).then_inc(s_mix, 16)
            for b in range(B):
                att_sync_stack(sp, b)
            att_sync_negmax_rows(sp)
            sp.wait_ge(s_b1, 1)
            for i in range(3):
                sp.dma_start(b1row[i:i + 1, :].rearrange("i (e f) -> i e f", e=NE), b1p[:, i, :]).then_inc(s_b1row, 16)
            out_view = A["out"].rearrange("(t p) d -> p t d", p=P)
            for q in range(4):
                sp.wait_ge(m5.done, 17 * (q + 1))
                sp.dma_start(out_view[:, 4 * q:4 * q + 4, :], x[:, 4 * q:4 * q + 4, :]).then_inc(s_out, 16)
            sp.wait_ge(s_out, 64)

        @block.gpsimd
        def _(pool):
            nc.gpsimd.memset(ones3[:, :], 1.0).then_inc(s_set, 1)
            nc.gpsimd.memset(xt[:, :, 0:PAD], 0.0).then_inc(s_set, 1)
            nc.gpsimd.memset(zerob[:, :], 0.0).then_inc(s_set, 1)
            pool.wait_ge(s_w, 48)
            nc.gpsimd.tensor_copy(identb[:, :], cc("ident")).then_inc(s_set, 1)
            pool.wait_ge(s_set, 4)
            att_pool_set(pool)
            pool.wait_ge(n3.stat, n3.before(1) + 1)
            nc.gpsimd.memset(l_vp[:, :, :, :], 0.0).then_inc(l.vp, 1)
            mix_pool(pool, m3)
            lin_pool(pool, n4)
            mix_pool(pool, m5)

        def centre_experts(dve, vs):
            dve.wait_ge(s_mix, 64)
            mw, mb = small[:, 20, 0:NE], small[0:NE, 21, 0:1]
            vs.step(nc.vector.tensor_reduce(mw, w1[:, :, :], AX.X, ALU.add))
            vs.step(nc.vector.tensor_scalar(mw, mw, 1.0 / P, None, ALU.mult))
            vs.step(nc.vector.tensor_tensor(w1[:, :, :], w1[:, :, :], bc(mw.unsqueeze(2), [P, NE, P]), ALU.subtract))
            vs.step(nc.vector.tensor_reduce(mb, b1[:, :], AX.X, ALU.add))
            vs.step(nc.vector.tensor_scalar(mb, mb, 1.0 / P, None, ALU.mult))
            vs.step(nc.vector.tensor_scalar(b1[:, :], b1[:, :], mb, None, ALU.subtract))
            vs.step(nc.vector.tensor_copy(b1p[:, 0, :], b1[:, :]))
            vs.step(nc.vector.tensor_tensor(b1r[:, :], b1[:, :], b1p[:, 0, :], ALU.subtract))
            vs.step(nc.vector.tensor_copy(b1p[:, 1, :], b1r[:, :]))
            nc.vector.tensor_tensor(b1p[:, 2, :], b1r[:, :], b1p[:, 1, :], ALU.subtract).then_inc(s_b1, 1)

        @block.vector
        def _(dve):
            vs = Steps(dve, s_v)
            for half in range(2):
                dve.wait_ge(s_x[half], 32)
                norm_vector_stats(dve, vs, n0, half, False)
                if half == 0:
                    dve.wait_ge(s_set, 4)
                    dve.wait_ge(s_w, 48)
                norm_vector_xt(dve, n0, half)
                ffn_vector_mix(dve, vs, n0, f0, half)
                if half == 0:
                    dve.wait_ge(s_wv, 16)
                    nc.vector.tensor_reduce(wvs[:, :], arena_f(28672, P, 8), AX.X, ALU.add).then_inc(s_wvs, 1)
                    nc.vector.tensor_reduce(bvs[:, :], rc("bv").rearrange("p (a b) -> p a b", b=8), AX.X, ALU.add)\
                        .then_inc(s_wvs, 1)
                ffn_vector_add(dve, vs, f0, half)
                norm_vector_stats(dve, vs, n1, half, True)
                norm_vector_xt(dve, n1, half, permuted=True, affine=True)
                dve.wait_ge(s_wvs, 2)
                att_vector_project(dve, half)
            att_vector(dve, vs, centre_experts)
            for half in range(2):
                norm_vector_stats(dve, vs, n2, half, False)
            for half in range(2):
                norm_vector_xt(dve, n2, half)
                ffn_vector_mix(dve, vs, n2, f2, half)
            ffn_vector_add(dve, vs, f2, 0)
            ffn_vector_add(dve, vs, f2, 1)
            for half in range(2):
                norm_vector_stats(dve, vs, n3, half, False)
            for half in range(2):
                norm_vector_xt(dve, n3, half)
            mix_vector_route(dve, vs, m3)
            mix_vector(dve, vs, m3)
            for half in range(2):
                dve.wait_ge(m3.done, 34 * (half + 1))
                norm_vector_stats(dve, vs, n4, half, False)
            for half in range(2):
                norm_vector_xt(dve, n4, half)
            lin_vector(dve, vs)
            dve.wait_ge(l.y, 4)
            for half in range(2):
                norm_vector_stats(dve, vs, n5, half, False)
            for half in range(2):
                norm_vector_xt(dve, n5, half)
            mix_vector_route(dve, vs, m5)
            mix_vector(dve, vs, m5)

        @block.scalar
        def _(act):
            for half in range(2):
                norm_scalar_apply(act, n0, half)
                if half == 0:
                    act.wait_ge(s_w, 48)
                norm_scalar_xt(act, n0, half)
                ffn_scalar(act, f0, half)
                norm_scalar_apply(act, n1, half)
                norm_scalar_xt(act, n1, half, permuted=True, affine=True)
                att_scalar_project(act, half)
            att_scalar(act)
            for half in range(2):
                norm_scalar_apply(act, n2, half)
            for half in range(2):
                norm_scalar_xt(act, n2, half)
            for half in range(2):
                ffn_scalar(act, f2, half)
            for half in range(2):
                norm_scalar_apply(act, n3, half)
            for half in range(2):
                norm_scalar_xt(act, n3, half)
            mix_scalar_route(act, m3)
            mix_scalar(act, m3)
            for half in range(2):
                norm_scalar_apply(act, n4, half)
            for half in range(2):
                norm_scalar_xt(act, n4, half)
            lin_scalar(act)
            for half in range(2):
                norm_scalar_apply(act, n5, half)
            for half in range(2):
                norm_scalar_xt(act, n5, half)
            mix_scalar_route(act, m5)
            mix_scalar(act, m5)

        @block.tensor
        def _(pe):
            pe.wait_ge(s_w, 48)
            pe.wait_ge(s_set, 4)
            for half in range(2):
                norm_tensor(pe, n0, half)
                ffn_tensor(pe, f0, half, projected=half == 1)
                norm_tensor(pe, n1, half)
                att_tensor_project(pe, n1, half)
            pe.wait_ge(a.onesk, 4)
            att_tensor(pe)
            for half in range(2):
                norm_tensor(pe, n2, half)
            for half in range(2):
                ffn_tensor(pe, f2, half)
            for half in range(2):
                norm_tensor(pe, n3, half)
            for half in range(2):
                mix_tensor_logits(pe, n3, m3, half)
            mix_tensor(pe, n3, m3)
            for half in range(2):
                norm_tensor(pe, n4, half)
            lin_tensor(pe, n4)
            for half in range(2):
                norm_tensor(pe, n5, half)
            for half in range(2):
                mix_tensor_logits(pe, n5, m5, half)
            mix_tensor(pe, n5, m5)


def shape_constants(np):
    c = np.zeros((P, CTOTAL), np.float32)

    def put(name, v):
        a, n = CCOLS[name]
        c[:, a:a + n] = v
    i = np.arange(P)
    put("ident", np.eye(P))
    put("causal", (i[:, None] <= i[None, :]))
    put("blocks", (i[:, None] // DK == i[None, :] // DK))
    half = DK // 2
    inv = (np.float32(1.0) / np.power(np.float32(10000.0), np.arange(half, dtype=np.float32) / np.float32(half)))
    ang = np.arange(S, dtype=np.float32)[:, None] * inv.astype(np.float32)[None, :]
    for name, f in (("cos", np.cos), ("sin", np.sin)):
        put(name, f(ang).astype(np.float32).reshape(TB, P, half).transpose(1, 0, 2).reshape(P, TB * half))
    put("rank", NE - np.arange(NE)[None, :])
    put("quarter", (i[:, None] // DK) % 4 == np.arange(4)[None, :])
    put("ones", 1.0)
    return c


def kernel(**inputs):
    import numpy as _np
    import concourse.bacc as _bacc
    from concourse.bass_utils import run_bass_kernel_spmd as _run

    g = {k: _np.ascontiguousarray(v) for k, v in inputs.items()}
    col = lambda v: v.reshape(P, 1)
    rowv = lambda v: v.reshape(1, -1)
    wpack = _np.concatenate([
        g["L0_ffn_W_r"].T, g["L0_ffn_W_k"].T, g["L0_ffn_W_v"].T, g["L0_attn_Wq"], g["L0_attn_Wk"],
        g["L1_attn_Wq"].T, g["L1_attn_Wk"].T, g["L1_attn_Wv"].T, g["L1_attn_Walpha"].T, g["L1_attn_Wbeta"].T,
        g["L1_attn_Wo"].T, g["L1_ffn_Wr"], col(g["L0_ffn_mu_r"]), col(g["L0_ffn_mu_k"]), col(g["L0_attn_gamma"]),
        col(g["L0_attn_beta"]), col(g["L0_attn_bq"]), col(g["L0_attn_bk"]), g["L1_ffn_g1"].T, g["L1_ffn_be1"].T], axis=1)
    rows = _np.concatenate([rowv(g["L0_attn_bv"]), rowv(g["L1_attn_bo"]), rowv(g["L1_attn_balpha"]),
                            rowv(g["L1_attn_bbeta"]), rowv(g["L1_ffn_br"])], axis=1)
    arrays = {
        "x": g["L0_attn_x"].reshape(B * S, P), "wpack": _np.ascontiguousarray(wpack), "consts": shape_constants(_np),
        "rows": _np.ascontiguousarray(rows), "wv": g["L0_attn_Wv"], "w1": g["L1_ffn_W1"], "w2": g["L1_ffn_W2"],
        "b1": g["L1_ffn_b1"], "b2": g["L1_ffn_b2"]}
    nc = _bacc.Bacc("TRN2", target_bir_lowering=False, num_devices=1)
    A = {k: nc.dram_tensor(f"in_{k}", v.shape, F32, kind="ExternalInput").ap() for k, v in arrays.items()}
    A["out"] = nc.dram_tensor("out_x", (B * S, P), F32, kind="ExternalOutput").ap()
    build(nc, A)
    r = _run(nc, [{f"in_{k}": v for k, v in arrays.items()}], core_ids=[0])
    return r.results[0]["out_x"].reshape(B, S, P)
```

```python
from contextlib import ExitStack

import concourse.bass as bass
from concourse import mybir

F32 = mybir.dt.float32
BF16 = mybir.dt.bfloat16
I32 = mybir.dt.int32
ACT = mybir.ActivationFunctionType
ALU = mybir.AluOpType
AX = mybir.AxisListType

P = 128
B, S = 2, 1024
NT = B * S // P
TB = NT // B
NH, DK = 8, 16
NE = 16
EPS = 1e-5
BETA_MIN, BETA_MAX = 0.85, 0.999
RSQRT_SEED = float(0x5F3759DF)
CLOCK_FILL = 28
PAD = 8

WCOLS = {}
_at = 0
for _name, _n in (("ffn_r", P), ("ffn_k", P), ("ffn_v", P), ("att_q", P), ("att_k", P),
                  ("lin_qkvab", 3 * P + 2 * NH), ("lin_o", P), ("router", NE), ("mu_r", 1), ("mu_k", 1),
                  ("gamma", 1), ("beta", 1), ("bq", 1), ("bk", 1), ("g1", NE), ("be1", NE)):
    WCOLS[_name] = (_at, _n)
    _at += _n
WTOTAL = _at
CCOLS = {}
_at = 0
for _name, _n in (("ident", P), ("causal", P), ("blocks", P), ("cos", TB * DK // 2), ("sin", TB * DK // 2),
                  ("rank", NE), ("quarter", 4), ("ones", P), ("head", NH)):
    CCOLS[_name] = (_at, _n)
    _at += _n
CTOTAL = _at
RCOLS = {}
_at = 0
for _name, _n in (("bv", NH * P), ("bo", P), ("ab", 2 * NH), ("br", NE)):
    RCOLS[_name] = (_at, _n)
    _at += _n
RTOTAL = _at


def build(nc, A):
    with ExitStack() as ctx:
        def sb(name, shape, dt=F32):
            return ctx.enter_context(nc.sbuf_tensor(name, shape, dt))

        def sem(name):
            return ctx.enter_context(nc.semaphore(name))

        x = sb("x", [P, NT, P])
        xl = sb("xl", [P, NT, P])
        xt = sb("xt", [P, B, PAD + S])
        w = sb("w", [P, WTOTAL])
        cst = sb("cst", [P, CTOTAL])
        row = sb("row", [P, RTOTAL])
        w1 = sb("w1", [P, NE, P])
        w2 = sb("w2", [P, NE, P])
        wvs = sb("wvs", [P, P])
        bvs = sb("bvs", [P, P])
        b1 = sb("b1", [NE, P])
        b1r = sb("b1r", [NE, P])
        b1p = sb("b1p", [NE, 3, P], BF16)
        b2 = sb("b2", [NE, P])
        b1row = sb("b1row", [3, NE * P], BF16)
        ones3 = sb("ones3", [3, P], BF16)
        identb = sb("identb", [P, P], BF16)
        zerob = sb("zerob", [P, 512], BF16)
        stat = sb("stat", [P, NT, 6])
        small = sb("small", [P, 24, 64])
        smalli = sb("smalli", [P, 2, 64], I32)
        arena = sb("arena", [P, 32 * 1024])
        ps = ctx.enter_context(nc.psum_tensor("ps", [P, 8, 512], F32))
        scratch = nc.dram_tensor("att_parts", [B, 2, NH, 3, DK, S], BF16, kind="Internal").ap()

        def wc(name):
            a, n = WCOLS[name]
            return w[:, a:a + n]

        def cc(name):
            a, n = CCOLS[name]
            return cst[:, a:a + n]

        def rc(name):
            a, n = RCOLS[name]
            return row[:, a:a + n]

        def arena_f(at, *shape):
            n = 1
            for d in shape:
                n *= d
            v = arena[:, at:at + n]
            names = "abcd"[:len(shape)]
            if len(shape) == 1:
                return v
            return v.rearrange("p (" + " ".join(names) + ") -> p " + " ".join(names),
                               **{k: d for k, d in zip(names, shape)})

        def arena_b(at, *shape):
            n = 1
            for d in shape:
                n *= d
            v = arena[:, at:at + n // 2].bitcast(BF16)
            names = "abcd"[:len(shape)]
            return v.rearrange("p (" + " ".join(names) + ") -> p " + " ".join(names),
                               **{k: d for k, d in zip(names, shape)})

        s_x = [sem(f"x_loaded{half}") for half in range(B)]
        s_w = sem("weights_loaded")
        s_mix = sem("expert_weights_loaded")
        s_out = sem("out_stored")
        s_v = sem("vector_steps")
        s_p = sem("pool_steps")
        s_set = sem("constants_set")
        s_b1 = sem("b1_parts_ready")
        s_b1row = sem("b1_rows_loaded")
        s_wv = sem("wv_loaded")
        s_wvs = sem("summed_wv_ready")

        class Steps:

            def __init__(self, eng, s):
                self.eng, self.s, self.n = eng, s, 0

            def mark(self, ins):
                ins.then_inc(self.s, 1)
                self.n += 1
                return self.n

            def step(self, ins):
                self.eng.wait_ge(self.s, self.mark(ins))

            def advance(self, chain):
                if chain.last:
                    self.eng.wait_ge(self.s, chain.last)
                chain.last = next(chain.steps, None)
                return chain.last is None

            def finish(self, chain):
                while not self.advance(chain):
                    pass

        class Chain:

            def __init__(self, steps):
                self.steps, self.last = steps, 0

        def keep_clock(pe, bank, n):
            for _ in range(n):
                pe.matmul(ps[:, bank, :], zerob[:, 0:P], zerob[:, :], start=True, stop=True)

        def bc(ap, shape):
            return ap.to_broadcast(shape)

        class Norm:
            stat = sem("norm_stats")
            xl_v, xl_a = sem("norm_xl_by_vector"), sem("norm_xl_by_scalar")
            tp = sem("norm_turned")
            xt_v, xt_a = sem("norm_xt_by_vector"), sem("norm_xt_by_scalar")

            def __init__(self, first, stride=1):
                self.first, self.stride = first, stride

            def before(self, half):
                return self.first + self.stride * half

        rstd = small[:, 0, 0:NT]
        nmr = small[:, 1, 0:NT]
        mean = small[:, 2, 0:NT]

        def rsqrt(vs, out, v, n, at=12, ti=0):
            y, t, hv = small[:, at, 0:n], small[:, at + 1, 0:n], small[:, at + 2, 0:n]
            yield vs.mark(nc.vector.tensor_scalar(smalli[:, ti, 0:n], v.bitcast(I32), 1, None, ALU.logical_shift_right))
            yield vs.mark(nc.vector.tensor_scalar(y.bitcast(I32), smalli[:, ti, 0:n], -1.0, RSQRT_SEED, ALU.mult, ALU.add))
            yield vs.mark(nc.vector.tensor_scalar(hv, v, -0.5, None, ALU.mult))
            for it in range(3):
                yield vs.mark(nc.vector.tensor_tensor(t, y, y, ALU.mult))
                yield vs.mark(nc.vector.tensor_tensor(t, t, hv, ALU.mult))
                yield vs.mark(nc.vector.scalar_tensor_tensor(out=out if it == 2 else y, in0=t, scalar=1.5, in1=y,
                                                       op0=ALU.add, op1=ALU.mult))

        def norm_vector_stats(dve, vs, n, half, double):
            lo, hi = TB * half, TB * (half + 1)
            for t in range(lo, hi):
                ins = nc.vector.bn_stats(stat[:, t, :], x[:, t, :])
                if t % 2 and t < hi - 1:
                    yield 0
            yield vs.mark(ins)
            me, mo = stat[:, lo:hi, 1], stat[:, lo:hi, 4]
            ve, vo = stat[:, lo:hi, 2], stat[:, lo:hi, 5]
            d, d2, v, v4 = (small[:, i, 0:TB] for i in (4, 5, 6, 7))
            nc.vector.tensor_tensor(d, me, mo, ALU.subtract)
            nc.vector.tensor_tensor(v, ve, vo, ALU.add)
            yield vs.mark(nc.vector.tensor_tensor(mean[:, lo:hi], me, mo, ALU.add))
            nc.vector.tensor_scalar(mean[:, lo:hi], mean[:, lo:hi], 0.5, None, ALU.mult)
            yield vs.mark(nc.vector.tensor_tensor(d2, d, d, ALU.mult))
            yield vs.mark(nc.vector.scalar_tensor_tensor(out=v4, in0=v, scalar=4.0 / P, in1=d2, op0=ALU.mult, op1=ALU.add))
            yield vs.mark(nc.vector.tensor_scalar(v, v4, 0.25, EPS, ALU.mult, ALU.add))
            r = rstd[:, lo:hi]
            yield from rsqrt(vs, r, v, TB)
            if double:
                u, r2 = small[:, 8, 0:TB], small[:, 9, 0:TB]
                yield vs.mark(nc.vector.tensor_tensor(d2, r, r, ALU.mult))
                yield vs.mark(nc.vector.scalar_tensor_tensor(out=u, in0=v4, scalar=0.25, in1=d2, op0=ALU.mult, op1=ALU.mult))
                yield vs.mark(nc.vector.tensor_scalar(u, u, EPS, None, ALU.add))
                yield from rsqrt(vs, r2, u, TB)
                yield vs.mark(nc.vector.tensor_tensor(r, r, r2, ALU.mult))
            nc.vector.scalar_tensor_tensor(out=nmr[:, lo:hi], in0=mean[:, lo:hi], scalar=-1.0, in1=r,
                                           op0=ALU.mult, op1=ALU.mult).then_inc(n.stat, 1)
            for t in range(lo, hi, 2):
                ins = nc.vector.tensor_scalar(xl[:, t, :], x[:, t, :], mean[:, t:t + 1], rstd[:, t:t + 1],
                                              ALU.subtract, ALU.mult)
                if t < hi - 2:
                    yield 0
            ins.then_inc(n.xl_v, 1)

        def norm_scalar_apply(act, n, half):
            act.wait_ge(n.stat, n.before(half) + 1)
            for t in range(TB * half + 1, TB * (half + 1), 2):
                ins = nc.scalar.activation(xl[:, t, :], x[:, t, :], ACT.Identity, bias=nmr[:, t:t + 1],
                                           scale=rstd[:, t:t + 1])
            ins.then_inc(n.xl_a, 1)

        def norm_tensor(pe, n, half):
            pe.wait_ge(n.xl_v, n.before(half) + 1)
            pe.wait_ge(n.xl_a, n.before(half) + 1)
            for g in range(2):
                if n.before(half):
                    pe.wait_ge(n.xt_a if g == 0 else n.xt_v, n.before(half))
                for j in range(4):
                    ins = pe.transpose(ps[:, 6 + g, j * P:(j + 1) * P], xl[:, TB * half + 4 * g + j, :], cc("ident"))
                ins.then_inc(n.tp, 1)

        def xt_out(half, g, permuted):
            if permuted:
                v = xt[:, half, PAD:PAD + S].rearrange("c (j r) -> c j r", j=8)[:, :, 64 * g:64 * g + 64]
                return v
            return xt[:, half, PAD + 512 * g:PAD + 512 * (g + 1)]

        def norm_xt_in(g, permuted):
            if permuted:
                return ps[:, 6 + g, :].rearrange("c (r j) -> c j r", j=8)
            return ps[:, 6 + g, :]

        def norm_scalar_xt(act, n, half, permuted=False, affine=False):
            act.wait_ge(n.tp, 2 * n.before(half) + 1)
            if affine:
                ins = nc.scalar.activation(xt_out(half, 0, permuted), norm_xt_in(0, permuted), ACT.Identity,
                                           bias=wc("beta"), scale=wc("gamma"))
            else:
                ins = nc.scalar.activation(xt_out(half, 0, permuted), norm_xt_in(0, permuted), ACT.Copy)
            ins.then_inc(n.xt_a, 1)

        def norm_vector_xt(dve, n, half, permuted=False, affine=False):
            dve.wait_ge(n.tp, 2 * n.before(half) + 2)
            if affine:
                ins = nc.vector.tensor_scalar(xt_out(half, 1, permuted), norm_xt_in(1, permuted), wc("gamma"),
                                              wc("beta"), ALU.mult, ALU.add)
            else:
                ins = nc.vector.tensor_copy(xt_out(half, 1, permuted), norm_xt_in(1, permuted))
            ins.then_inc(n.xt_v, 1)

        class Ffn:

            def __init__(self, f, places, k_banks, r_banks, v_banks):
                self.signals(f)
                self.banks = {"k": k_banks, "r": r_banks, "v": v_banks}
                self.xd, self.xr, self.xk = ([arena_f(places[b][i], S) for b in range(B)] for i in range(3))
                self.relu_, self.ka_, self.gate_, self.t_ = (
                    [arena_f(places[q // 2][i] + 512 * (q % 2), 512) for q in range(2 * B)] for i in range(3, 7))

            def bank(self, name, q):
                return ps[:, self.banks[name][q % 2], :]

            def signals(self, f):
                self.mixed = sem(f"f{f}_mixed")
                self.k, self.r, self.v = sem(f"f{f}_k"), sem(f"f{f}_r"), sem(f"f{f}_v")
                self.relu, self.ka = sem(f"f{f}_relu"), sem(f"f{f}_relu_squared")
                self.rs = sem(f"f{f}_gate")
                self.done = sem(f"f{f}_gated")

        def ffn_vector_mix(dve, vs, n, f, half):
            dve.wait_ge(n.xt_a, n.before(half) + 1)
            dve.wait_ge(n.xt_v, n.before(half) + 1)
            cur, prev = xt[:, half, PAD:PAD + S], xt[:, half, PAD - 1:PAD - 1 + S]
            vs.step(nc.vector.tensor_tensor(f.xd[half], cur, prev, ALU.subtract))
            nc.vector.scalar_tensor_tensor(out=f.xk[half], in0=f.xd[half], scalar=wc("mu_k"), in1=prev,
                                           op0=ALU.mult, op1=ALU.add).then_inc(f.mixed, 1)
            nc.vector.scalar_tensor_tensor(out=f.xr[half], in0=f.xd[half], scalar=wc("mu_r"), in1=prev,
                                           op0=ALU.mult, op1=ALU.add).then_inc(f.mixed, 1)

        def ffn_tensor_k(pe, f, half):
            for q in (2 * half, 2 * half + 1):
                pe.wait_ge(f.mixed, 2 * half + 1)
                if half:
                    pe.wait_ge(f.relu, q - 1)
                at = 512 * (q % 2)
                pe.matmul(f.bank("k", q), wc("ffn_k"), f.xk[half][:, at:at + 512], start=True, stop=True).then_inc(f.k, 1)

        def ffn_tensor_r(pe, f, half):
            for q in (2 * half, 2 * half + 1):
                pe.wait_ge(f.mixed, 2 * half + 2)
                if f.banks["r"] == f.banks["k"]:
                    pe.wait_ge(f.relu, q + 1)
                elif half:
                    pe.wait_ge(f.rs, q - 1)
                for j in range(4):
                    at = 512 * (q % 2) + j * P
                    ins = pe.matmul(f.bank("r", q)[:, j * P:(j + 1) * P], f.xr[half][:, at:at + P], wc("ffn_r"),
                                    start=True, stop=True)
                ins.then_inc(f.r, 1)

        def ffn_tensor_v(pe, f, half):
            for q in (2 * half, 2 * half + 1):
                pe.wait_ge(f.ka, q + 1)
                if f.banks["v"] == f.banks["r"]:
                    pe.wait_ge(f.rs, q + 1)
                elif half:
                    pe.wait_ge(f.done, q - 1)
                for j in range(4):
                    ins = pe.matmul(f.bank("v", q)[:, j * P:(j + 1) * P], f.ka_[q][:, j * P:(j + 1) * P], wc("ffn_v"),
                                    start=True, stop=True)
                ins.then_inc(f.v, 1)

        def ffn_scalar_k(act, f, half):
            for q in (2 * half, 2 * half + 1):
                act.wait_ge(f.k, q + 1)
                nc.scalar.activation(f.relu_[q], f.bank("k", q), ACT.Relu).then_inc(f.relu, 1)
                act.wait_ge(f.relu, q + 1)
                nc.scalar.activation(f.ka_[q], f.relu_[q], ACT.Square).then_inc(f.ka, 1)

        def ffn_scalar_r(act, f, half):
            for q in (2 * half, 2 * half + 1):
                act.wait_ge(f.r, q + 1)
                nc.scalar.activation(f.gate_[q], f.bank("r", q), ACT.Tanh, scale=0.5).then_inc(f.rs, 1)

        def ffn_vector_add(dve, vs, f, half):
            for q in (2 * half, 2 * half + 1):
                dve.wait_ge(f.rs, q + 1)
                dve.wait_ge(f.v, q + 1)
                nc.vector.scalar_tensor_tensor(out=f.t_[q], in0=f.gate_[q], scalar=1.0, in1=f.bank("v", q), op0=ALU.add,
                                               op1=ALU.mult).then_inc(f.done, 1)
                dve.wait_ge(f.done, q + 1)
                xq = x[:, 4 * q:4 * q + 4, :]
                vs.step(nc.vector.scalar_tensor_tensor(
                    out=xq, in0=f.t_[q].rearrange("p (a b) -> p a b", a=4), scalar=0.25, in1=xq,
                    op0=ALU.mult, op1=ALU.add))

        NQ = 4
        a_qs = arena_b(0, B, NH, S)
        a_ks = arena_b(8192, B, NH, S)
        a_v = arena_f(16384, NT, NH, 32)
        a_p = arena_f(20480, 8, S)
        a_parts = arena_b(20480, B, 6, S)
        a_f = arena_f(20480 + 6144, S)
        a_r = arena_f(20480 + 7168, S)
        a_ot = arena_f(28672, S)
        a_tmp = arena_f(29696, 2, 4, P)
        a_nm = arena_f(30720, 2, 2, 8)
        a_nmr = arena_f(30752, 4, 8)
        a_nmb = arena_b(30784, 2, 24)
        a_nmt = arena_b(30832, 2, P)
        a_rd = arena_f(30960, 8, 4)

        class a:
            raw, f32 = sem("a_qk_product"), sem("a_qk_float")
            p1, r1, p2, p3 = sem("a_part1"), sem("a_rest1"), sem("a_part2"), sem("a_part3")
            vps, v = sem("a_values_product"), sem("a_values")
            stored = [sem(f"a_parts_stored{i}") for i in range(2 * B)]
            stack = [sem(f"a_stack{i}") for i in range(4)]
            onesk = sem("a_ones_set")
            mp, mpu = sem("a_ring_filled"), sem("a_ring_taken")
            mn, nm = sem("a_negmax"), sem("a_negmax_parts")
            nmrow = [sem(f"a_negmax_rows{i}") for i in range(B * NH)]
            st, ex, av = sem("a_scores"), sem("a_probs"), sem("a_values_summed")
            ot_a, ot_v = sem("a_out_by_scalar"), sem("a_out_by_vector")
            otp, done = sem("a_out_turned"), sem("a_out_normalised")

        HEADS = [(b, h) for b in range(B) for h in range(NH)]

        RING_BANKS = (3, 6, 7)
        ring = []
        for hd in range(len(HEADS)):
            for u in range(16):
                ring.append(("mp", hd, u))
                if u == 3 and hd:
                    ring.append(("turn", hd - 1, 0))
        ring.append(("turn", len(HEADS) - 1, 0))
        turn_at = {hd: i for i, (k, hd, u) in enumerate(ring) if k == "turn"}
        RING_FIRST = turn_at[3] + 1 + 4
        RING_SLOTS = 190

        def ring_upto(quad, slot):
            return min(len(ring), RING_FIRST + ((64 * quad + slot) * (len(ring) - RING_FIRST) + RING_SLOTS - 1) // RING_SLOTS)

        LAST_QUAD = 2 * 32 * 3

        def score_bank(unit):
            return unit % 3 if unit < LAST_QUAD else (unit - LAST_QUAD) % 4

        def att_tensor_project(pe, n, half):
            pe.wait_ge(n.xt_a, n.before(half) + 1)
            pe.wait_ge(n.xt_v, n.before(half) + 1)
            if half == 0:
                pe.wait_ge(s_wvs, 2)
            for i, name in enumerate(("att_q", "att_k")):
                if half:
                    pe.wait_ge(a.f32, i + 1)
                for g in range(2):
                    ins = pe.matmul(ps[:, 2 * i + g, :], wc(name), xt[:, half, PAD + 512 * g:PAD + 512 * (g + 1)],
                                    start=True, stop=True)
                ins.then_inc(a.raw, 1)
            if half:
                pe.wait_ge(a.v, 1)
            for t in range(TB):
                ins = pe.matmul(ps[:, 4 + t // 4, (t % 4) * P:(t % 4 + 1) * P],
                                xt[:, half, PAD + t * P:PAD + (t + 1) * P], wvs[:, :], start=True, stop=True)
            ins.then_inc(a.vps, 1)

        def att_scalar_project(act, half, between=None):
            for i in range(2):
                u = 2 * half + i
                if i and between:
                    between()
                act.wait_ge(a.raw, u + 1)
                if u:
                    act.wait_ge(a.r1, u)
                nc.scalar.activation(a_f[:, :].rearrange("p (a b) -> p a b", a=2), ps[:, 2 * i:2 * i + 2, :],
                                     ACT.Identity, bias=wc("bq" if i == 0 else "bk")).then_inc(a.f32, 1)
                act.wait_ge(a.f32, u + 1)
                nc.scalar.activation(a_parts[:, half, 3 * i, :], a_f[:, :], ACT.Copy).then_inc(a.p1, 1)
                act.wait_ge(a.r1, u + 1)
                nc.scalar.activation(a_parts[:, half, 3 * i + 1, :], a_r[:, :], ACT.Copy).then_inc(a.p2, 1)

        def att_vector_project(dve, half, between=None):
            for i in range(2):
                u = 2 * half + i
                if i and between:
                    between()
                dve.wait_ge(a.p1, u + 1)
                if u:
                    dve.wait_ge(a.p3, u)
                nc.vector.tensor_tensor(a_r[:, :], a_f[:, :], a_parts[:, half, 3 * i, :], ALU.subtract).then_inc(a.r1, 1)
                if i == 0:
                    dve.wait_ge(a.vps, half + 1)
                    nc.vector.tensor_tensor(
                        a_v[:, TB * half:TB * (half + 1), :, 0:DK],
                        ps[:, 4:6, :].rearrange("p a (b c d) -> p (a b) c d", b=4, c=NH),
                        bc(bvs[:, :].rearrange("p (c d) -> p c d", c=NH).unsqueeze(1), [P, TB, NH, DK]),
                        ALU.add).then_inc(a.v, 1)
                dve.wait_ge(a.r1, u + 1)
                dve.wait_ge(a.p2, u + 1)
                nc.vector.tensor_tensor(a_parts[:, half, 3 * i + 2, :], a_r[:, :], a_parts[:, half, 3 * i + 1, :],
                                        ALU.subtract).then_inc(a.p3, 1)

        def att_sync_stack(sp, b):
            def to_dram(i):
                for k, made in enumerate((a.p1, a.p2, a.p3)):
                    sp.wait_ge(made, 2 * b + i + 1)
                    sp.dma_start(scratch[b, i, :, k], a_parts[:, b, 3 * i + k, :]).then_inc(a.stored[2 * b + i], 16)

            def back(i, quad):
                hs = slice(NQ * quad, NQ * quad + NQ)
                sp.wait_ge(a.stored[2 * b + i], 48)
                dst, runs = ((a_qs, ((0, 1), (0, 1), (0, 1), (1, 1), (1, 1), (2, 1))), (a_ks, ((0, 3), (0, 2), (0, 1))))[i]
                at = 0
                for part, n in runs:
                    sp.dma_start(dst[at:at + DK * n, b, hs, :],
                                 scratch[b, i, hs, part:part + n].rearrange("h k d s -> (k d) h s"))\
                        .then_inc(a.stack[2 * b + quad], 16)
                    at += DK * n

            to_dram(0)
            to_dram(1)
            back(0, 0)
            back(1, 0)
            back(0, 1)
            back(1, 1)

        def att_sync_negmax_rows(sp):
            for hd, (b, h) in enumerate(HEADS):
                sp.wait_ge(a.mpu, turn_at[hd] + 1)
                sp.dma_start(a_qs[96:99, b, h, :].rearrange("i (j s) -> i j s", j=8),
                             a_nmt[0:24, hd % 2, :]).then_inc(a.nmrow[hd], 16)

        def att_tensor(pe, between):
            class done:
                ring = 0

            def ring_units(upto):
                while done.ring < upto:
                    u = done.ring
                    kind, hd, k = ring[u]
                    b, h = HEADS[hd]
                    bank = RING_BANKS[u % 3]
                    if kind == "mp":
                        if k == 0 and hd % 4 == 0:
                            pe.wait_ge(a.stack[hd // 4], 16 * 9)
                        if u >= 3:
                            pe.wait_ge(a.mpu, u - 2)
                        j, half = k // 2, k % 2
                        pe.matmul(ps[:, bank, :], a_qs[0:96, b, h, j * P:(j + 1) * P],
                                  a_ks[0:96, b, h, half * 512:(half + 1) * 512], start=True, stop=True).then_inc(a.mp, 1)
                    else:
                        pe.wait_ge(a.nm, hd + 1)
                        pe.wait_ge(a.mpu, u - 2)
                        pe.transpose(ps[0:24, bank, 0:64].bitcast(BF16), a_nmb[:, hd % 2, :], identb[:, :])\
                            .then_inc(a.mp, 1)
                    done.ring += 1

            def scores(v, half):
                step, h4, unit = v // 4, v % 4, 2 * v + half
                quad, i = step // 8, step % 8
                b, h = HEADS[4 * quad + h4]
                if i == 0 and half == 0:
                    pe.wait_ge(a.nmrow[4 * quad + h4], 16)
                if unit == LAST_QUAD + 3:
                    pe.wait_ge(a.mpu, len(ring))
                elif unit >= 3:
                    pe.wait_ge(a.ex, unit - 2 if unit < LAST_QUAD + 3 else unit - 3)
                pe.matmul(ps[:, score_bank(unit), :], a_ks[0:99, b, h, i * P:(i + 1) * P],
                          a_qs[0:99, b, h, half * 512:(half + 1) * 512], start=True, stop=True).then_inc(a.st, 1)

            def values(step, half):
                quad, i = step // 8, step % 8
                b = HEADS[4 * quad][0]
                if i == 0 and quad:
                    pe.wait_ge(a.done, quad)
                pe.wait_ge(a.ex, 8 * step + 8)
                for h4 in range(4):
                    h = HEADS[4 * quad + h4][1]
                    ins = pe.matmul(ps[32 * h4:32 * h4 + 32, 4 + half, :], a_v[:, TB * b + i, h, :],
                                    a_p[:, (4 * step + h4) % 8, half * 512:(half + 1) * 512],
                                    start=(i == 0), stop=(i == 7))
                if half:
                    ins.then_inc(a.av, 1)

            def turn_out(quad):
                pe.wait_ge(a.ot_a, quad + 1)
                pe.wait_ge(a.ot_v, quad + 1)
                for j in range(8):
                    ins = pe.transpose(ps[:, 4 + j // 4, (j % 4) * P:(j % 4 + 1) * P], a_ot[:, j * P:(j + 1) * P],
                                       cc("ident"))
                ins.then_inc(a.otp, 1)

            pe.wait_ge(a.v, 2)
            pe.wait_ge(a.f32, 4)
            ring_units(RING_FIRST)
            for step in range(32):
                quad, i = step // 8, step % 8
                for h4 in range(4):
                    for half in range(2):
                        scores(4 * step + h4, half)
                        ring_units(ring_upto(quad, 8 * i + 2 * h4 + half + 1))
                    if h4 % 2 == 1 and step:
                        if i == 1 and quad and h4 == 1:
                            turn_out(quad - 1)
                        values(step - 1, h4 // 2)
                    if h4 == 3:
                        between(pe, step)
            for half in range(2):
                values(31, half)
            turn_out(3)

        def att_vector(dve, vs, before_last_copy, in_last_quad):
            def halves_joined(hd):
                dve.wait_ge(a.mpu, ring.index(("mp", hd, 15)) + 1)
                if hd >= 2:
                    dve.wait_ge(a.nm, hd - 1)
                nc.vector.tensor_tensor(a_nmr[:, hd % 2, :], a_nm[:, hd % 2, 0, :], a_nm[:, hd % 2, 1, :], ALU.min)\
                    .then_inc(a.mn, 1)

            class done:
                ring = 0

            def ring_units(upto):
                while done.ring < upto:
                    u = done.ring
                    kind, hd, k = ring[u]
                    dve.wait_ge(a.mp, u + 1)
                    if kind == "mp":
                        nc.vector.tensor_reduce(a_nm[:, hd % 2, k % 2, k // 2:k // 2 + 1], ps[:, RING_BANKS[u % 3], :], AX.X,
                                                ALU.max, negate=True).then_inc(a.mpu, 1)
                        if k == 0 and hd:
                            halves_joined(hd - 1)
                        if hd == len(HEADS) - 1 and k == 15:
                            halves_joined(hd)
                    else:
                        if hd >= 2:
                            dve.wait_ge(a.nmrow[hd - 2], 16)
                        nc.vector.tensor_copy(a_nmt[0:24, hd % 2, :], ps[0:24, RING_BANKS[u % 3], 0:64].bitcast(BF16))\
                            .then_inc(a.mpu, 1)
                    done.ring += 1

            def out_copy(quad):
                dve.wait_ge(a.av, 8 * (quad + 1))
                if quad:
                    dve.wait_ge(a.otp, quad)
                nc.vector.tensor_copy(a_ot[:, 512:1024], ps[:, 5, :]).then_inc(a.ot_v, 1)

            def out_add(quad):
                dve.wait_ge(a.otp, quad + 1)
                b, h0 = HEADS[4 * quad]
                o = ps[:, 4:6, :].rearrange("p a (j h e) -> p (a j) h e", j=4, h=4)
                vs.step(nc.vector.reciprocal(a_rd[:, :, :], o[:, :, :, DK]))
                for half in range(2):
                    dst = a_tmp[:, quad % 2, :, :].rearrange("p h (j g) -> p j h g", j=8)[:, 4 * half:4 * half + 4]
                    ins = nc.vector.tensor_tensor(
                        dst, o[:, 4 * half:4 * half + 4, :, 0:DK],
                        bc(a_rd[:, 4 * half:4 * half + 4, :].unsqueeze(3), [P, 4, 4, DK]), ALU.mult)
                ins.then_inc(a.done, 1)
                dve.wait_ge(a.done, quad + 1)
                xq = x[:, TB * b + h0:TB * b + h0 + 4, :]
                vs.step(nc.vector.tensor_tensor(xq, xq, a_tmp[:, quad % 2, :, :], ALU.add))

            ring_units(RING_FIRST)
            for quad in range(4):
                if quad == 3:
                    before_last_copy(dve, vs)
                if quad:
                    ring_units(ring_upto(quad, 8))
                    out_copy(quad - 1)
                    ring_units(ring_upto(quad, 11))
                    out_add(quad - 1)
                ring_units(ring_upto(quad, 64))
            in_last_quad(dve, vs)
            out_copy(3)
            out_add(3)

        def att_scalar(act, between):
            for i in range(2 * B):
                act.wait_ge(a.stored[i], 48)
            for v in range(128):
                step = v // 4
                between(act, v)
                if v % 32 == 4 and v > 4:
                    quad = v // 32 - 1
                    act.wait_ge(a.av, 8 * (quad + 1))
                    if quad:
                        act.wait_ge(a.otp, quad)
                    nc.scalar.activation(a_ot[:, 0:512], ps[:, 4, :], ACT.Copy).then_inc(a.ot_a, 1)
                if step >= 2:
                    act.wait_ge(a.av, step - 1)
                for half in range(2):
                    unit = 2 * v + half
                    act.wait_ge(a.st, unit + 1)
                    nc.scalar.activation(a_p[:, v % 8, half * 512:(half + 1) * 512], ps[:, score_bank(unit), :], ACT.Exp,
                                         scale=0.25).then_inc(a.ex, 1)
            between(act, 128)
            act.wait_ge(a.av, 32)
            act.wait_ge(a.otp, 3)
            nc.scalar.activation(a_ot[:, 0:512], ps[:, 4, :], ACT.Copy).then_inc(a.ot_a, 1)

        def att_pool_negmax(pool, gs):
            for hd in range(len(HEADS)):
                pool.wait_ge(a.mn, hd + 1)
                if hd >= 2:
                    pool.wait_ge(a.mp, turn_at[hd - 2] + 1)
                nm, r1 = a_nmr[:, hd % 2, :], a_nmr[:, 2, :]
                parts = a_nmb[:, hd % 2, :].rearrange("p (i j) -> p i j", i=3)
                gs.step(nc.gpsimd.tensor_copy(parts[:, 0, :], nm))
                gs.step(nc.gpsimd.tensor_tensor(r1, nm, parts[:, 0, :], ALU.subtract))
                gs.step(nc.gpsimd.tensor_copy(parts[:, 1, :], r1))
                nc.gpsimd.tensor_tensor(parts[:, 2, :], r1, parts[:, 1, :], ALU.subtract).then_inc(a.nm, 1)
                pool.wait_ge(a.nm, hd + 1)

        def att_pool_set(pool):
            nc.gpsimd.memset(a_ks[96:99, 0, :, :], 1.0).then_inc(a.onesk, 1)
            pool.wait_ge(a.onesk, 1)
            nc.gpsimd.memset(a_v[:, :, :, DK:32], 0.0).then_inc(a.onesk, 1)
            pool.wait_ge(a.onesk, 2)
            nc.gpsimd.memset(a_v[:, :, :, DK:DK + 1], 1.0).then_inc(a.onesk, 1)
            pool.wait_ge(a.onesk, 3)
            pool.wait_ge(n1.stat, n1.before(1) + 1)
            nc.gpsimd.memset(a_ks[96:99, 1, :, :], 1.0).then_inc(a.onesk, 1)

        class Mix:
            def __init__(self, m):
                self.logits, self.e = sem(f"m{m}_logits"), sem(f"m{m}_logit_gap")
                self.w, self.wt, self.wtc = sem(f"m{m}_weights"), sem(f"m{m}_weights_turned"), sem(f"m{m}_weights_by_expert")
                self.h, self.hc, self.hq, self.sqr = sem(f"m{m}_h"), sem(f"m{m}_h_copied"), sem(f"m{m}_h_squared"), sem(f"m{m}_h_sums")
                self.z, self.zt, self.ac = sem(f"m{m}_normed"), sem(f"m{m}_normed_turned"), sem(f"m{m}_gelu")
                self.y, self.tmp, self.done = sem(f"m{m}_y"), sem(f"m{m}_y_weighted"), sem(f"m{m}_x_added")

        AHEAD = 3
        m_s = arena_f(0, 10, NT, NE)
        m_wt = arena_f(2560, NT * P)
        m_h = arena_f(4608, AHEAD, 4, 512)
        m_sq = arena_f(10752, 2, 512)
        m_z = arena_f(11776, 2, 4, 512)
        m_a = arena_f(15872, 4, 512)
        m_tmp = arena_f(17920, 4, 512)
        m_ss = arena_f(19968, AHEAD, 16)
        m_rs = arena_f(20016, AHEAD, 16)
        m_e = arena_f(32128, 4, NT)
        m_unused = arena_b(20080, 4, P)
        m_w = m_s[:, 9]
        LOGIT_BANKS = (5, 6)
        NSU = 16

        def mix_tensor_logits(pe, n, m, half):
            pe.wait_ge(n.xt_a, n.before(half) + 1)
            pe.wait_ge(n.xt_v, n.before(half) + 1)
            for t in range(TB):
                ins = pe.matmul(ps[:, LOGIT_BANKS[half], t * NE:(t + 1) * NE], xt[:, half, PAD + t * P:PAD + (t + 1) * P], wc("router"),
                                start=True, stop=True)
            ins.then_inc(m.logits, 1)

        def mix_vector_route(dve, vs, m, half):
            ts = slice(TB * half, TB * (half + 1))
            lg, t, oh1, oh2, l2 = (m_s[:, i, ts, :] for i in range(5))
            m1, m2, d, r = (m_e[:, i, ts] for i in range(4))
            full = [P, TB, NE]
            dve.wait_ge(m.logits, half + 1)
            yield vs.mark(nc.vector.tensor_tensor(lg, ps[:, LOGIT_BANKS[half], 0:TB * NE].rearrange("p (t e) -> p t e", e=NE),
                                            bc(rc("br").unsqueeze(1), full), ALU.add))
            rank = bc(cc("rank").unsqueeze(1), full)
            src = lg
            for mx, oh in ((m1, oh1), (m2, oh2)):
                yield vs.mark(nc.vector.tensor_reduce(mx, src, AX.X, ALU.max))
                yield vs.mark(nc.vector.tensor_tensor(t, src, bc(mx.unsqueeze(2), full), ALU.is_equal))
                yield vs.mark(nc.vector.tensor_tensor(t, t, rank, ALU.mult))
                yield vs.mark(nc.vector.tensor_reduce(r, t, AX.X, ALU.max))
                yield vs.mark(nc.vector.tensor_tensor(oh, t, bc(r.unsqueeze(2), full), ALU.is_equal))
                if src is lg:
                    yield vs.mark(nc.vector.scalar_tensor_tensor(out=l2, in0=oh, scalar=-3.0e38, in1=lg, op0=ALU.mult,
                                                           op1=ALU.add))
                src = l2
            nc.vector.tensor_tensor(d, m1, m2, ALU.subtract).then_inc(m.e, 1)
            for _ in range(3):
                yield 0
            dve.wait_ge(m.e, 2 * half + 2)
            nc.vector.tensor_scalar(m1, d, 0.25, 0.25, ALU.mult, ALU.add)
            yield vs.mark(nc.vector.tensor_scalar(m2, d, -0.25, 0.25, ALU.mult, ALU.add))
            nc.vector.tensor_tensor(oh1, oh1, bc(m1.unsqueeze(2), full), ALU.mult)
            yield vs.mark(nc.vector.tensor_tensor(oh2, oh2, bc(m2.unsqueeze(2), full), ALU.mult))
            nc.vector.tensor_tensor(m_w[:, ts, :], oh1, oh2, ALU.add).then_inc(m.w, 1)

        def mix_scalar_route(act, m, half):
            act.wait_ge(m.e, 2 * half + 1)
            d = m_e[:, 2, TB * half:TB * (half + 1)]
            nc.scalar.activation(d, d, ACT.Tanh, scale=0.5).then_inc(m.e, 1)

        def mix_tensor_weights(pe, m, half):
            pe.wait_ge(m.w, half + 1)
            for k in range(TB):
                ins = pe.transpose(ps[0:NE, 6 + k // 4, (k % 4) * P:(k % 4 + 1) * P], m_w[:, TB * half + k, :], cc("ident"))
            ins.then_inc(m.wt, 1)

        def mix_scalar_weights(act, m, half):
            act.wait_ge(m.wt, half + 1)
            nc.scalar.activation(m_wt[0:NE, S * half:S * (half + 1)].rearrange("p (a b) -> p a b", a=2),
                                 ps[0:NE, 6:8, :], ACT.Copy).then_inc(m.wtc, 1)

        def mix_tensor_between(pe, n, m, after, s, e):
            if (s, e) == (3, 1):
                pe.wait_ge(m.wtc, 1)
                norm_tensor(pe, n, 1)
            if (s, e) == (4, 0):
                mix_tensor_logits(pe, n, m, 1)
            if (s, e) == (8, 2):
                mix_tensor_weights(pe, m, 1)
            if (s, e) == (12, 1) and after is not None:
                pe.wait_ge(m.wtc, 2)
                norm_tensor(pe, after, 0)

        def mix_scalar_between(act, n, m, after, s, e):
            if (s, e) == (2, 3):
                norm_scalar_apply(act, n, 1)
            if (s, e) == (3, 2):
                norm_scalar_xt(act, n, 1)
            if (s, e) == (5, 2):
                mix_scalar_route(act, m, 1)
            if (s, e) == (9, 0):
                mix_scalar_weights(act, m, 1)
            if (s, e) == (11, 3) and after is not None:
                norm_scalar_apply(act, after, 0)
            if (s, e) == (13, 0) and after is not None:
                norm_scalar_xt(act, after, 0)

        def mix_tensor(pe, n, m, after=None, ffn=None):
            def hidden(s, j):
                u = 4 * s + j
                q, eq = s // 4, s % 4
                half, at = q // 2, PAD + 512 * (q % 2) + j * P
                if u % 32 == 0:
                    pe.wait_ge(n.xt_a, n.before(half) + 1)
                    pe.wait_ge(n.xt_v, n.before(half) + 1)
                if u == 0:
                    pe.wait_ge(s_b1row, 48)
                    pe.wait_ge(s_set, 4)
                if u >= 2:
                    pe.wait_ge(m.hq, u - 1)
                pe.matmul(ps[:, u % 2, :], ones3[:, :], b1row[:, 512 * eq:512 * (eq + 1)], start=True, stop=False)
                pe.matmul(ps[:, u % 2, :], xt[:, half, at:at + P],
                          w1[:, 4 * eq:4 * eq + 4, :].rearrange("c e f -> c (e f)"), start=False, stop=True)\
                    .then_inc(m.h, 1)

            def turn(s, e):
                u = 4 * s + e
                pe.wait_ge(m.z, 4 * s + 4)
                if u >= 2:
                    pe.wait_ge(m.ac, u - 1)
                for j in range(4):
                    ins = pe.transpose(ps[:, 2 + u % 2, j * P:(j + 1) * P], m_z[:, s % 2, j, e * P:(e + 1) * P], cc("ident"))
                ins.then_inc(m.zt, 1)

            def out(s, e):
                u = 4 * s + e
                v = u + s // 4
                pe.wait_ge(m.ac, u + 1)
                if v >= 2:
                    pe.wait_ge(m.tmp, v - 1)
                if v < 2:
                    pe.wait_ge(m.w, 1)
                for j in range(4):
                    ins = pe.matmul(ps[:, 4 + v % 2, j * P:(j + 1) * P], m_a[:, u % 4, j * P:(j + 1) * P],
                                    w2[:, 4 * (s % 4) + e, :], start=True, stop=True)
                ins.then_inc(m.y, 1)

            def out_bias(q):
                v = 17 * q + 16
                if q % 2 == 0:
                    pe.wait_ge(m.wtc, q // 2 + 1)
                pe.wait_ge(m.tmp, v - 1)
                for j in range(4):
                    ins = pe.matmul(ps[:, 4 + v % 2, j * P:(j + 1) * P],
                                    m_wt[0:NE, (4 * q + j) * P:(4 * q + j + 1) * P], b2[:, :], start=True, stop=True)
                ins.then_inc(m.y, 1)

            def finish(u):
                out(u // 4, u % 4)
                if u % 16 == 15:
                    out_bias(u // 16)

            for s in range(AHEAD):
                for j in range(4):
                    hidden(s, j)
                if s == 0:
                    mix_tensor_logits(pe, n, m, 0)
                if ffn is not None:
                    n_ffn, f = ffn
                    if s == 0:
                        norm_tensor(pe, n_ffn, 1)
                    if s == 1:
                        ffn_tensor_k(pe, f, 1)
                    if s == 2:
                        ffn_tensor_r(pe, f, 1)
            for s in range(NSU):
                for e in range(4):
                    if (s, e) == (0, 3) and ffn is not None:
                        ffn_tensor_v(pe, f, 1)
                    mix_tensor_between(pe, n, m, after, s, e)
                    if s + AHEAD < NSU:
                        hidden(s + AHEAD, e)
                    turn(s, e)
                    if 4 * s + e:
                        finish(4 * s + e - 1)
                if s == 1:
                    if ffn is not None:
                        pe.wait_ge(f.done, 4)
                    mix_tensor_weights(pe, m, 0)
            finish(4 * NSU - 1)

        def mix_scalar(act, n, m, after=None, ffn=None):
            def hidden(s, j):
                u = 4 * s + j
                if s >= AHEAD and j == 0:
                    act.wait_ge(m.z, 4 * (s - AHEAD) + 4)
                act.wait_ge(m.h, u + 1)
                nc.scalar.activation(m_h[:, s % AHEAD, j, :], ps[:, u % 2, :], ACT.Copy).then_inc(m.hc, 1)
                if u % 2 == 0:
                    if u >= 4:
                        act.wait_ge(m.sqr, u // 2 - 1)
                    nc.scalar.activation(m_sq[:, u // 2 % 2, :], ps[:, u % 2, :], ACT.Square).then_inc(m.hq, 1)
                else:
                    if u >= 3:
                        act.wait_ge(m.hq, u - 1)
                    for e in range(4):
                        ins = nc.scalar.activation(m_unused[:, e, :], ps[:, u % 2, e * P:(e + 1) * P], ACT.Square,
                                                   accum_out=m_ss[:, s % AHEAD, 4 * j + e:4 * j + e + 1])
                    ins.then_inc(m.hq, 1)

            for s in range(AHEAD):
                for j in range(4):
                    hidden(s, j)
                if ffn is not None:
                    n_ffn, f = ffn
                    if s == 0:
                        norm_scalar_apply(act, n_ffn, 1)
                        norm_scalar_xt(act, n_ffn, 1)
                    if s == 1:
                        ffn_scalar_k(act, f, 1)
                    if s == 2:
                        ffn_scalar_r(act, f, 1)
                if s == 1:
                    mix_scalar_route(act, m, 0)
            for s in range(NSU):
                for e in range(4):
                    mix_scalar_between(act, n, m, after, s, e)
                    if s + AHEAD < NSU:
                        hidden(s + AHEAD, e)
                    u = 4 * s + e
                    ex = 4 * (s % 4) + e
                    act.wait_ge(m.zt, u + 1)
                    if u >= 4:
                        act.wait_ge(m.y, u - 4 + (u - 4) // 16 + 1)
                    nc.scalar.activation(m_a[:, u % 4, :], ps[:, 2 + u % 2, :], ACT.Gelu,
                                         bias=wc("be1")[:, ex:ex + 1], scale=wc("g1")[:, ex:ex + 1]).then_inc(m.ac, 1)
                if s == 1:
                    mix_scalar_weights(act, m, 0)

        def mix_vector(dve, vs, n, m, after=None, ffn=None):
            def squares(s, j):
                u = 4 * s + j
                if u % 2:
                    return
                dve.wait_ge(m.hq, u + 1)
                nc.vector.tensor_reduce(m_ss[:, s % AHEAD, 4 * j:4 * j + 4],
                                        m_sq[:, u // 2 % 2, :].rearrange("p (e f) -> p e f", e=4), AX.X, ALU.add)\
                    .then_inc(m.sqr, 1)

            def rstds(s):
                dve.wait_ge(m.sqr, 2 * s + 2)
                dve.wait_ge(m.hq, 4 * s + 4)
                v = m_ss[:, s % AHEAD, :]
                yield vs.mark(nc.vector.tensor_scalar(v, v, 1.0 / P, EPS, ALU.mult, ALU.add))
                yield from rsqrt(vs, m_rs[:, s % AHEAD, :], v, 16, at=16, ti=1)

            def scaled(s, j):
                dve.wait_ge(m.hc, 4 * s + 4)
                if s >= 2 and j == 0:
                    dve.wait_ge(m.zt, 4 * (s - 2) + 4)
                nc.vector.tensor_tensor(
                    m_z[:, s % 2, j, :].rearrange("p (e f) -> p e f", e=4),
                    m_h[:, s % AHEAD, j, :].rearrange("p (e f) -> p e f", e=4),
                    bc(m_rs[:, s % AHEAD, 4 * j:4 * j + 4].unsqueeze(2), [P, 4, P]), ALU.mult).then_inc(m.z, 1)

            def weighted(v):
                q, k = v // 17, v % 17
                if q % 2 == 0 and k == 0:
                    dve.wait_ge(m.w, q // 2 + 1)
                dve.wait_ge(m.y, v + 1)
                if v >= 4:
                    dve.wait_ge(m.done, v - 3)
                y = ps[:, 4 + v % 2, :].rearrange("p (j o) -> p j o", j=4)
                dst = m_tmp[:, v % 4, :].rearrange("p (j o) -> p j o", j=4)
                if k < 16:
                    wgt = m_w[:, 4 * q:4 * q + 4, k:k + 1]
                    nc.vector.tensor_tensor(dst, y, bc(wgt, [P, 4, P]), ALU.mult).then_inc(m.tmp, 1)
                else:
                    nc.vector.tensor_copy(dst, y).then_inc(m.tmp, 1)

            def finished(u):
                weighted(u + u // 16)
                if u % 16 == 15:
                    weighted(u + u // 16 + 1)

            def behind_at(s):
                if s == 1:
                    return Chain(norm_vector_stats(dve, vs, n, 1, False))
                if s == 4:
                    return Chain(mix_vector_route(dve, vs, m, 1))
                if s == 9 and after is not None:
                    dve.wait_ge(m.done, 34)
                    return Chain(norm_vector_stats(dve, vs, after, 0, False))
                return None

            for j in range(4):
                squares(0, j)
            if ffn is not None:
                n_ffn, f = ffn
                norm_vector_xt(dve, n_ffn, 1)
                ffn_vector_mix(dve, vs, n_ffn, f, 1)
            rs, route = Chain(rstds(0)), Chain(mix_vector_route(dve, vs, m, 0))
            for j in range(4):
                squares(1, j)
                vs.advance(rs)
                vs.advance(route)
            for k in range(9):
                vs.advance(route)
                vs.advance(rs)
            vs.finish(rs)
            rs = Chain(rstds(1))
            for j in range(4):
                scaled(0, j)
                vs.advance(rs)
            for j in range(4):
                squares(2, j)
                vs.advance(rs)
                vs.advance(route)
            vs.finish(rs)
            vs.finish(route)
            behind = None
            for s in range(NSU):
                rs = Chain(rstds(s + 2)) if s + 2 < NSU else None
                if s == 1 and ffn is not None:
                    ffn_vector_add(dve, vs, f, 1)
                if s in (1, 4, 9):
                    behind = behind_at(s)
                for j in range(4):
                    if (s, j) == (3, 3):
                        norm_vector_xt(dve, n, 1)
                    if (s, j) == (13, 0) and after is not None:
                        norm_vector_xt(dve, after, 0)
                    for k in range(3):
                        if k == 0 and s + 1 < NSU:
                            scaled(s + 1, j)
                        if k == 1 and s + AHEAD < NSU:
                            squares(s + AHEAD, j)
                        if k == 2 and 4 * s + j:
                            finished(4 * s + j - 1)
                        if rs is not None and vs.advance(rs):
                            rs = None
                        if behind is not None and vs.advance(behind):
                            behind = None
                if rs is not None:
                    vs.finish(rs)
            finished(4 * NSU - 1)

        def mix_pool(pool, m):
            for v in range(68):
                q = v // 17
                pool.wait_ge(m.tmp, v + 1)
                if v:
                    pool.wait_ge(m.done, v)
                xq = x[:, 4 * q:4 * q + 4, :]
                nc.gpsimd.tensor_tensor(xq, xq, m_tmp[:, v % 4, :].rearrange("p (j o) -> p j o", j=4), ALU.add)\
                    .then_inc(m.done, 1)

        NG = 2 * NH
        l_g = arena_f(0, NT, 3 * P)
        l_q = arena_f(6400, NT, P)
        l_k = arena_f(8448, NT, P)
        l_tv = arena_f(10496, 4, 512)
        l_tp = arena_f(12544, 4, 512)
        l_gate = arena_f(14592, NT, 2 * NH)
        l_ln = arena_f(14848, NT, NH)
        l_dq = arena_f(14976, NT, NH)
        l_dk = arena_f(15104, NT, NH)
        l_tot = arena_f(15232, NT, NH)
        l_ot = arena_f(15616, NT, P)
        l_qm = arena_f(17664, 4, NT * P)
        l_kt = arena_f(8448, NT * P)
        l_as = arena_f(10496, 2, NH, P)
        l_te = arena_f(25856, NT, P)
        l_et = arena_f(27904, NT)
        l_vp = arena_f(28032, NT, NH, 2 * DK)
        l_qt = arena_f(6400, NT * P)
        l_s = xl

        KV_BANKS = (0, 1, 5, 6)

        class l:
            g, g_in = sem("l_products"), sem("l_products_in")
            g_in_v, gp = sem("l_products_in_by_vector"), sem("l_gate_products")
            gate, sig, bet, ln = sem("l_gates"), sem("l_sigmoids"), sem("l_beta"), sem("l_ln_beta")
            cum, dec, dk = sem("l_sums"), sem("l_decays"), sem("l_key_decay")
            q, kp = sem("l_q"), sem("l_k_steps")
            qt, qm, kt, ktc = sem("l_q_turned"), sem("l_q_in"), sem("l_k_turned"), sem("l_k_in")
            kv, te, s = sem("l_kv"), sem("l_kv_in"), sem("l_states")
            sc, as_ = sem("l_scores"), sem("l_scores_masked")
            vp, o, oc = sem("l_values_spread"), sem("l_out"), sem("l_out_in")
            done, y, bo = sem("l_projected"), sem("l_x_added"), sem("l_bias_added")

        def lin_tensor(pe, n):
            def columns(t):
                return xt[:, t // TB, PAD + (t % TB) * P:PAD + (t % TB + 1) * P]

            def product(t):
                if t >= 4:
                    pe.wait_ge(l.g_in_v if t % 2 else l.g_in, t // 2 - 1)
                a0 = WCOLS["lin_qkvab"][0]
                pe.matmul(ps[:, t % 4, 0:3 * P], columns(t), w[:, a0:a0 + 3 * P], start=True, stop=True).then_inc(l.g, 1)

            for b in range(B):
                if b:
                    keep_clock(pe, 5, 16)
                    norm_tensor(pe, n, 1)
                pe.wait_ge(n.xt_a, n.before(b) + 1)
                pe.wait_ge(n.xt_v, n.before(b) + 1)
                for t in range(TB * b, TB * (b + 1)):
                    a0 = WCOLS["lin_qkvab"][0] + 3 * P
                    ins = pe.matmul(ps[:, 4, t * NG:(t + 1) * NG], columns(t), w[:, a0:a0 + NG], start=True, stop=True)
                ins.then_inc(l.gp, 1)
                for t in range(4 * b, 4 * (b + 1)):
                    product(t)
            pe.wait_ge(l.ln, 1)
            pe.matmul(ps[:, 5, 0:P], cc("causal"), l_ln.rearrange("p t h -> p (t h)"), start=True, stop=True)
            pe.matmul(ps[:, 5, P:2 * P], cc("ones"), l_ln.rearrange("p t h -> p (t h)"), start=True, stop=True)\
                .then_inc(l.cum, 1)
            for t in range(TB, NT):
                product(t)

            def q_turn(g):
                if g >= 2:
                    pe.wait_ge(l.qm, 5 * (g - 1))
                for j in range(4):
                    ins = pe.transpose(ps[:, 2 + g % 2, j * P:(j + 1) * P], l_q[:, 4 * g + j, :], cc("ident"))
                ins.then_inc(l.qt, 1)

            def k_turn(g):
                for j in range(4):
                    ins = pe.transpose(ps[:, 6 + g % 2, j * P:(j + 1) * P], l_k[:, 4 * g + j, :], cc("ident"))
                ins.then_inc(l.kt, 1)
                if g == 3:
                    pe.wait_ge(l.ktc, 3)
                for j in range(4):
                    t = 4 * g + j
                    ins = pe.matmul(ps[:, KV_BANKS[g], j * P:(j + 1) * P], l_k[:, t, :], l_g[:, t, 2 * P:3 * P],
                                    start=True, stop=True)
                ins.then_inc(l.kv, 1)

            pe.wait_ge(l.g_in, NT // 2)
            pe.wait_ge(l.g_in_v, NT // 2)
            pe.wait_ge(l.q, 1)
            q_turn(0)
            q_turn(1)
            pe.wait_ge(l.kp, 7)
            k_turn(0)
            k_turn(1)
            pe.wait_ge(l.q, 2)
            q_turn(2)
            q_turn(3)
            keep_clock(pe, 4, 12)
            pe.wait_ge(l.te, 2)
            pe.wait_ge(l.ktc, 2)
            pe.wait_ge(l.vp, 3)

            def scores(t, k):
                if t >= 2:
                    pe.wait_ge(l.as_, 2 * (t - 2) + k + 1)
                if t == 1 and k == 0:
                    pe.wait_ge(l.qm, 20)
                if t == TB and k == 0:
                    pe.wait_ge(l.ktc, 4)
                r = slice(64 * k, 64 * k + 64)
                pe.matmul(ps[:, 2 * (t % 2) + k, :], l_kt[r, t * P:(t + 1) * P], l_qm[r, :, t * P:(t + 1) * P],
                          start=True, stop=True).then_inc(l.sc, 1)

            def values(t):
                g, at = t // 4, (t % 4) * P
                if t % 4 == 0 and g >= 2:
                    pe.wait_ge(l.oc, g - 1)
                if t % TB == 0:
                    pe.wait_ge(l.s, t // TB + 1)
                if t == 4:
                    pe.wait_ge(l.te, 3)
                pe.matmul(ps[:, 4 + g % 2, at:at + P], l_s[:, t, :], l_qt[:, t * P:(t + 1) * P], start=True, stop=False)
                pe.wait_ge(l.as_, 2 * t + 2)
                for par in range(2):
                    for i in range(4):
                        ins = pe.matmul(ps[32 * i:32 * i + 32, 4 + g % 2, at:at + P], l_vp[:, t, 2 * i + par, :],
                                        l_as[:, t % 2, 2 * i + par, :], start=False, stop=(par == 1))
                ins.then_inc(l.o, 1)

            def project(g):
                pe.wait_ge(l.oc, g + 1)
                if g == 0:
                    pe.wait_ge(l.te, 4)
                if g >= 2:
                    pe.wait_ge(l.y, g - 1)
                for j in range(4):
                    ins = pe.matmul(ps[:, 6 + g % 2, j * P:(j + 1) * P], l_ot[:, 4 * g + j, :], wc("lin_o"),
                                    start=True, stop=True)
                ins.then_inc(l.done, 1)

            for t in range(NT):
                scores(t, 0)
                scores(t, 1)
                if t == 3:
                    pe.wait_ge(l.kp, 14)
                    k_turn(2)
                    k_turn(3)
                if t:
                    values(t - 1)
                if t >= 6 and t % 4 == 2:
                    project(t // 4 - 1)
            values(NT - 1)
            project(3)

        def lin_scalar(act, n, after):
            def product_in(t):
                act.wait_ge(l.g, t + 1)
                nc.scalar.activation(l_g[:, t, :], ps[:, t % 4, 0:3 * P], ACT.Copy).then_inc(l.g_in, 1)

            product_in(0)
            product_in(2)
            norm_scalar_apply(act, n, 1)
            norm_scalar_xt(act, n, 1)
            act.wait_ge(l.gate, 1)
            nc.scalar.activation(l_gate[:, :, :], l_gate[:, :, :], ACT.Sigmoid).then_inc(l.sig, 1)
            act.wait_ge(l.bet, 1)
            nc.scalar.activation(l_ln[:, :, :], l_ln[:, :, :], ACT.Ln).then_inc(l.ln, 1)
            for t in range(4, TB, 2):
                product_in(t)
            act.wait_ge(l.cum, 1)
            cum = ps[:, 5, 0:P].rearrange("p (t h) -> p t h", h=NH)
            nc.scalar.activation(l_dq[:, :, :], cum, ACT.Exp).then_inc(l.dec, 1)
            nc.scalar.activation(l_dk[:, :, :], cum, ACT.Exp, scale=-1.0).then_inc(l.dec, 1)
            nc.scalar.activation(l_tot[:, :, :], ps[:, 5, P:2 * P].rearrange("p (t h) -> p t h", h=NH), ACT.Exp)\
                .then_inc(l.dec, 1)
            for t in range(TB, NT, 2):
                product_in(t)
            act.wait_ge(l.g_in, NT // 2)
            act.wait_ge(l.g_in_v, NT // 2)
            act.wait_ge(l.vp, 1)
            for par in range(2):
                nc.scalar.activation(
                    l_vp.rearrange("p t (i two) d -> p t i two d", two=2)[:, :, :, par, DK * par:DK * par + DK],
                    l_g[:, :, 2 * P:3 * P].rearrange("p t (i two d) -> p t i two d", two=2, d=DK)[:, :, :, par, :],
                    ACT.Copy).then_inc(l.vp, 1)
            def q_in(g):
                act.wait_ge(l.qt, g + 1)
                for m in range(4):
                    nc.scalar.activation(l_qm[:, m, 512 * g:512 * (g + 1)], ps[:, 2 + g % 2, :], ACT.Copy,
                                         scale=cc("quarter")[:, m:m + 1]).then_inc(l.qm, 1)
                nc.scalar.activation(l_qt[:, 512 * g:512 * (g + 1)], ps[:, 2 + g % 2, :], ACT.Copy).then_inc(l.qm, 1)

            def k_in(g):
                act.wait_ge(l.kt, g + 1)
                act.wait_ge(l.kv, g + 1)
                nc.scalar.activation(l_kt[:, 512 * g:512 * (g + 1)], ps[:, 6 + g % 2, :], ACT.Copy).then_inc(l.ktc, 1)

            for b in range(B):
                if b == 0:
                    q_in(0)
                    q_in(1)
                    k_in(0)
                    k_in(1)
                    q_in(2)
                    q_in(3)
                else:
                    k_in(2)
                    k_in(3)
            for g in range(4):
                if g == 3:
                    norm_scalar_apply(act, after, 0)
                act.wait_ge(l.o, 4 * g + 4)
                nc.scalar.activation(l_ot[:, 4 * g:4 * g + 4, :].rearrange("p a b -> p (a b)"), ps[:, 4 + g % 2, :],
                                     ACT.Copy).then_inc(l.oc, 1)

        def lin_rope(eng, src, t4, b, after, each=False):
            pairs = src[:, TB * b:TB * (b + 1), :].rearrange("p t (h i two) -> p t h i two", h=NH, two=2)
            x1, x2 = pairs[:, :, :, :, 0], pairs[:, :, :, :, 1]
            sh = [P, TB, NH, DK // 2]
            cos = bc(cc("cos").rearrange("p (t i) -> p t i", t=TB).unsqueeze(2), sh)
            sin = bc(cc("sin").rearrange("p (t i) -> p t i", t=TB).unsqueeze(2), sh)
            tt = [t4[:, i, :].rearrange("p (t h i) -> p t h i", t=TB, h=NH) for i in range(4)]
            for out, a0, a1 in ((tt[0], x1, cos), (tt[1], x2, sin), (tt[2], x2, cos), (tt[3], x1, sin)):
                ins = eng.tensor_tensor(out, a0, a1, ALU.mult)
                if each:
                    after(ins)
            if not each:
                after(ins)
            return (x1, tt[0], tt[1], ALU.subtract), (x2, tt[2], tt[3], ALU.add)

        def lin_vector(dve, vs, n, m, after):
            def product_in(t):
                dve.wait_ge(l.g, t + 1)
                nc.vector.tensor_copy(l_g[:, t, :], ps[:, t % 4, 0:3 * P]).then_inc(l.g_in_v, 1)

            dve.wait_ge(m.done, 68)
            vs.finish(Chain(norm_vector_stats(dve, vs, n, 1, False)))
            product_in(1)
            product_in(3)
            norm_vector_xt(dve, n, 1)
            dve.wait_ge(l.gp, 2)
            nc.vector.tensor_tensor(l_gate[:, :, :], ps[:, 4, 0:NT * NG].rearrange("p (t c) -> p t c", c=NG),
                                    bc(rc("ab").unsqueeze(1), [P, NT, NG]), ALU.add).then_inc(l.gate, 1)
            dve.wait_ge(l.sig, 1)
            nc.vector.tensor_scalar(l_ln[:, :, :], l_gate[:, :, NH:2 * NH], BETA_MAX - BETA_MIN, BETA_MIN, ALU.mult,
                                    ALU.add).then_inc(l.bet, 1)
            for t in range(5, TB, 2):
                product_in(t)
            dve.wait_ge(l.dec, 3)
            nc.vector.tensor_tensor(l_dk[:, :, :], l_dk[:, :, :], l_gate[:, :, 0:NH], ALU.mult).then_inc(l.dk, 1)
            vs.step(nc.vector.tensor_tensor(l_tot[:, :, :], l_tot[:, :, :], bc(cc("head").unsqueeze(1), [P, NT, NH]),
                                            ALU.mult))
            nc.vector.tensor_reduce(l_et[:, :], l_tot[:, :, :], AX.X, ALU.add)
            for t in range(TB + 1, NT, 2):
                product_in(t)

            def heads(v, b, col=0):
                return v[:, TB * b:TB * (b + 1), col:col + P].rearrange("p t (h d) -> p t h d", h=NH)

            def turned(dst, col, decay, b, done, count):
                wide = bc(decay[:, TB * b:TB * (b + 1), :].unsqueeze(3), [P, TB, NH, DK])
                vs.step(nc.vector.tensor_tensor(heads(dst, b), heads(l_g, b, col), wide, ALU.mult))
                first, second = lin_rope(nc.vector, dst, l_tv, b, vs.step)
                nc.vector.tensor_tensor(*first)
                nc.vector.tensor_tensor(*second).then_inc(done, 1)
                dve.wait_ge(done, count)

            def states(b):
                for g in (2 * b, 2 * b + 1):
                    dve.wait_ge(l.kv, g + 1)
                    for j in range(4):
                        t = 4 * g + j
                        ins = nc.vector.scalar_tensor_tensor(
                            out=l_te[:, t, :], in0=ps[:, KV_BANKS[g], j * P:(j + 1) * P], scalar=l_et[:, t:t + 1],
                            in1=cc("blocks"), op0=ALU.mult, op1=ALU.mult)
                    ins.then_inc(l.te, 1)
                vs.step(nc.vector.memset(l_s[:, TB * b, :], 0.0))
                dve.wait_ge(l.te, 2 * b + 2)
                for t in range(TB * b, TB * (b + 1) - 1):
                    ins = nc.vector.scalar_tensor_tensor(out=l_s[:, t + 1, :], in0=l_s[:, t, :], scalar=l_et[:, t:t + 1],
                                                         in1=l_te[:, t, :], op0=ALU.mult, op1=ALU.add)
                    if t < TB * (b + 1) - 2:
                        vs.step(ins)
                ins.then_inc(l.s, 1)

            dve.wait_ge(l.g_in, NT // 4)
            dve.wait_ge(l.g_in_v, NT // 4)
            turned(l_q, 0, l_dq, 0, l.q, 1)
            dve.wait_ge(l.g_in, NT // 2)
            dve.wait_ge(l.g_in_v, NT // 2)
            turned(l_q, 0, l_dq, 1, l.q, 2)
            states(0)
            for t in range(NT):
                if t == 4:
                    states(1)
                for k in range(2):
                    dve.wait_ge(l.sc, 2 * t + k + 1)
                    if t >= 2:
                        dve.wait_ge(l.o, t - 1)
                    nc.vector.tensor_tensor(
                        l_as[:, t % 2, 4 * k:4 * k + 4, :], ps[:, 2 * (t % 2) + k, :].rearrange("p (m t) -> p m t", m=4),
                        bc(cc("causal").unsqueeze(1), [P, 4, P]), ALU.mult).then_inc(l.as_, 1)
                    if t >= 11:
                        for _ in range(3):
                            vs.advance(stats)
                if t == 8:
                    lin_vector_add(dve, 0)
                if t == 10:
                    lin_vector_add(dve, 1)
                    dve.wait_ge(l.y, 2)
                    stats = Chain(norm_vector_stats(dve, vs, after, 0, False))
            vs.finish(stats)
            lin_vector_add(dve, 2)
            lin_vector_add(dve, 3)

        def lin_vector_add(dve, g):
            dve.wait_ge(l.done, g + 1)
            if g == 0:
                dve.wait_ge(l.bo, 2)
            xq = x[:, 4 * g:4 * g + 4, :]
            nc.vector.tensor_tensor(xq, xq, ps[:, 6 + g % 2, :].rearrange("p (a b) -> p a b", a=4), ALU.add).then_inc(l.y, 1)

        def lin_pool(pool, n):
            pool.wait_ge(n.xl_a, n.before(1) + 1)
            pool.wait_ge(n.xl_v, n.before(1) + 1)
            for b in range(B):
                xb = x[:, TB * b:TB * (b + 1), :]
                nc.gpsimd.tensor_tensor(xb, xb, bc(rc("bo").unsqueeze(1), [P, TB, P]), ALU.add).then_inc(l.bo, 1)
            pool.wait_ge(l.dk, 1)
            pool.wait_ge(l.g_in, NT // 2)
            pool.wait_ge(l.g_in_v, NT // 2)
            gs = Steps(pool, l.kp)
            for b in range(B):
                ts = slice(TB * b, TB * (b + 1))
                gs.step(nc.gpsimd.tensor_tensor(
                    l_k[:, ts, :].rearrange("p t (h d) -> p t h d", h=NH),
                    l_g[:, ts, P:2 * P].rearrange("p t (h d) -> p t h d", h=NH),
                    bc(l_dk[:, ts, :].unsqueeze(3), [P, TB, NH, DK]), ALU.mult))
                first, second = lin_rope(nc.gpsimd, l_k, l_tp, b, gs.step, True)
                gs.step(nc.gpsimd.tensor_tensor(*first))
                gs.step(nc.gpsimd.tensor_tensor(*second))

        def places(*starts):
            return [start + S * i for start, n in starts for i in range(n)]

        n0, f0 = Norm(0), Ffn(0, [places((20480, 7)), places((4096, 4), (12288, 3))], (0, 1), (2, 3), (4, 5))
        n1 = Norm(2)
        n2, f2 = Norm(4, 2), Ffn(2, [places((0, 4), (8192, 3)), places((20480, 7))], (6, 7), (6, 7), (6, 7))
        n3, m3 = Norm(5, 2), Mix(3)
        n4 = Norm(8)
        n5, m5 = Norm(10), Mix(5)

        block = ctx.enter_context(nc.Block())

        @block.sync
        def _(sp):
            for g in range(4):
                sp.dma_start(x[:, 4 * g:4 * g + 4, :],
                             A["x"].rearrange("(t p) d -> p t d", p=P)[:, 4 * g:4 * g + 4, :]).then_inc(s_x[g // 2], 16)
            sp.dma_start(w[:, :], A["wpack"]).then_inc(s_w, 16)
            sp.dma_start(cst[:, :], A["consts"]).then_inc(s_w, 16)
            sp.dma_start(row[:, :], A["rows"].to_broadcast([P, RTOTAL])).then_inc(s_w, 16)
            sp.dma_start(arena_f(28672, NH * P), A["wv"]).then_inc(s_wv, 16)
            sp.dma_start(w1[:, :, :], A["w1"].rearrange("e c f -> c e f")).then_inc(s_mix, 16)
            sp.dma_start(w2[:, :, :], A["w2"].rearrange("e c f -> c e f")).then_inc(s_mix, 16)
            sp.dma_start(b1[:, :], A["b1"]).then_inc(s_mix, 16)
            sp.dma_start(b2[:, :], A["b2"]).then_inc(s_mix, 16)
            for b in range(B):
                att_sync_stack(sp, b)
            att_sync_negmax_rows(sp)
            sp.wait_ge(s_b1, 1)
            for i in range(3):
                sp.dma_start(b1row[i:i + 1, :].rearrange("i (e f) -> i e f", e=NE), b1p[:, i, :]).then_inc(s_b1row, 16)
            out_view = A["out"].rearrange("(t p) d -> p t d", p=P)
            for q in range(4):
                sp.wait_ge(m5.done, 17 * (q + 1))
                sp.dma_start(out_view[:, 4 * q:4 * q + 4, :], x[:, 4 * q:4 * q + 4, :]).then_inc(s_out, 16)
            sp.wait_ge(s_out, 64)

        @block.gpsimd
        def _(pool):
            nc.gpsimd.memset(ones3[:, :], 1.0).then_inc(s_set, 1)
            nc.gpsimd.memset(xt[:, :, 0:PAD], 0.0).then_inc(s_set, 1)
            nc.gpsimd.memset(zerob[:, :], 0.0).then_inc(s_set, 1)
            pool.wait_ge(s_w, 48)
            nc.gpsimd.tensor_copy(identb[:, :], cc("ident")).then_inc(s_set, 1)
            pool.wait_ge(s_set, 4)
            att_pool_set(pool)
            att_pool_negmax(pool, Steps(pool, s_p))
            pool.wait_ge(n2.stat, n2.before(1) + 1)
            nc.gpsimd.memset(l_vp[:, :, :, :], 0.0).then_inc(l.vp, 1)
            mix_pool(pool, m3)
            lin_pool(pool, n4)
            mix_pool(pool, m5)

        def tensor_in_last_quad(pe, step):
            if step == 25:
                pe.wait_ge(a.mpu, len(ring))
                norm_tensor(pe, n2, 0)
            if step == 26:
                ffn_tensor_k(pe, f2, 0)
            if step == 27:
                ffn_tensor_r(pe, f2, 0)
            if step == 28:
                ffn_tensor_v(pe, f2, 0)

        def scalar_in_last_quad(act, v):
            if v == 101:
                norm_scalar_apply(act, n2, 0)
            if v == 105:
                norm_scalar_xt(act, n2, 0)
            if v == 110:
                ffn_scalar_k(act, f2, 0)
            if v == 115:
                ffn_scalar_r(act, f2, 0)
            if v == 128:
                norm_scalar_apply(act, n3, 0)

        def vector_before_last_copy(dve, vs):
            vs.finish(Chain(norm_vector_stats(dve, vs, n2, 0, False)))

        def vector_in_last_quad(dve, vs):
            norm_vector_xt(dve, n2, 0)
            ffn_vector_mix(dve, vs, n2, f2, 0)
            centre_experts(dve, vs)
            ffn_vector_add(dve, vs, f2, 0)
            vs.finish(Chain(norm_vector_stats(dve, vs, n3, 0, False)))

        def centre_experts(dve, vs):
            dve.wait_ge(s_mix, 64)
            mw, mb = small[:, 20, 0:NE], small[0:NE, 21, 0:1]
            vs.step(nc.vector.tensor_reduce(mw, w1[:, :, :], AX.X, ALU.add))
            vs.step(nc.vector.tensor_scalar(mw, mw, 1.0 / P, None, ALU.mult))
            vs.step(nc.vector.tensor_tensor(w1[:, :, :], w1[:, :, :], bc(mw.unsqueeze(2), [P, NE, P]), ALU.subtract))
            vs.step(nc.vector.tensor_reduce(mb, b1[:, :], AX.X, ALU.add))
            vs.step(nc.vector.tensor_scalar(mb, mb, 1.0 / P, None, ALU.mult))
            vs.step(nc.vector.tensor_scalar(b1[:, :], b1[:, :], mb, None, ALU.subtract))
            vs.step(nc.vector.tensor_copy(b1p[:, 0, :], b1[:, :]))
            vs.step(nc.vector.tensor_tensor(b1r[:, :], b1[:, :], b1p[:, 0, :], ALU.subtract))
            vs.step(nc.vector.tensor_copy(b1p[:, 1, :], b1r[:, :]))
            nc.vector.tensor_tensor(b1p[:, 2, :], b1r[:, :], b1p[:, 1, :], ALU.subtract).then_inc(s_b1, 1)

        @block.vector
        def _(dve):
            vs = Steps(dve, s_v)
            for half in range(2):
                dve.wait_ge(s_x[half], 32)
                vs.finish(Chain(norm_vector_stats(dve, vs, n0, half, False)))
            dve.wait_ge(s_set, 4)
            dve.wait_ge(s_w, 48)
            for half in range(2):
                norm_vector_xt(dve, n0, half)
                ffn_vector_mix(dve, vs, n0, f0, half)
            dve.wait_ge(s_wv, 16)
            nc.vector.tensor_reduce(wvs[:, :], arena_f(28672, P, 8), AX.X, ALU.add).then_inc(s_wvs, 1)
            nc.vector.tensor_reduce(bvs[:, :], rc("bv").rearrange("p (a b) -> p a b", b=8), AX.X, ALU.add)\
                .then_inc(s_wvs, 1)
            ffn_vector_add(dve, vs, f0, 0)
            vs.finish(Chain(norm_vector_stats(dve, vs, n1, 0, True)))
            ffn_vector_add(dve, vs, f0, 1)
            norm_vector_xt(dve, n1, 0, permuted=True, affine=True)
            vs.finish(Chain(norm_vector_stats(dve, vs, n1, 1, True)))
            dve.wait_ge(s_wvs, 2)
            att_vector_project(dve, 0, lambda: norm_vector_xt(dve, n1, 1, permuted=True, affine=True))
            att_vector_project(dve, 1)
            att_vector(dve, vs, vector_before_last_copy, vector_in_last_quad)
            norm_vector_xt(dve, n3, 0)
            vs.finish(Chain(norm_vector_stats(dve, vs, n2, 1, False)))
            mix_vector(dve, vs, n3, m3, after=n4, ffn=(n2, f2))
            lin_vector(dve, vs, n4, m3, n5)
            dve.wait_ge(l.y, 4)
            norm_vector_xt(dve, n5, 0)
            mix_vector(dve, vs, n5, m5)

        @block.scalar
        def _(act):
            for half in range(2):
                norm_scalar_apply(act, n0, half)
            act.wait_ge(s_w, 48)
            for half in range(2):
                norm_scalar_xt(act, n0, half)
            ffn_scalar_k(act, f0, 0)
            ffn_scalar_r(act, f0, 0)
            ffn_scalar_k(act, f0, 1)
            ffn_scalar_r(act, f0, 1)
            norm_scalar_apply(act, n1, 0)
            norm_scalar_xt(act, n1, 0, permuted=True, affine=True)
            norm_scalar_apply(act, n1, 1)
            att_scalar_project(act, 0, lambda: norm_scalar_xt(act, n1, 1, permuted=True, affine=True))
            att_scalar_project(act, 1)
            att_scalar(act, scalar_in_last_quad)
            norm_scalar_xt(act, n3, 0)
            mix_scalar(act, n3, m3, after=n4, ffn=(n2, f2))
            lin_scalar(act, n4, n5)
            norm_scalar_xt(act, n5, 0)
            mix_scalar(act, n5, m5)

        @block.tensor
        def _(pe):
            pe.wait_ge(s_set, 3)
            keep_clock(pe, 0, CLOCK_FILL)
            pe.wait_ge(s_w, 48)
            pe.wait_ge(s_set, 4)
            for half in range(2):
                norm_tensor(pe, n0, half)
            for half in range(2):
                ffn_tensor_k(pe, f0, half)
                ffn_tensor_r(pe, f0, half)
                ffn_tensor_v(pe, f0, half)
            keep_clock(pe, 0, CLOCK_FILL)
            norm_tensor(pe, n1, 0)
            att_tensor_project(pe, n1, 0)
            norm_tensor(pe, n1, 1)
            pe.wait_ge(a.f32, 1)
            keep_clock(pe, 0, CLOCK_FILL)
            att_tensor_project(pe, n1, 1)
            pe.wait_ge(a.onesk, 4)
            att_tensor(pe, tensor_in_last_quad)
            norm_tensor(pe, n3, 0)
            pe.wait_ge(a.done, 4)
            mix_tensor(pe, n3, m3, after=n4, ffn=(n2, f2))
            pe.wait_ge(m3.tmp, 68)
            lin_tensor(pe, n4)
            keep_clock(pe, 0, 6)
            pe.wait_ge(l.y, 4)
            norm_tensor(pe, n5, 0)
            mix_tensor(pe, n5, m5)


def shape_constants(np):
    c = np.zeros((P, CTOTAL), np.float32)

    def put(name, v):
        a, n = CCOLS[name]
        c[:, a:a + n] = v
    i = np.arange(P)
    put("ident", np.eye(P))
    put("causal", (i[:, None] <= i[None, :]))
    put("blocks", (i[:, None] // DK == i[None, :] // DK))
    half = DK // 2
    inv = (np.float32(1.0) / np.power(np.float32(10000.0), np.arange(half, dtype=np.float32) / np.float32(half)))
    ang = np.arange(S, dtype=np.float32)[:, None] * inv.astype(np.float32)[None, :]
    for name, f in (("cos", np.cos), ("sin", np.sin)):
        put(name, f(ang).astype(np.float32).reshape(TB, P, half).transpose(1, 0, 2).reshape(P, TB * half))
    put("rank", NE - np.arange(NE)[None, :])
    put("quarter", (i[:, None] // DK) % 4 == np.arange(4)[None, :])
    put("ones", 1.0)
    put("head", i[:, None] // DK == np.arange(NH)[None, :])
    return c


def kernel(**inputs):
    import numpy as _np
    import concourse.bacc as _bacc
    from concourse.bass_utils import run_bass_kernel_spmd as _run

    g = {k: _np.ascontiguousarray(v) for k, v in inputs.items()}
    col = lambda v: v.reshape(P, 1)
    rowv = lambda v: v.reshape(1, -1)
    wpack = _np.concatenate([
        g["L0_ffn_W_r"].T, g["L0_ffn_W_k"].T, g["L0_ffn_W_v"].T, g["L0_attn_Wq"], g["L0_attn_Wk"],
        g["L1_attn_Wq"].T, g["L1_attn_Wk"].T, g["L1_attn_Wv"].T, g["L1_attn_Walpha"].T, g["L1_attn_Wbeta"].T,
        g["L1_attn_Wo"].T, g["L1_ffn_Wr"], col(g["L0_ffn_mu_r"]), col(g["L0_ffn_mu_k"]), col(g["L0_attn_gamma"]),
        col(g["L0_attn_beta"]), col(g["L0_attn_bq"]), col(g["L0_attn_bk"]), g["L1_ffn_g1"].T, g["L1_ffn_be1"].T], axis=1)
    rows = _np.concatenate([rowv(g["L0_attn_bv"]), rowv(g["L1_attn_bo"]), rowv(g["L1_attn_balpha"]),
                            rowv(g["L1_attn_bbeta"]), rowv(g["L1_ffn_br"])], axis=1)
    arrays = {
        "x": g["L0_attn_x"].reshape(B * S, P), "wpack": _np.ascontiguousarray(wpack), "consts": shape_constants(_np),
        "rows": _np.ascontiguousarray(rows), "wv": g["L0_attn_Wv"], "w1": g["L1_ffn_W1"], "w2": g["L1_ffn_W2"],
        "b1": g["L1_ffn_b1"], "b2": g["L1_ffn_b2"]}
    nc = _bacc.Bacc("TRN2", target_bir_lowering=False, num_devices=1)
    A = {k: nc.dram_tensor(f"in_{k}", v.shape, F32, kind="ExternalInput").ap() for k, v in arrays.items()}
    A["out"] = nc.dram_tensor("out_x", (B * S, P), F32, kind="ExternalOutput").ap()
    build(nc, A)
    r = _run(nc, [{f"in_{k}": v for k, v in arrays.items()}], core_ids=[0])
    return r.results[0]["out_x"].reshape(B, S, P)
```
